# Optimizing a Trainium2 kernel written in Bass

```python
import numpy as np
import jax
import jax.numpy as jnp

def _softmax(x, axis=-1):
    return jax.nn.softmax(x, axis=axis)

def _gelu(x):
    return jax.nn.gelu(x, approximate=True)

def _silu(x):
    return jax.nn.silu(x)

def _sigmoid(x):
    return jax.nn.sigmoid(x)

def _layernorm(x, axis=-1, eps=1e-05):
    m = jnp.mean(x, axis=axis, keepdims=True)
    v = jnp.var(x, axis=axis, keepdims=True)
    return (x - m) / jnp.sqrt(v + eps)

def _scatter_add(tgt, idx, src, axis=0):
    return tgt.at[idx].add(src)

def _segment_sum(src, seg, n):
    return jax.ops.segment_sum(src, seg, n)
kernel_name = 'mk_gnn_resnorm_d4_gnn_r8_260f5a'

def setup_inputs(seed: int=0):
    np.random.seed(seed)
    _w = jnp.asarray

    def _rec_inputs():
        import jax
        import jax.numpy as jnp
        _gk = jax.random.key(seed)
        x = -8.776e-05 + 1 * jax.random.normal(jax.random.fold_in(_gk, 1), (1250, 512), jnp.float32)
        _s = jax.random.randint(jax.random.fold_in(_gk, 2), (10000,), 0, 1250, jnp.int32)
        _d = jax.random.randint(jax.random.fold_in(_gk, 3), (10000,), 0, 1250, jnp.int32)
        _loop = jnp.arange(1250, dtype=jnp.int32)
        src = jnp.concatenate([_s, _d, _loop])
        dst = jnp.concatenate([_d, _s, _loop])
        _o = jnp.argsort(dst, stable=True)
        src = src[_o]
        dst = dst[_o]
        edge_attr_4 = 0.00171547 + 0.999346 * jax.random.normal(jax.random.fold_in(_gk, 11), (21250, 4), jnp.float32)
        edge_attr_8 = 0.000126197 + 0.999763 * jax.random.normal(jax.random.fold_in(_gk, 12), (21250, 8), jnp.float32)
        return (x, src, dst, edge_attr_4, edge_attr_8)
    x, src, dst, edge_attr_4, edge_attr_8 = _rec_inputs()

    def _L0_gnn_setup():
        import jax, jax.numpy as jnp
        import numpy as np
        N = 1250
        DIM = 512
        H = 8
        C = DIM // H
        E = 20000
        NEG_SLOPE = 0.2
        BN_EPS = 1e-05
        key = jax.random.key(seed)
        ks = jax.random.split(key, 8)
        x = jax.random.normal(ks[0], (N, DIM), dtype=jnp.float32)
        edge_index = jax.random.randint(ks[1], (2, E), 0, N, dtype=jnp.int32)
        s = 1.0 / np.sqrt(DIM)
        W_gat = jax.random.normal(ks[2], (DIM, DIM), dtype=jnp.float32) * s
        att_src = jax.random.normal(ks[3], (H, C), dtype=jnp.float32) * s
        att_dst = jax.random.normal(ks[4], (H, C), dtype=jnp.float32) * s
        gat_bias = jnp.zeros((DIM,), dtype=jnp.float32)
        bn_gamma = jnp.ones((DIM,), dtype=jnp.float32)
        bn_beta = jnp.zeros((DIM,), dtype=jnp.float32)
        W_skip = jax.random.normal(ks[5], (DIM, DIM), dtype=jnp.float32) * s
        b_skip = jnp.zeros((DIM,), dtype=jnp.float32)
        return {'x': x, 'edge_index': edge_index, 'W_gat': W_gat, 'att_src': att_src, 'att_dst': att_dst, 'gat_bias': gat_bias, 'bn_gamma': bn_gamma, 'bn_beta': bn_beta, 'W_skip': W_skip, 'b_skip': b_skip}
    _L0_gnn_all = _L0_gnn_setup()
    _L0_gnn_in = {k: v for k, v in _L0_gnn_all.items() if k in ('W_gat', 'att_src', 'att_dst', 'gat_bias', 'bn_gamma', 'bn_beta', 'W_skip', 'b_skip')}
    del _L0_gnn_all

    def _L1_gnn_setup():
        import jax, jax.numpy as jnp
        import numpy as np
        MUL = 128
        N_NODES = 1250
        N_EDGES = 20000
        R_BASIS = 8
        HIDDEN = 64
        W_NUMEL = 4 * MUL
        SQRT3 = 3.0 ** 0.5
        SILU_2MOM = 1.679177
        AVG_NUM_NEIGHBORS = 10.0

        def _lin_irreps(x0, x1, W0, W1):
            y0 = x0 @ W0 / jnp.sqrt(jnp.float32(W0.shape[0]))
            y1 = jnp.einsum('num,uv->nvm', x1, W1) / jnp.sqrt(jnp.float32(W1.shape[0]))
            return (y0, y1)

        def _forward(node_feats, edge_attrs, edge_feats, edge_index, W_up0, W_up1, W_mlp1, W_mlp2, W_mlp3, W_mlp4, W_out0, W_out1):
            num_nodes = node_feats.shape[0]
            sender, receiver = (edge_index[0], edge_index[1])
            x0 = node_feats[:, :MUL]
            x1 = node_feats[:, MUL:].reshape(num_nodes, MUL, 3)
            x0, x1 = _lin_irreps(x0, x1, W_up0, W_up1)
            h = edge_feats
            for W in (W_mlp1, W_mlp2, W_mlp3):
                h = SILU_2MOM * jax.nn.silu(h @ W / jnp.sqrt(jnp.float32(W.shape[0])))
            tpw = h @ W_mlp4 / jnp.sqrt(jnp.float32(W_mlp4.shape[0]))
            w1, w2, w3, w4 = jnp.split(tpw, 4, axis=-1)
            s0 = x0[sender]
            s1 = x1[sender]
            y0 = edge_attrs[:, 0:1]
            y1 = edge_attrs[:, 1:4]
            p1 = w1 * s0 * y0
            p2 = (w2 * s0)[:, :, None] * y1[:, None, :]
            p3 = w3[:, :, None] * s1 * y0[:, None, :]
            p4 = w4 * jnp.einsum('eum,em->eu', s1, y1) / SQRT3
            m0 = jnp.concatenate([p1, p4], axis=-1)
            m1 = jnp.concatenate([p2, p3], axis=1)
            msg0 = jax.ops.segment_sum(m0, receiver, num_segments=num_nodes)
            msg1 = jax.ops.segment_sum(m1, receiver, num_segments=num_nodes)
            o0, o1 = _lin_irreps(msg0, msg1, W_out0, W_out1)
            out = jnp.concatenate([o0, o1.reshape(num_nodes, 3 * MUL)], axis=-1)
            return out / AVG_NUM_NEIGHBORS
        key = jax.random.key(seed)
        ks = jax.random.split(key, 12)
        rn = lambda k, s: jax.random.normal(k, s, dtype=jnp.float32)
        return {'node_feats': rn(ks[0], (N_NODES, 4 * MUL)), 'edge_attrs': rn(ks[1], (N_EDGES, 4)), 'edge_feats': rn(ks[2], (N_EDGES, R_BASIS)), 'edge_index': jax.random.randint(ks[3], (2, N_EDGES), 0, N_NODES), 'W_up0': rn(ks[4], (MUL, MUL)), 'W_up1': rn(ks[5], (MUL, MUL)), 'W_mlp1': rn(ks[6], (R_BASIS, HIDDEN)), 'W_mlp2': rn(ks[7], (HIDDEN, HIDDEN)), 'W_mlp3': rn(ks[8], (HIDDEN, HIDDEN)), 'W_mlp4': rn(ks[9], (HIDDEN, W_NUMEL)), 'W_out0': rn(ks[10], (2 * MUL, MUL)), 'W_out1': rn(ks[11], (2 * MUL, MUL))}
    _L1_gnn_all = _L1_gnn_setup()
    _L1_gnn_in = {k: v for k, v in _L1_gnn_all.items() if k in ('W_up0', 'W_up1', 'W_mlp1', 'W_mlp2', 'W_mlp3', 'W_mlp4', 'W_out0', 'W_out1')}
    del _L1_gnn_all

    def _L2_gnn_setup():
        import jax, jax.numpy as jnp
        import numpy as np
        N_NODES = 1250
        IN_F = 512
        OUT_F = 512
        N_EDGES = 20000
        GRID_SIZE = 5
        SPLINE_ORDER = 3
        ALPHA = 0.2

        def _grid():
            step = 2.0 / GRID_SIZE
            return jnp.arange(-SPLINE_ORDER, GRID_SIZE + SPLINE_ORDER + 1, dtype=jnp.float32) * step - 1.0

        def _b_splines(x, grid):
            x = x[..., None]
            bases = ((x >= grid[:-1]) & (x < grid[1:])).astype(x.dtype)
            for p in range(1, SPLINE_ORDER + 1):
                left = (x - grid[:-(p + 1)]) / (grid[p:-1] - grid[:-(p + 1)]) * bases[..., :-1]
                right = (grid[p + 1:] - x) / (grid[p + 1:] - grid[1:-p]) * bases[..., 1:]
                bases = left + right
            return bases
        key = jax.random.key(seed)
        k1, k2, k3, k4, k5, k6 = jax.random.split(key, 6)
        h = jax.random.normal(k1, (N_NODES, IN_F), dtype=jnp.float32)
        edge_index = jax.random.randint(k2, (2, N_EDGES), 0, N_NODES, dtype=jnp.int64)
        xav = float(np.sqrt(2.0 / (IN_F + OUT_F))) * 1.414
        W = jax.random.normal(k3, (IN_F, OUT_F), dtype=jnp.float32) * xav
        a = jax.random.normal(k4, (2 * OUT_F, 1), dtype=jnp.float32) * float(np.sqrt(2.0 / (2 * OUT_F + 1)))
        base_w = jax.random.normal(k5, (OUT_F, IN_F), dtype=jnp.float32) * xav
        n_coef = GRID_SIZE + SPLINE_ORDER
        spline_w = jax.random.normal(k6, (OUT_F, IN_F, n_coef), dtype=jnp.float32) * 0.1
        return {'h': h, 'W': W, 'a': a, 'base_w': base_w, 'spline_w': spline_w, 'edge_index': edge_index}
    _L2_gnn_all = _L2_gnn_setup()
    _L2_gnn_in = {k: v for k, v in _L2_gnn_all.items() if k in ('W', 'a', 'base_w', 'spline_w')}
    del _L2_gnn_all

    def _L3_gnn_setup():
        import jax, jax.numpy as jnp
        import numpy as np
        N_NODES = 1250
        IN_FEAT = 512
        OUT_FEAT = 512
        N_EDGES = 20000
        key = jax.random.key(seed)
        kx, kw, ks, kd = jax.random.split(key, 4)
        x = jax.random.normal(kx, (N_NODES, IN_FEAT), dtype=jnp.float32)
        fan_in, fan_out = (2 * IN_FEAT, OUT_FEAT)
        limit = float(np.sqrt(6.0 / (fan_in + fan_out)))
        w = jax.random.uniform(kw, (OUT_FEAT, 2 * IN_FEAT), dtype=jnp.float32, minval=-limit, maxval=limit)
        src = jax.random.randint(ks, (N_EDGES,), 0, N_NODES, dtype=jnp.int32)
        dst = jax.random.randint(kd, (N_EDGES,), 0, N_NODES, dtype=jnp.int32)
        edge_index = jnp.stack([src, dst], axis=0)
        return {'x': x, 'w': w, 'edge_index': edge_index}
    _L3_gnn_all = _L3_gnn_setup()
    _L3_gnn_in = {k: v for k, v in _L3_gnn_all.items() if k in ('w',)}
    del _L3_gnn_all
    return {'x': x, 'src': src, 'dst': dst, 'edge_attr_4': edge_attr_4, 'edge_attr_8': edge_attr_8, 'L0_gnn_W_gat': _L0_gnn_in['W_gat'], 'L0_gnn_att_src': _L0_gnn_in['att_src'], 'L0_gnn_att_dst': _L0_gnn_in['att_dst'], 'L0_gnn_gat_bias': _L0_gnn_in['gat_bias'], 'L0_gnn_bn_gamma': _L0_gnn_in['bn_gamma'], 'L0_gnn_bn_beta': _L0_gnn_in['bn_beta'], 'L0_gnn_W_skip': _L0_gnn_in['W_skip'], 'L0_gnn_b_skip': _L0_gnn_in['b_skip'], 'L1_gnn_W_up0': _L1_gnn_in['W_up0'], 'L1_gnn_W_up1': _L1_gnn_in['W_up1'], 'L1_gnn_W_mlp1': _L1_gnn_in['W_mlp1'], 'L1_gnn_W_mlp2': _L1_gnn_in['W_mlp2'], 'L1_gnn_W_mlp3': _L1_gnn_in['W_mlp3'], 'L1_gnn_W_mlp4': _L1_gnn_in['W_mlp4'], 'L1_gnn_W_out0': _L1_gnn_in['W_out0'], 'L1_gnn_W_out1': _L1_gnn_in['W_out1'], 'L2_gnn_W': _L2_gnn_in['W'], 'L2_gnn_a': _L2_gnn_in['a'], 'L2_gnn_base_w': _L2_gnn_in['base_w'], 'L2_gnn_spline_w': _L2_gnn_in['spline_w'], 'L3_gnn_w': _L3_gnn_in['w']}

def reference(x, src, dst, edge_attr_4, edge_attr_8, L0_gnn_W_gat, L0_gnn_att_src, L0_gnn_att_dst, L0_gnn_gat_bias, L0_gnn_bn_gamma, L0_gnn_bn_beta, L0_gnn_W_skip, L0_gnn_b_skip, L1_gnn_W_up0, L1_gnn_W_up1, L1_gnn_W_mlp1, L1_gnn_W_mlp2, L1_gnn_W_mlp3, L1_gnn_W_mlp4, L1_gnn_W_out0, L1_gnn_W_out1, L2_gnn_W, L2_gnn_a, L2_gnn_base_w, L2_gnn_spline_w, L3_gnn_w):
    import jax
    import jax.numpy as jnp

    def _L0_gnn_ref(x, edge_index, W_gat, att_src, att_dst, gat_bias, bn_gamma, bn_beta, W_skip, b_skip):
        import jax, jax.numpy as jnp
        import numpy as np
        N = 1250
        DIM = 512
        H = 8
        C = DIM // H
        E = 20000
        NEG_SLOPE = 0.2
        BN_EPS = 1e-05
        identity = x @ W_skip + b_skip
        loops = jnp.arange(N, dtype=edge_index.dtype)
        src = jnp.concatenate([edge_index[0], loops])
        dst = jnp.concatenate([edge_index[1], loops])
        h = (x @ W_gat).reshape(N, H, C)
        a_src = jnp.einsum('nhc,hc->nh', h, att_src)
        a_dst = jnp.einsum('nhc,hc->nh', h, att_dst)
        e = a_src[src] + a_dst[dst]
        e = jnp.where(e >= 0, e, NEG_SLOPE * e)
        m = jax.ops.segment_max(e, dst, num_segments=N)
        ex = jnp.exp(e - m[dst])
        denom = jax.ops.segment_sum(ex, dst, num_segments=N)
        alpha = ex / denom[dst]
        msgs = alpha[:, :, None] * h[src]
        out = jax.ops.segment_sum(msgs, dst, num_segments=N)
        out = out.reshape(N, DIM) + gat_bias
        mean = out.mean(axis=0)
        var = out.var(axis=0)
        out = (out - mean) * jax.lax.rsqrt(var + BN_EPS) * bn_gamma + bn_beta
        out = jax.nn.gelu(out, approximate=False)
        return out + identity

    def _L1_gnn_ref(node_feats, edge_attrs, edge_feats, edge_index, W_up0, W_up1, W_mlp1, W_mlp2, W_mlp3, W_mlp4, W_out0, W_out1):
        import jax, jax.numpy as jnp
        import numpy as np
        MUL = 128
        N_NODES = 1250
        N_EDGES = 20000
        R_BASIS = 8
        HIDDEN = 64
        W_NUMEL = 4 * MUL
        SQRT3 = 3.0 ** 0.5
        SILU_2MOM = 1.679177
        AVG_NUM_NEIGHBORS = 10.0

        def _lin_irreps(x0, x1, W0, W1):
            y0 = x0 @ W0 / jnp.sqrt(jnp.float32(W0.shape[0]))
            y1 = jnp.einsum('num,uv->nvm', x1, W1) / jnp.sqrt(jnp.float32(W1.shape[0]))
            return (y0, y1)

        def _forward(node_feats, edge_attrs, edge_feats, edge_index, W_up0, W_up1, W_mlp1, W_mlp2, W_mlp3, W_mlp4, W_out0, W_out1):
            num_nodes = node_feats.shape[0]
            sender, receiver = (edge_index[0], edge_index[1])
            x0 = node_feats[:, :MUL]
            x1 = node_feats[:, MUL:].reshape(num_nodes, MUL, 3)
            x0, x1 = _lin_irreps(x0, x1, W_up0, W_up1)
            h = edge_feats
            for W in (W_mlp1, W_mlp2, W_mlp3):
                h = SILU_2MOM * jax.nn.silu(h @ W / jnp.sqrt(jnp.float32(W.shape[0])))
            tpw = h @ W_mlp4 / jnp.sqrt(jnp.float32(W_mlp4.shape[0]))
            w1, w2, w3, w4 = jnp.split(tpw, 4, axis=-1)
            s0 = x0[sender]
            s1 = x1[sender]
            y0 = edge_attrs[:, 0:1]
            y1 = edge_attrs[:, 1:4]
            p1 = w1 * s0 * y0
            p2 = (w2 * s0)[:, :, None] * y1[:, None, :]
            p3 = w3[:, :, None] * s1 * y0[:, None, :]
            p4 = w4 * jnp.einsum('eum,em->eu', s1, y1) / SQRT3
            m0 = jnp.concatenate([p1, p4], axis=-1)
            m1 = jnp.concatenate([p2, p3], axis=1)
            msg0 = jax.ops.segment_sum(m0, receiver, num_segments=num_nodes)
            msg1 = jax.ops.segment_sum(m1, receiver, num_segments=num_nodes)
            o0, o1 = _lin_irreps(msg0, msg1, W_out0, W_out1)
            out = jnp.concatenate([o0, o1.reshape(num_nodes, 3 * MUL)], axis=-1)
            return out / AVG_NUM_NEIGHBORS
        return _forward(node_feats, edge_attrs, edge_feats, edge_index, W_up0, W_up1, W_mlp1, W_mlp2, W_mlp3, W_mlp4, W_out0, W_out1)

    def _L2_gnn_ref(h, W, a, base_w, spline_w, edge_index):
        import jax, jax.numpy as jnp
        import numpy as np
        N_NODES = 1250
        IN_F = 512
        OUT_F = 512
        N_EDGES = 20000
        GRID_SIZE = 5
        SPLINE_ORDER = 3
        ALPHA = 0.2

        def _grid():
            step = 2.0 / GRID_SIZE
            return jnp.arange(-SPLINE_ORDER, GRID_SIZE + SPLINE_ORDER + 1, dtype=jnp.float32) * step - 1.0

        def _b_splines(x, grid):
            x = x[..., None]
            bases = ((x >= grid[:-1]) & (x < grid[1:])).astype(x.dtype)
            for p in range(1, SPLINE_ORDER + 1):
                left = (x - grid[:-(p + 1)]) / (grid[p:-1] - grid[:-(p + 1)]) * bases[..., :-1]
                right = (grid[p + 1:] - x) / (grid[p + 1:] - grid[1:-p]) * bases[..., 1:]
                bases = left + right
            return bases
        HW = h @ W
        row, col = (edge_index[0], edge_index[1])
        s = HW @ a[:OUT_F, 0]
        t = HW @ a[OUT_F:, 0]
        e = jax.nn.leaky_relu(s[row] + t[col], negative_slope=ALPHA)
        m = jax.ops.segment_max(e, row, num_segments=N_NODES)
        ex = jnp.exp(e - m[row])
        den = jax.ops.segment_sum(ex, row, num_segments=N_NODES)
        att = ex / den[row]
        agg = jax.ops.segment_sum(att[:, None] * h[col], row, num_segments=N_NODES)
        grid = _grid()
        basis = _b_splines(agg, grid)
        out = jax.nn.silu(agg) @ base_w.T + jnp.einsum('nip,oip->no', basis, spline_w)
        return out

    def _L3_gnn_ref(x, w, edge_index):
        import jax, jax.numpy as jnp
        import numpy as np
        N_NODES = 1250
        IN_FEAT = 512
        OUT_FEAT = 512
        N_EDGES = 20000
        src, dst = (edge_index[0], edge_index[1])
        msgs = x[src]
        summed = jax.ops.segment_sum(msgs, dst, num_segments=x.shape[0])
        deg = jax.ops.segment_sum(jnp.ones_like(dst, dtype=x.dtype), dst, num_segments=x.shape[0])
        neighbor_mean = summed / jnp.maximum(deg, 1.0)[:, None]
        message = jnp.concatenate([x, neighbor_mean], axis=-1)
        weighted = jnp.einsum('of,nf->no', w, message)
        return jax.nn.relu(weighted)
    edge_index = jnp.stack([src, dst])
    x = _layernorm(x + _L0_gnn_ref(x, edge_index, L0_gnn_W_gat, L0_gnn_att_src, L0_gnn_att_dst, L0_gnn_gat_bias, L0_gnn_bn_gamma, L0_gnn_bn_beta, L0_gnn_W_skip, L0_gnn_b_skip), axis=-1)
    x = _layernorm(x + _L1_gnn_ref(x, edge_attr_4, edge_attr_8, edge_index, L1_gnn_W_up0, L1_gnn_W_up1, L1_gnn_W_mlp1, L1_gnn_W_mlp2, L1_gnn_W_mlp3, L1_gnn_W_mlp4, L1_gnn_W_out0, L1_gnn_W_out1), axis=-1)
    x = _layernorm(x + _L2_gnn_ref(x, L2_gnn_W, L2_gnn_a, L2_gnn_base_w, L2_gnn_spline_w, edge_index), axis=-1)
    x = _layernorm(x + _L3_gnn_ref(x, L3_gnn_w, edge_index), axis=-1)
    return x

_drawn_inputs = setup_inputs


def setup_inputs(seed=0):
    import zlib

    import numpy as np

    out = dict(_drawn_inputs(seed))
    spreads = {'L0_gnn_gat_bias': (0.0, 0.1),
     'L0_gnn_bn_gamma': (1.0, 0.2),
     'L0_gnn_bn_beta': (0.0, 0.1),
     'L0_gnn_b_skip': (0.0, 0.1)}
    factors = {}
    for name, (base, spread) in spreads.items():
        noise = np.random.default_rng([zlib.crc32(name.encode()), seed]).standard_normal(out[name].shape)
        drawn = base * np.exp(spread * noise) if base else spread * noise
        out[name] = jnp.asarray(drawn.astype(out[name].dtype))
    for name, factor in factors.items():
        out[name] = (out[name] * factor).astype(out[name].dtype)
    return out
```

```python
import numpy as np
import concourse.bass as bass
from concourse import mybir
from contextlib import ExitStack

N, D, E = 1250, 512, 21250
H, C = 8, 64
MUL, HID = 128, 64
NP, NB = 125, 10
KT = D // 128
EC = E // NP
GT = 4
GS = GT * 128
G = (E + NB * (GS - 1)) // GS
G += G % 2
RW = 16
R_DL, R_SRCF, R_SRCI, R_Y, R_F = 0, 1, 2, 4, 8
NEG = -1.0e30
SLOPE = 0.2
EPS = 1e-5
SB = 10
NSPL = 8
STEP = 2.0 / 5
KAPPA = (1.0 / 6.0) ** (1.0 / 3.0)
SILU2 = 1.679177
HB = NB // 2
assert NP * NB == N and NP * EC == E and EC % SB == 0


class Chain:

    def __init__(self, eng, sem):
        self.eng, self.sem, self.n, self.i, self.per, self.at = eng, sem, 0, None, 0, 0

    def link(self, ins):
        ins.then_inc(self.sem, 1)
        self.at += 1
        if self.i is None:
            self.n, self.at = self.n + self.at, 0
            self.eng.wait_ge(self.sem, self.n)
        else:
            self.eng.wait_ge(self.sem, self.i * self.per + (self.n + self.at))

    def enter(self, i, per):
        self.i, self.per, self.at = i, per, 0

    def leave(self, times):
        assert self.at == self.per, (self.at, self.per)
        self.n += times * self.per
        self.i, self.at = None, 0


def build(nc, a, out):
    f32, i32, u32 = mybir.dt.float32, mybir.dt.int32, mybir.dt.uint32
    bf16, f16, u16 = mybir.dt.bfloat16, mybir.dt.float16, mybir.dt.uint16
    ALU = mybir.AluOpType
    ACT = mybir.ActivationFunctionType
    X = mybir.AxisListType.X
    ctx = ExitStack()
    with ctx:
        def sb(name, shape, dt=f32):
            return ctx.enter_context(nc.sbuf_tensor(name, shape, dt))

        def dram(name, shape, dt=f32):
            return nc.dram_tensor(name, shape, dt, kind="Internal").ap()

        def sem(name):
            return ctx.enter_context(nc.semaphore(name))

        recs = dram("recs", ((G + 2) * GS, RW))
        as_rows = dram("as_rows", (2 * H, N))
        uv_rows = dram("uv_rows", (2 * H, N))
        st_rows = dram("st_rows", (2, N))
        uv2_rows = dram("uv2_rows", (2, N))
        xup = dram("xup", (N, D))

        x_sb = sb("x_sb", [NP, NB, D])
        cnt_d = sb("cnt_d", [NP, NB * N], u16)
        cnt_s = sb("cnt_s", [NP, NB, N], u16)
        rec_sb = sb("rec_sb", [128, G + 2, GT * RW])
        ident = sb("ident", [128, 128])
        upper = sb("upper", [128, 128])
        ones = sb("ones", [128, 192])
        iota_src = sb("iota_src", [128, N], f16)
        iota_dst = sb("iota_dst", [128, NP], f32)
        iota_dsth = sb("iota_dsth", [128, NP], f16)
        gblk = sb("gblk", [1, G + 2], i32)
        epsc = sb("epsc", [128, 1])
        mv = sb("mv", [NP, NB, 2])
        bst = sb("bst", [NP, NB, 6])
        rstd = sb("rstd", [NP, NB])
        deg = sb("deg", [NP, NB])
        ARENA = 28800
        arena = sb("arena", [128, ARENA])

        def at(off, shape, dt=f32):
            size = int(np.prod(shape[1:]))
            words = size if dt in (f32, i32, u32) else (size + 1) // 2
            assert off + words <= ARENA
            v = arena[:shape[0], off:off + words]
            if dt != f32:
                v = v.bitcast(dt)
            if len(shape) == 3:
                v = v.rearrange("p (a b) -> p a b", a=shape[1])
            if len(shape) == 4:
                v = v.rearrange("p (a b c) -> p a b c", a=shape[1], b=shape[2])
            return v

        PS = ctx.enter_context(nc.psum_tensor("PS", [128, 8, 512], f32))

        o = [0]

        def nxt(shape, dt=f32):
            v = at(o[0], shape, dt)
            o[0] += int(np.prod(shape[1:]))
            return v
        srci, dsti = nxt([NP, EC], i32), nxt([NP, EC], i32)
        dstf, blk, ge, posf = (nxt([NP, EC]) for _ in range(4))
        pos = nxt([NP, EC], u32)
        mask, cum = nxt([NP, NB, EC]), nxt([NP, NB, EC])
        a4, a8, rec = nxt([NP, EC, 4]), nxt([NP, EC, 8]), nxt([NP, EC, RW])
        EMP = 54
        assert (G + 2) * GS % (128 * EMP) == 0
        empty = nxt([128, EMP, RW])
        tot, base = nxt([NP, NB]), nxt([NP, NB])
        ngi, ngf, gend, gbase = nxt([128, NB], i32), nxt([128, NB]), nxt([128, NB]), nxt([128, NB])
        gi, gf, gbf = nxt([1, G + 2], i32), nxt([1, G + 2]), nxt([1, G + 2])
        stage_rec, stage_pos = nxt([NP, SB, RW]), nxt([NP, SB], u32)
        assert o[0] <= 12000
        b_skip_b = at(12000, [NP, D])
        xT = at(13000, [128, KT, N])
        w_gat, w_skip = at(18000, [128, KT, D]), at(20048, [128, KT, D])
        att_b = at(22096, [128, 2, D])
        h_sb = at(23120, [NP, NB, H * (C + 1)])
        h4 = h_sb.rearrange("p b (h c) -> p b h c", h=H)
        wa = sb("wa", [128, KT, 2 * H])
        sc = sb("sc", [NP, NB, 2 * H])
        rows16 = cnt_s[0:2 * H, 0:2, :].rearrange("p a n -> p (a n)").bitcast(f32)
        mx1 = sb("mx1", [NP, NB])
        mxh = sb("mxh", [NP, H, NB])
        uv = sb("uv", [NP, NB, 2 * H])
        c8 = sb("c8", [NP, 2, NB])
        c2 = sb("c2", [NP, 2, NB])
        sc8 = sb("sc8", [NP, H, NB])
        sc2 = sb("sc2", [NP, H, NB])
        rden = sb("rden", [NP, NB])
        oh_src = at(0, [128, 2 * GT, N], bf16)
        oh_dst = at(5000, [128, 2 * GT, NP + 1], bf16)
        cnt_f = at(5600, [NP, 2, N])
        rslot = sb("rslot", [128, 2, GT * RW])
        nomask = at(13000, [NP, NB, N], bf16)
        as_b = at(2000, [NP, 2, N])
        junk = at(4600, [NP, N])
        uvrow_sb = at(8000, [2 * H, N])
        UV = at(0, [NP, 2, 2, N])
        tt, ee, pp = at(5000, [NP, 2, N]), at(7500, [NP, 2, N]), at(10000, [NP, 2, N])
        O = at(13000, [NP, NB, D])
        bias_b, gam_b, bet_b = at(18200, [NP, D]), at(18712, [NP, D]), at(19224, [NP, D])
        sq, mean_b, scl_b = at(20000, [NP, 2, D]), at(21024, [NP, D]), at(21536, [NP, D])
        acc = at(0, [NP, NB * 1024])
        ring = at(10240, [128, 2 * GT, D])
        xT1 = at(14336, [128, KT, N])
        xup_st = at(19500, [NP, 2, D])
        prod = at(14336, [128, GT, 8 * MUL])
        sel = at(18432, [128, 2 * GT, 4 * NP])
        fT = at(22432, [8, GS])
        hid = at(23456, [HID, 4, GS])
        w_up0, w_up1 = at(25504, [128, MUL]), at(25632, [128, MUL])
        w_m1, w_m2, w_m3 = at(25760, [8, HID]), at(25824, [HID, HID]), at(25888, [HID, HID])
        w_m4 = at(25952, [HID, 4 * MUL])
        w_o0, w_o1 = at(26464, [128, 2, MUL]), at(26720, [128, 2, MUL])
        msgT = at(18432, [128, 2, 8 * NP])
        gidx = sb("gidx", [128, 2, GT], u32)
        gslot = sb("gslot", [128, 2, GT * RW])
        fsl = sb("fsl", [128, 2, GT * RW])
        P50 = at(0, [NP, NB, N])
        UV2 = at(12500, [NP, 2, N])
        t2, e2 = at(15000, [NP, 2, N]), at(17500, [NP, 2, N])
        agg = at(20000, [NP, NB, D])
        w_l2 = at(0, [128, KT, D])
        a_b = at(2048, [128, 2, D])
        xT2 = at(3100, [128, KT, N])
        tmp2 = at(25200, [128, D])
        rows2 = at(8200, [2, N])
        uvrow2 = at(9500, [2, N])
        st_b = at(10800, [NP, N])
        nomask2 = at(13000, [NP, NB, N], bf16)
        junk2 = at(19300, [NP, N], bf16)
        aggT = at(0, [128, KT, N])
        basis = at(5000, [128, 2, KT * HB * NP])
        sv, sa, sbb, sa2, sb2 = (at(10000 + 2500 * k, [128, KT * HB * NP]) for k in range(5))
        w_sp = at(22500, [128, 2, KT * D])
        cen = sb("cen", [128, NSPL])
        cslot = sb("cslot", [128, 2])
        w_l3 = at(0, [128, 2 * KT, D])
        nm = at(12500, [NP, NB, D])
        nmT, xT3 = at(17620, [128, KT, N]), at(22620, [128, KT, N])
        fin = at(5000, [NP, 2, D])

        s_acc_done = sem("s_acc_done")
        s_acc_free = sem("s_acc_free")
        s_acc_zero = sem("s_acc_zero")
        s_aggT_ok = sem("s_aggT_ok")
        s_asb_free = sem("s_asb_free")
        s_asb_in0 = sem("s_asb_in0")
        s_asb_in1 = sem("s_asb_in1")
        s_at_cp = sem("s_at_cp")
        s_at_ps = sem("s_at_ps")
        s_basis_ok = sem("s_basis_ok")
        s_bn_in = sem("s_bn_in")
        s_bn_ok = sem("s_bn_ok")
        s_bn_ps = sem("s_bn_ps")
        s_bnsd_ok = sem("s_bnsd_ok")
        s_cen_ok = sem("s_cen_ok")
        s_cnt_flushed = sem("s_cnt_flushed")
        s_cnt_ps = sem("s_cnt_ps")
        s_cntf_ok = sem("s_cntf_ok")
        s_cnts_cp = sem("s_cnts_cp")
        s_cntt_ps = sem("s_cntt_ps")
        s_cols2_cp = sem("s_cols2_cp")
        s_cols2_ps = sem("s_cols2_ps")
        s_cols_cp = sem("s_cols_cp")
        s_cols_ps = sem("s_cols_ps")
        s_const0 = sem("s_const0")
        s_consts = sem("s_consts")
        s_cslot_ok = sem("s_cslot_ok")
        s_dst_in = sem("s_dst_in")
        s_dve_chain = sem("s_dve_chain")
        s_e2_ok = sem("s_e2_ok")
        s_e_ok = sem("s_e_ok")
        s_empty_ok = sem("s_empty_ok")
        s_final_ok = sem("s_final_ok")
        s_fs_ok = sem("s_fs_ok")
        s_ft_cp = sem("s_ft_cp")
        s_ft_ps = sem("s_ft_ps")
        s_gelu_ok = sem("s_gelu_ok")
        s_gidx_ok = sem("s_gidx_ok")
        s_h_cp = sem("s_h_cp")
        s_h_ps = sem("s_h_ps")
        s_head_free = sem("s_head_free")
        s_hid_ok = sem("s_hid_ok")
        s_l2_agg = sem("s_l2_agg")
        s_l2_cp = sem("s_l2_cp")
        s_l3_agg = sem("s_l3_agg")
        s_l3_cp = sem("s_l3_cp")
        s_ln1_sd = sem("s_ln1_sd")
        s_ln1_var = sem("s_ln1_var")
        s_ln2_sd = sem("s_ln2_sd")
        s_ln2_var = sem("s_ln2_var")
        s_ln3_sd = sem("s_ln3_sd")
        s_ln3_var = sem("s_ln3_var")
        s_ln4_sd = sem("s_ln4_sd")
        s_ln4_var = sem("s_ln4_var")
        s_mask_ok = sem("s_mask_ok")
        s_max_done = sem("s_max_done")
        s_mlp_ps = sem("s_mlp_ps")
        s_mt_cp = sem("s_mt_cp")
        s_mt_ps = sem("s_mt_ps")
        s_nt_cp = sem("s_nt_cp")
        s_nt_ps = sem("s_nt_ps")
        s_o_ok = sem("s_o_ok")
        s_oh_ok = sem("s_oh_ok")
        s_out_done = sem("s_out_done")
        s_p2_ok = sem("s_p2_ok")
        s_p3_ok = sem("s_p3_ok")
        s_p_ok = sem("s_p_ok")
        s_prefix_cp = sem("s_prefix_cp")
        s_prefix_ps = sem("s_prefix_ps")
        s_prod_ok = sem("s_prod_ok")
        s_pv_done = sem("s_pv_done")
        s_rec_in = sem("s_rec_in")
        s_rec_ok = sem("s_rec_ok")
        s_recs_clear = sem("s_recs_clear")
        s_recs_in = sem("s_recs_in")
        s_rows2_cp = sem("s_rows2_cp")
        s_rows2_out = sem("s_rows2_out")
        s_rows2_ps = sem("s_rows2_ps")
        s_rows_cp = sem("s_rows_cp")
        s_rows_out = sem("s_rows_out")
        s_rows_ps = sem("s_rows_ps")
        s_sa_ok = sem("s_sa_ok")
        s_scat_done = sem("s_scat_done")
        s_scattered = sem("s_scattered")
        s_sel_ok = sem("s_sel_ok")
        s_silu_ok = sem("s_silu_ok")
        s_skip_cp = sem("s_skip_cp")
        s_skip_ps = sem("s_skip_ps")
        s_sp_free = sem("s_sp_free")
        s_sq2_ok = sem("s_sq2_ok")
        s_sq_ok = sem("s_sq_ok")
        s_sq_used = sem("s_sq_used")
        s_st_in = sem("s_st_in")
        s_staged = sem("s_staged")
        s_sv_ok = sem("s_sv_ok")
        s_t2_ok = sem("s_t2_ok")
        s_t_ok = sem("s_t_ok")
        s_tot_ok = sem("s_tot_ok")
        s_tpw_ps = sem("s_tpw_ps")
        s_uv2_in = sem("s_uv2_in")
        s_uv2_ok = sem("s_uv2_ok")
        s_uv_free = sem("s_uv_free")
        s_uv_in0 = sem("s_uv_in0")
        s_uv_in1 = sem("s_uv_in1")
        s_uv_ok = sem("s_uv_ok")
        s_uvrow2_ok = sem("s_uvrow2_ok")
        s_uvrow_ok = sem("s_uvrow_ok")
        s_uvt2_ps = sem("s_uvt2_ps")
        s_uvt_ps = sem("s_uvt_ps")
        s_var_ok = sem("s_var_ok")
        s_w1_in = sem("s_w1_in")
        s_wa2_ok = sem("s_wa2_ok")
        s_wa_ok = sem("s_wa_ok")
        s_wg_in = sem("s_wg_in")
        s_wk_in = sem("s_wk_in")
        s_wl2_in = sem("s_wl2_in")
        s_wl3_in = sem("s_wl3_in")
        s_wsp_in0 = sem("s_wsp_in0")
        s_wsp_in1 = sem("s_wsp_in1")
        s_x1_ok = sem("s_x1_ok")
        s_x2_ok = sem("s_x2_ok")
        s_x3_ok = sem("s_x3_ok")
        s_x4_ok = sem("s_x4_ok")
        s_x_in = sem("s_x_in")
        s_xt1_cp = sem("s_xt1_cp")
        s_xt1_ps = sem("s_xt1_ps")
        s_xt2_cp = sem("s_xt2_cp")
        s_xt2_ps = sem("s_xt2_ps")
        s_xt3_cp = sem("s_xt3_cp")
        s_xt3_ps = sem("s_xt3_ps")
        s_xt_cp = sem("s_xt_cp")
        s_xt_ps = sem("s_xt_ps")
        s_xup_cp = sem("s_xup_cp")
        s_xup_out0 = sem("s_xup_out0")
        s_xup_out1 = sem("s_xup_out1")
        s_xup_ps = sem("s_xup_ps")
        s_y1_cp = sem("s_y1_cp")
        s_y1_ps = sem("s_y1_ps")
        s_y2_cp = sem("s_y2_cp")
        s_y3_cp = sem("s_y3_cp")
        s_y3_ps = sem("s_y3_ps")
        s_gath = [sem(f"s_gath{k}") for k in range(2 * GT)]
        block = ctx.enter_context(nc.Block())

        def kview(w):
            return w.rearrange("(k p) n -> p k n", p=128)

        def bass_row(v, p):
            return v.rearrange("(a n) -> a n", a=1).to_broadcast([p, v.shape[0]])

        @block.sync
        def _(sp):
            sp.dma_start(dsti, a["dst"].rearrange("(p e) -> p e", p=NP)).then_inc(s_dst_in, 16)
            sp.dma_start(srci, a["src"].rearrange("(p e) -> p e", p=NP)).then_inc(s_rec_in, 16)
            sp.dma_start(a4, a["edge_attr_4"].rearrange("(p e) k -> p e k", p=NP)).then_inc(s_rec_in, 16)
            sp.dma_start(a8, a["edge_attr_8"].rearrange("(p e) k -> p e k", p=NP)).then_inc(s_rec_in, 16)
            sp.dma_start(x_sb[:], a["x"].rearrange("(b p) n -> p b n", p=NP)).then_inc(s_x_in, 16)
            sp.dma_start(w_gat, kview(a["L0_gnn_W_gat"])).then_inc(s_wg_in, 16)
            sp.dma_start(att_b[:, 0, :], bass_row(a["L0_gnn_att_src"].rearrange("h c -> (h c)"), 128)).then_inc(s_wg_in, 16)
            sp.dma_start(att_b[:, 1, :], bass_row(a["L0_gnn_att_dst"].rearrange("h c -> (h c)"), 128)).then_inc(s_wg_in, 16)
            sp.dma_start(w_skip, kview(a["L0_gnn_W_skip"])).then_inc(s_wk_in, 16)
            sp.dma_start(b_skip_b, bass_row(a["L0_gnn_b_skip"], NP)).then_inc(s_wk_in, 16)
            sp.wait_ge(s_empty_ok, 2)
            flat = recs.rearrange("(q p e) k -> q p (e k)", p=128, e=EMP)
            nq = (G + 2) * GS // (128 * EMP)
            for q in range(nq):
                sp.dma_start(flat[q], empty.rearrange("p e k -> p (e k)")).then_inc(s_recs_clear, 16)
            sp.wait_ge(s_scattered, 16 * EC)
            sp.dma_start(rec_sb[:], recs.rearrange("(g p t) k -> p g (t k)", p=128, t=GT)).then_inc(s_recs_in, 16)

            sp.wait_ge(s_rows_cp, 3)
            sp.dma_start(as_rows, rows16).then_inc(s_rows_out, 16)
            sp.wait_ge(s_rows_out, 16)
            sp.wait_ge(s_mask_ok, 1)
            with sp.Fori(0, H // 2) as i:
                for par in range(2):
                    sp.wait_ge(s_asb_free, i * 2 + (par + 1))
                    sp.dma_start(as_b[:, par, :], as_rows[bass.ds(i * 2 + par, 1), :].to_broadcast([NP, N]))\
                      .then_inc(s_asb_in0 if par == 0 else s_asb_in1, 16)
            sp.wait_ge(s_uvrow_ok, 1)
            sp.dma_start(uv_rows, uvrow_sb).then_inc(s_rows_out, 16)
            sp.wait_ge(s_rows_out, 32)
            sp.wait_ge(s_max_done, 1)
            with sp.Fori(0, H // 2) as i:
                for par in range(2):
                    sp.wait_ge(s_uv_free, i * 2 + (par + 1))
                    for q in range(2):
                        sp.dma_start(UV[:, par, q, :], uv_rows[bass.ds(i * 2 + (par + q * H), 1), :].to_broadcast([NP, N]))\
                          .then_inc(s_uv_in0 if par == 0 else s_uv_in1, 16)
            sp.dma_start(bias_b, bass_row(a["L0_gnn_gat_bias"], NP)).then_inc(s_bn_in, 16)
            sp.dma_start(gam_b, bass_row(a["L0_gnn_bn_gamma"], NP)).then_inc(s_bn_in, 16)
            sp.dma_start(bet_b, bass_row(a["L0_gnn_bn_beta"], NP)).then_inc(s_bn_in, 16)

            sp.wait_ge(s_x1_ok, 1)
            sp.dma_start(w_up0, a["L1_gnn_W_up0"]).then_inc(s_w1_in, 16)
            sp.dma_start(w_up1, a["L1_gnn_W_up1"]).then_inc(s_w1_in, 16)
            sp.dma_start(w_m1, a["L1_gnn_W_mlp1"]).then_inc(s_w1_in, 16)
            sp.dma_start(w_m2, a["L1_gnn_W_mlp2"]).then_inc(s_w1_in, 16)
            sp.dma_start(w_m3, a["L1_gnn_W_mlp3"]).then_inc(s_w1_in, 16)
            sp.dma_start(w_m4, a["L1_gnn_W_mlp4"]).then_inc(s_w1_in, 16)
            sp.dma_start(w_o0, kview(a["L1_gnn_W_out0"])).then_inc(s_w1_in, 16)
            sp.dma_start(w_o1, kview(a["L1_gnn_W_out1"])).then_inc(s_w1_in, 16)
            for b in range(NB):
                sp.wait_ge(s_xup_cp, b + 1)
                sp.dma_start(xup[b * NP:(b + 1) * NP, :], xup_st[:, b % 2, :]).then_inc(s_xup_out0 if b % 2 == 0 else s_xup_out1, 16)

            sp.wait_ge(s_x2_ok, 1)
            sp.dma_start(w_l2, kview(a["L2_gnn_W"])).then_inc(s_wl2_in, 16)
            av = a["L2_gnn_a"].rearrange("(q n) k -> q (n k)", q=2)
            sp.dma_start(a_b[:, 0, :], av[0:1, :].to_broadcast([128, D])).then_inc(s_wl2_in, 16)
            sp.dma_start(a_b[:, 1, :], av[1:2, :].to_broadcast([128, D])).then_inc(s_wl2_in, 16)
            sp.wait_ge(s_rows2_cp, 3)
            sp.dma_start(st_rows, rows2).then_inc(s_rows2_out, 16)
            sp.wait_ge(s_rows2_out, 16)
            sp.dma_start(st_b, st_rows[1:2, :].to_broadcast([NP, N])).then_inc(s_st_in, 16)
            sp.wait_ge(s_uvrow2_ok, 1)
            sp.dma_start(uv2_rows, uvrow2).then_inc(s_rows2_out, 16)
            sp.wait_ge(s_rows2_out, 32)
            for q in range(2):
                sp.dma_start(UV2[:, q, :], uv2_rows[q:q + 1, :].to_broadcast([NP, N])).then_inc(s_uv2_in, 16)
            sp.wait_ge(s_aggT_ok, 1)
            spl = a["spline_wT"].rearrange("q (k p) n -> q p k n", p=128)
            for half in range(2):
                sp.wait_ge(s_sp_free, 10 * half + 1)
                sp.dma_start(w_sp[:, 0, :].rearrange("p (k n) -> p k n", k=KT), kview(a["base_wT"])).then_inc(s_wsp_in0, 16)
                with sp.Fori(0, NSPL // 2) as i:
                    for par in range(2):
                        slot = 1 - par
                        sp.wait_ge(s_sp_free, i * 2 + (9 * half + par + 2))
                        sp.dma_start(w_sp[:, slot, :].rearrange("p (k n) -> p k n", k=KT),
                                     spl[bass.ds(i * 2 + par, 1), :, :, :].rearrange("q p k n -> (q p) k n"))\
                          .then_inc(s_wsp_in0 if slot == 0 else s_wsp_in1, 16)
            sp.wait_ge(s_l3_agg, NB)
            sp.dma_start(w_l3, kview(a["w_l3T"])).then_inc(s_wl3_in, 16)

            sp.wait_ge(s_final_ok, 1)
            sp.dma_start(out.rearrange("(b p) n -> p b n", p=NP), x_sb[:]).then_inc(s_out_done, 16)
            sp.wait_ge(s_out_done, 16)

        @block.gpsimd
        def _(pool):
            pool.memset(upper[:], 1.0)
            pool.memset(ident[:], 0.0)
            pool.memset(ones[:], 1.0)
            pool.memset(epsc[:], EPS)
            pool.memset(gidx[:], 0).then_inc(s_const0, 1)
            pool.iota(gi, pattern=[[1, G + 2]], base=0, channel_multiplier=0)
            pool.iota(iota_src[:], pattern=[[1, N]], base=0, channel_multiplier=0, allow_small_or_imprecise_dtypes=True)
            pool.iota(iota_dst[:], pattern=[[1, NP]], base=0, channel_multiplier=0, allow_small_or_imprecise_dtypes=True)
            pool.iota(cen[:], pattern=[[1, NSPL]], base=0, channel_multiplier=0, allow_small_or_imprecise_dtypes=True)
            pool.iota(iota_dsth[:], pattern=[[1, NP]], base=0, channel_multiplier=0, allow_small_or_imprecise_dtypes=True)
            pool.wait_ge(s_const0, 1)
            pool.affine_select(out=upper[:], in_=upper[:], compare_op=ALU.is_gt, fill=0.0, base=0,
                               pattern=[[1, 128]], channel_multiplier=-1)
            pool.affine_select(out=ident[:], in_=ident[:], compare_op=ALU.not_equal, fill=1.0, base=0,
                               pattern=[[-1, 128]], channel_multiplier=1).then_inc(s_consts, 1)
            nq = (G + 2) * GS // (128 * EMP)
            pool.wait_ge(s_recs_clear, 16 * nq)
            pool.wait_ge(s_rec_ok, 1)

            def scatter_round(j, n_staged):
                pool.tensor_copy(stage_pos, pos[:, bass.ds(j * SB, SB)])
                pool.tensor_copy(stage_rec, rec[:, bass.ds(j * SB, SB), :]).then_inc(s_staged, 1)
                pool.wait_ge(s_staged, n_staged)
                pool.nop(nofuse=True)
                for k in range(SB):
                    pool.indirect_dma_start(out=recs, out_offset=bass.IndirectOffsetOnAxis(stage_pos[:, k:k + 1], 0),
                                            in_=stage_rec[:, k, :], in_offset=None).then_inc(s_scattered, 16)
            scatter_round(0, 1)
            with pool.Fori(1, EC // SB) as j:
                pool.wait_ge(s_scattered, j * (16 * SB))
                scatter_round(j, j + 1)

            pool.wait_ge(s_recs_in, 16)
            for sl in range(2):
                pool.wait_ge(s_xup_out0 if sl == 0 else s_xup_out1, 16 * NB // 2)

            pool.wait_ge(s_acc_zero, 1)

            def gathers(g, par, n):
                pool.tensor_copy(gidx[:, par, :], rec_sb[:, bass.ds(g, 1), :].bitcast(u32)
                                 .rearrange("p a (t k) -> p (a t) k", k=RW)[:, :, R_SRCI])
                pool.tensor_copy(gslot[:, par, :], rec_sb[:, bass.ds(g, 1), :].rearrange("p a k -> p (a k)"))\
                    .then_inc(s_gidx_ok, 1)
                pool.wait_ge(s_gidx_ok, n)
                pool.nop(nofuse=True)
                for k in range(GT):
                    pool.indirect_dma_start(out=ring[:, par * GT + k, :], out_offset=None, in_=xup,
                                            in_offset=bass.IndirectOffsetOnAxis(gidx[:, par, k:k + 1], 0))\
                        .then_inc(s_gath[par * GT + k], 16)

            def selectors(par):
                for k in range(GT):
                    r = gslot[:, par, k * RW:(k + 1) * RW]
                    for m in range(4):
                        ins = pool.tensor_scalar(sel[:, par * GT + k, m * NP:(m + 1) * NP], iota_dst[:],
                                                 r[:, R_DL:R_DL + 1], r[:, R_Y + m:R_Y + m + 1],
                                                 ALU.is_equal, ALU.mult)
                    ins.then_inc(s_sel_ok, 1)
            for g in range(2):
                gathers(g, g, g + 1)
                selectors(g)
            with pool.Fori(0, G // 2 - 1) as i:
                for par in range(2):
                    pool.wait_ge(s_prod_ok, i * 8 + (4 * par + 5))
                    pool.wait_ge(s_scat_done, i * 8 + (4 * par + 4 + GT))
                    gathers(i * 2 + (2 + par), par, i * 2 + (3 + par))
                    selectors(par)

        @block.tensor
        def _(pe):
            t = nc.tensor

            def transposes(src, ready, done, copied, banks, copied0=0):
                for b in range(NB):
                    if ready is not None:
                        pe.wait_ge(*ready(b))
                    if b >= 2:
                        pe.wait_ge(copied, copied0 + b - 1)
                    for k in range(KT):
                        ins = t.transpose(PS[:, banks[b % 2], k * 128:k * 128 + NP], src(b, k), ident[:NP, :NP])
                    ins.then_inc(done, 1)

            def node_product(lhs, rhs, nk, done, copied, banks, cols=D):
                for b in range(NB):
                    if b >= 2:
                        pe.wait_ge(copied, b - 1)
                    for k in range(nk):
                        ins = t.matmul(PS[:NP, banks[b % 2], 0:cols], lhs(b, k), rhs(k), start=(k == 0), stop=(k == nk - 1))
                    ins.then_inc(done, 1)

            def blk_of(v):
                return lambda b, k: v[:, k, b * NP:(b + 1) * NP]

            def rows_product(w, nr, xt, done, b0):
                for q in range(3):
                    n0, n1 = q * 512, min(N, (q + 1) * 512)
                    for k in range(KT):
                        ins = t.matmul(PS[:nr, b0 + q, 0:n1 - n0], w[:, k, 0:nr], xt[:, k, n0:n1], start=(k == 0), stop=(k == KT - 1))
                    ins.then_inc(done, 1)

            def cols_product(w, nr, xt, done, bank):
                for b in range(NB):
                    for k in range(KT):
                        ins = t.matmul(PS[:NP, bank, b * nr:(b + 1) * nr], xt[:, k, b * NP:(b + 1) * NP], w[:, k, 0:nr],
                                       start=(k == 0), stop=(k == KT - 1))
                ins.then_inc(done, 1)

            def uv_transposes(src, nr, done, b0):
                for b in range(NB):
                    ins = t.transpose(PS[:nr, b0 + b // 4, (b % 4) * NP:(b % 4 + 1) * NP], src[:, b, 0:nr], ident[:NP, :NP])
                ins.then_inc(done, 1)

            pe.wait_ge(s_consts, 1)
            pe.wait_ge(s_x_in, 16)
            transposes(lambda b, k: x_sb[:, b, k * 128:(k + 1) * 128], None, s_xt_ps, s_xt_cp, (6, 7))
            pe.wait_ge(s_tot_ok, 1)
            t.matmul(PS[:NP, 5, 0:NB], upper[:NP, :NP], tot, start=True, stop=True)
            t.matmul(PS[:, 5, 16:16 + NB], ones[:NP, 0:128], tot, start=True, stop=True).then_inc(s_prefix_ps, 1)
            pe.wait_ge(s_wg_in, 48)
            pe.wait_ge(s_xt_cp, NB)
            node_product(blk_of(xT), lambda k: w_gat[:, k, :], KT, s_h_ps, s_h_cp, (6, 7))
            pe.wait_ge(s_wa_ok, 1)
            rows_product(wa, 2 * H, xT, s_rows_ps, 0)
            cols_product(wa, 2 * H, xT, s_cols_ps, 3)
            pe.wait_ge(s_wk_in, 32)
            pe.wait_ge(s_h_cp, NB)
            node_product(blk_of(xT), lambda k: w_skip[:, k, :], KT, s_skip_ps, s_skip_cp, (6, 7))
            pe.wait_ge(s_rows_cp, 3)
            pe.wait_ge(s_cols_cp, 1)
            pe.wait_ge(s_prefix_cp, 1)

            with pe.Fori(0, G // 2) as i:
                for par in range(2):
                    pe.wait_ge(s_oh_ok, i * 2 + (par + 1))
                    pe.wait_ge(s_cnt_flushed, i * 2 + (par + 1))
                    for k in range(GT):
                        for q in range(3):
                            n0, n1 = q * 512, min(N, (q + 1) * 512)
                            ins = t.matmul(PS[:NP, 3 * par + q, 0:n1 - n0], oh_dst[:, par * GT + k, 0:NP],
                                           oh_src[:, par * GT + k, n0:n1], start=(k == 0), stop=(k == GT - 1))
                    ins.then_inc(s_cnt_ps, 1)
            pe.wait_ge(s_cnt_flushed, G + 2)
            for b in range(NB):
                pe.wait_ge(s_cntf_ok, b + 1)
                if b >= 2:
                    pe.wait_ge(s_cnts_cp, b - 1)
                for j in range(NB):
                    ins = t.transpose(PS[:NP, 3 * (b % 2) + j // 4, (j % 4) * NP:(j % 4 + 1) * NP],
                                      cnt_f[:, b % 2, j * NP:(j + 1) * NP], ident[:NP, :NP])
                ins.then_inc(s_cntt_ps, 1)
            pe.wait_ge(s_uv_ok, 1)
            pe.wait_ge(s_cnts_cp, NB)
            uv_transposes(uv, 2 * H, s_uvt_ps, 0)
            pe.wait_ge(s_uvrow_ok, 1)
            with pe.Fori(0, H // 2) as i:
                for par in range(2):
                    pe.wait_ge(s_head_free, i * 2 + (par + 1))
                    for sblk in range(NB):
                        pe.wait_ge(s_p_ok, i * (2 * NB) + (par * NB + sblk + 3))
                        for d in range(NB):
                            ins = t.matmul(PS[:NP, 2 * par + d // 5, (d % 5) * (C + 1):(d % 5 + 1) * (C + 1)],
                                           pp[:, sblk % 2, d * NP:(d + 1) * NP],
                                           h_sb[:, sblk, bass.ds(i * (2 * (C + 1)) + par * (C + 1), C + 1)],
                                           start=(sblk == 0 and d % 5 == 0), stop=(sblk == NB - 1),
                                           skip_group_check=True)
                        ins.then_inc(s_pv_done, 1)
            pe.wait_ge(s_o_ok, 1)
            for b in range(NB):
                ins = t.matmul(PS[:NP, 4, :], ones[:NP, 0:NP], O[:, b, :], start=(b == 0), stop=(b == NB - 1))
            ins.then_inc(s_bn_ps, 1)
            for b in range(NB):
                pe.wait_ge(s_sq_ok, b + 1)
                ins = t.matmul(PS[:NP, 5, :], ones[:NP, 0:NP], sq[:, b % 2, :], start=(b == 0), stop=(b == NB - 1))
                ins.then_inc(s_sq_used, 1)

            pe.wait_ge(s_x1_ok, 1)
            pe.wait_ge(s_w1_in, 16 * 8)

            def src1(b, k):
                return x_sb[:, b, 0:MUL] if k == 0 else x_sb[:, b, MUL + k - 1:D:3]
            transposes(src1, None, s_xt1_ps, s_xt1_cp, (6, 7))
            pe.wait_ge(s_xt1_cp, NB)
            for b in range(NB):
                if b >= 2:
                    pe.wait_ge(s_xup_cp, b - 1)
                for k in range(4):
                    ins = t.matmul(PS[:NP, 6 + b % 2, k * MUL:(k + 1) * MUL], xT1[:, k, b * NP:(b + 1) * NP],
                                   w_up0 if k == 0 else w_up1, start=True, stop=True)
                ins.then_inc(s_xup_ps, 1)
            pe.wait_ge(s_xup_cp, NB)

            def feat(par):
                for k in range(GT):
                    ins = t.transpose(PS[:8, 7, k * 128:(k + 1) * 128],
                                      fsl[:, par, k * RW + R_F:k * RW + R_F + 8], ident[:])
                ins.then_inc(s_ft_ps, 1)

            def mlp(l, h3slot):
                lhs, rhs = ((w_m1, fT), (w_m2, hid[:, 0, :]), (w_m3, hid[:, 1, :]))[l]
                t.matmul(PS[:HID, 6, :], lhs, rhs, start=True, stop=True).then_inc(s_mlp_ps, 1)

            def tpw(k, h3slot):
                t.matmul(PS[:, k % 2, :], hid[:, 2 + h3slot, k * 128:(k + 1) * 128], w_m4, start=True, stop=True)\
                    .then_inc(s_tpw_ps, 1)

            def scat(par, k):
                pr = prod[:, k, :].rearrange("p (j q n) -> p j q n", j=2, q=4)
                sl = sel[:, par * GT + k, :]
                t.matmul(PS[:NP, 2 + 2 * par, :], sl[:, 0:NP], prod[:, k, 0:4 * MUL], start=(k == 0), stop=(k == GT - 1))
                outv = PS[:NP, 3 + 2 * par, :].rearrange("p (q n) -> p q n", q=4)
                for m in range(3):
                    ins = t.matmul(outv[:, m:4:3 - m, :], sl[:, (m + 1) * NP:(m + 2) * NP],
                                   pr[:, 1, 0:m + 2:m + 1, :],
                                   start=(k == 0 and m == 0), stop=(k == GT - 1), skip_group_check=True)
                ins.then_inc(s_scat_done, 1)
            pe.wait_ge(s_fs_ok, 1)
            feat(0)
            pe.wait_ge(s_ft_cp, 1)
            for l in range(3):
                if l:
                    pe.wait_ge(s_hid_ok, l)
                mlp(l, 0)
            pe.wait_ge(s_hid_ok, 3)
            tpw(0, 0)
            with pe.Fori(0, G // 2) as i:
                for par in range(2):
                    g1 = i * 2 + (par + 1)
                    pe.wait_ge(s_fs_ok, i * 2 + (par + 2))
                    feat(1 - par)
                    pe.wait_ge(s_acc_free, i * 2 + (par + 1))
                    for k in range(GT):
                        T = i * 8 + (4 * par + k)
                        if k == 0:
                            pe.wait_ge(s_ft_cp, i * 2 + (par + 2))
                            pe.nop(nofuse=True)
                            mlp(0, None)
                        elif k < 3:
                            pe.wait_ge(s_hid_ok, i * 6 + (3 * par + 3 + k))
                            pe.nop(nofuse=True)
                            mlp(k, None)
                        else:
                            pe.wait_ge(s_hid_ok, i * 6 + (3 * par + 6))
                        pe.wait_ge(s_prod_ok, i * 8 + (4 * par + k + 1))
                        tpw((k + 1) % GT, par if k < 3 else 1 - par)
                        pe.wait_ge(s_sel_ok, i * 8 + (4 * par + k + 1))
                        pe.wait_ge(s_prod_ok, i * 8 + (4 * par + k + 2))
                        scat(par, k)
            pe.wait_ge(s_acc_done, 1)
            for b in range(NB):
                if b >= 2:
                    pe.wait_ge(s_mt_cp, 2 * (b - 1))
                for c in range(8):
                    ins = t.transpose(PS[:, 2 * (b % 2) + c // 4, (c % 4) * 128:(c % 4) * 128 + NP],
                                      acc[:, b * 1024 + c * 128:b * 1024 + (c + 1) * 128], ident[:NP, :NP])
                    if c % 4 == 3:
                        ins.then_inc(s_mt_ps, 1)
                pe.wait_ge(s_mt_cp, 2 * (b + 1))
                if b >= 2:
                    pe.wait_ge(s_y1_cp, b - 1)
                for q in range(4):
                    pair = ((0, w_o0[:, 0, :]), (7, w_o0[:, 1, :])) if q == 0 else \
                           ((3 + q, w_o1[:, 0, :]), (q, w_o1[:, 1, :]))
                    for n, (c, w) in enumerate(pair):
                        ins = t.matmul(PS[:NP, 4 + b % 2, q * MUL:(q + 1) * MUL], msgT[:, b % 2, c * NP:(c + 1) * NP], w,
                                       start=(n == 0), stop=(n == 1))
                ins.then_inc(s_y1_ps, 1)

            def aggregate(done, copied, den, banks, ready):
                for b in range(NB):
                    if ready is not None and b == 0:
                        pe.wait_ge(*ready)
                    if b >= 2:
                        pe.wait_ge(copied, b - 1)
                    for k in range(NB):
                        ins = t.matmul(PS[:NP, banks[b % 2], :], P50[:, k, b * NP:(b + 1) * NP], x_sb[:, k, :],
                                       start=(k == 0), stop=(k == NB - 1))
                    if den:
                        for k in range(NB):
                            ins = t.matmul(PS[:NP, banks[b % 2] + 2, 0:2], P50[:, k, b * NP:(b + 1) * NP], ones[:NP, 0:2],
                                           start=(k == 0), stop=(k == NB - 1))
                    ins.then_inc(done, 1)

            pe.wait_ge(s_x2_ok, 1)
            transposes(lambda b, k: x_sb[:, b, k * 128:(k + 1) * 128], None, s_xt2_ps, s_xt2_cp, (6, 7))
            pe.wait_ge(s_wa2_ok, 1)
            pe.wait_ge(s_xt2_cp, NB)
            rows_product(wa, 2, xT2, s_rows2_ps, 0)
            cols_product(wa, 2, xT2, s_cols2_ps, 3)
            pe.wait_ge(s_uv2_ok, 1)
            pe.wait_ge(s_rows2_cp, 3)
            uv_transposes(uv, 2, s_uvt2_ps, 0)
            pe.wait_ge(s_uvrow2_ok, 1)
            aggregate(s_l2_agg, s_l2_cp, True, (4, 5), (s_p2_ok, NB))
            pe.wait_ge(s_l2_cp, NB)
            transposes(lambda b, k: agg[:, b, k * 128:(k + 1) * 128], None, s_at_ps, s_at_cp, (6, 7))
            pe.wait_ge(s_at_cp, NB)

            def spline_step(slot, first, last):
                for b in range(HB):
                    for k in range(KT):
                        ins = t.matmul(PS[:NP, b, :], basis[:, slot, (k * HB + b) * NP:(k * HB + b + 1) * NP],
                                       w_sp[:, slot, k * D:(k + 1) * D], start=(first and k == 0), stop=(last and k == KT - 1),
                                       skip_group_check=True)
                ins.then_inc(s_sp_free, 1)
            for half in range(2):
                if half:
                    pe.wait_ge(s_y2_cp, HB)
                pe.wait_ge(s_wsp_in0, 16 * (5 * half + 1))
                pe.wait_ge(s_silu_ok, half + 1)
                spline_step(0, True, False)
                with pe.Fori(0, NSPL // 2) as i:
                    for par in range(2):
                        slot = 1 - par
                        if slot == 0:
                            pe.wait_ge(s_wsp_in0, i * 16 + 16 * (5 * half + 2))
                        else:
                            pe.wait_ge(s_wsp_in1, i * 16 + 16 * (4 * half + 1))
                        pe.wait_ge(s_basis_ok, i * 2 + (8 * half + par + 1))
                        spline_step(slot, False, False)
            pe.wait_ge(s_x3_ok, 1)
            aggregate(s_l3_agg, s_l3_cp, False, (0, 1), (s_p3_ok, NB))
            transposes(lambda b, k: x_sb[:, b, k * 128:(k + 1) * 128], None, s_xt3_ps, s_xt3_cp, (6, 7))
            pe.wait_ge(s_xt3_cp, NB)
            transposes(lambda b, k: nm[:, b, k * 128:(k + 1) * 128], lambda b: (s_l3_cp, b + 1), s_nt_ps, s_nt_cp, (6, 7))
            pe.wait_ge(s_nt_cp, NB)
            pe.wait_ge(s_wl3_in, 16)
            node_product(lambda b, k: (xT3 if k < KT else nmT)[:, k % KT, b * NP:(b + 1) * NP],
                         lambda k: w_l3[:, k, :], 2 * KT, s_y3_ps, s_y3_cp, (4, 5))

        @block.scalar
        def _(act):
            A = nc.scalar.activation

            def evac_T(dst, done, copied, banks):
                for b in range(NB):
                    act.wait_ge(done, b + 1)
                    A(dst[:, :, b * NP:(b + 1) * NP],
                      PS[:, banks[b % 2], :].rearrange("p (k n) -> p k n", k=KT)[:, :, 0:NP], ACT.Copy).then_inc(copied, 1)

            def evac_rows(dst, nr, done, copied, b0):
                for q in range(3):
                    n0, n1 = q * 512, min(N, (q + 1) * 512)
                    act.wait_ge(done, q + 1)
                    A(dst[:, n0:n1], PS[:nr, b0 + q, 0:n1 - n0], ACT.Copy).then_inc(copied, 1)

            def evac_uv(dst, nr, b0, ok, done):
                act.wait_ge(done, 1)
                for q in range(3):
                    n0, n1 = q * 4 * NP, min(N, (q + 1) * 4 * NP)
                    ins = A(dst[:, n0:n1], PS[:nr, b0 + q, 0:n1 - n0], ACT.Copy)
                ins.then_inc(ok, 1)

            evac_T(xT, s_xt_ps, s_xt_cp, (6, 7))
            for b in range(NB):
                act.wait_ge(s_h_ps, b + 1)
                A(h4[:, b, :, 0:C], PS[:NP, 6 + b % 2, :].rearrange("p (h c) -> p h c", h=H), ACT.Copy).then_inc(s_h_cp, 1)
            evac_rows(rows16, 2 * H, s_rows_ps, s_rows_cp, 0)
            act.wait_ge(s_cols_ps, 1)
            A(sc[:].rearrange("p b n -> p (b n)"), PS[:NP, 3, 0:NB * 2 * H], ACT.Copy).then_inc(s_cols_cp, 1)
            act.wait_ge(s_rows_out, 16)
            for b in range(NB):
                act.wait_ge(s_cntt_ps, b + 1)
                for q in range(3):
                    j0, j1 = 4 * q, min(NB, 4 * q + 4)
                    ins = A(cnt_s[:, j0:j1, b * NP:(b + 1) * NP],
                            PS[:NP, 3 * (b % 2) + q, 0:(j1 - j0) * NP].rearrange("p (j n) -> p j n", n=NP), ACT.Copy)
                ins.then_inc(s_cnts_cp, 1)
            evac_uv(uvrow_sb, 2 * H, 0, s_uvrow_ok, s_uvt_ps)
            with act.Fori(0, H // 2) as i:
                for par in range(2):
                    for sblk in range(NB):
                        act.wait_ge(s_t_ok, i * (2 * NB) + (par * NB + sblk + 1))
                        act.wait_ge(s_p_ok, i * (2 * NB) + (par * NB + sblk + 1))
                        A(ee[:, sblk % 2, :], tt[:, sblk % 2, :], ACT.Exp, bias=c2[:, par, sblk:sblk + 1]).then_inc(s_e_ok, 1)
            for b in range(NB):
                act.wait_ge(s_cen_ok, b + 1)
                if b >= 2:
                    act.wait_ge(s_sq_used, b - 1)
                A(sq[:, b % 2, :], O[:, b, :], ACT.Square).then_inc(s_sq_ok, 1)
            act.wait_ge(s_var_ok, 1)
            A(scl_b, mean_b, ACT.Sqrt, bias=epsc[:NP, :]).then_inc(s_bnsd_ok, 1)
            for b in range(NB):
                act.wait_ge(s_bn_ok, b + 1)
                A(O[:, b, :], O[:, b, :], ACT.Gelu).then_inc(s_gelu_ok, 1)

            def ln_sqrt(ready, ok):
                act.wait_ge(ready, 1)
                A(rstd[:], mv[:, :, 1], ACT.Sqrt, bias=epsc[:NP, :]).then_inc(ok, 1)
            ln_sqrt(s_ln1_var, s_ln1_sd)

            evac_T(xT1, s_xt1_ps, s_xt1_cp, (6, 7))
            for b in range(NB):
                act.wait_ge(s_xup_ps, b + 1)
                if b >= 2:
                    act.wait_ge(s_xup_out0 if b % 2 == 0 else s_xup_out1, 16 * (b // 2))
                A(xup_st[:, b % 2, :], PS[:NP, 6 + b % 2, :], ACT.Copy, scale=float(MUL) ** -0.5).then_inc(s_xup_cp, 1)

            def layer(l, slot, scale):
                A(hid[:, slot, :], PS[:HID, 6, :], ACT.Silu, scale=scale).then_inc(s_hid_ok, 1)

            def slot_load(g, par):
                A(fsl[:, par, :], rec_sb[:, bass.ds(g, 1), :].rearrange("p a k -> p (a k)"), ACT.Copy).then_inc(s_fs_ok, 1)
            sc0 = 8.0 ** -0.5
            sc1 = SILU2 * float(HID) ** -0.5
            slot_load(0, 0)
            slot_load(1, 1)
            act.wait_ge(s_ft_ps, 1)
            A(fT, PS[:8, 7, :], ACT.Copy).then_inc(s_ft_cp, 1)
            for l in range(3):
                act.wait_ge(s_mlp_ps, l + 1)
                layer(l, l, sc0 if l == 0 else sc1)
            with act.Fori(0, G // 2) as i:
                for par in range(2):
                    act.wait_ge(s_ft_ps, i * 2 + (par + 2))
                    A(fT, PS[:8, 7, :], ACT.Copy).then_inc(s_ft_cp, 1)
                    slot_load(i * 2 + (2 + par), par)
                    for l in range(3):
                        act.wait_ge(s_mlp_ps, i * 6 + (3 * par + 3 + l + 1))
                        layer(l, l if l < 2 else 3 - par, sc0 if l == 0 else sc1)
            for b in range(NB):
                for q in range(2):
                    act.wait_ge(s_mt_ps, 2 * b + q + 1)
                    if b >= 2 and q == 0:
                        act.wait_ge(s_y1_ps, b - 1)
                    v = PS[:, 2 * (b % 2) + q, :].rearrange("p (k n) -> p k n", k=4)[:, :, 0:NP]
                    dstv = msgT[:, b % 2, q * 4 * NP:(q + 1) * 4 * NP].rearrange("p (k n) -> p k n", k=4)
                    if q == 0:
                        ins = A(dstv, v, ACT.Copy)
                    else:
                        A(dstv[:, 0:3, :], v[:, 0:3, :], ACT.Copy)
                        ins = A(dstv[:, 3, :], v[:, 3, :], ACT.Copy, scale=3.0 ** -0.5)
                    ins.then_inc(s_mt_cp, 1)
            ln_sqrt(s_ln2_var, s_ln2_sd)

            evac_T(xT2, s_xt2_ps, s_xt2_cp, (6, 7))
            evac_rows(rows2, 2, s_rows2_ps, s_rows2_cp, 0)
            act.wait_ge(s_cols2_ps, 1)
            A(sc[:, :, 0:2], PS[:NP, 3, 0:NB * 2].rearrange("p (b n) -> p b n", n=2), ACT.Copy).then_inc(s_cols2_cp, 1)
            evac_uv(uvrow2, 2, 0, s_uvrow2_ok, s_uvt2_ps)
            for k in range(NB):
                act.wait_ge(s_t2_ok, k + 1)
                if k >= 2:
                    act.wait_ge(s_p2_ok, k - 1)
                A(e2[:, k % 2, :], t2[:, k % 2, :], ACT.Exp, bias=c2[:, 0, k:k + 1]).then_inc(s_e2_ok, 1)
            evac_T(aggT, s_at_ps, s_at_cp, (6, 7))

            HW = HB * NP
            for half in range(2):
                av = aggT[:, :, half * HW:(half + 1) * HW]

                def as3(v):
                    return v.rearrange("p (k n) -> p k n", k=KT)
                if half == 0:
                    act.wait_ge(s_at_cp, NB)
                act.wait_ge(s_sp_free, 10 * half + 1)
                A(as3(basis[:, 0, :]), av, ACT.Silu).then_inc(s_silu_ok, 1)
                with act.Fori(0, NSPL // 2) as i:
                    for par in range(2):
                        act.wait_ge(s_cslot_ok, i * 2 + (8 * half + par + 1))
                        A(as3(sv), av, ACT.Abs, scale=KAPPA / STEP, bias=cslot[:, par:par + 1]).then_inc(s_sv_ok, 1)
                        act.wait_ge(s_sa_ok, i * 4 + (16 * half + 2 * par + 1))
                        A(sa2, sa, ACT.Square).then_inc(s_sq2_ok, 1)
                        act.wait_ge(s_sa_ok, i * 4 + (16 * half + 2 * par + 2))
                        A(sb2, sbb, ACT.Square).then_inc(s_sq2_ok, 1)
            ln_sqrt(s_ln3_var, s_ln3_sd)
            evac_T(xT3, s_xt3_ps, s_xt3_cp, (6, 7))
            evac_T(nmT, s_nt_ps, s_nt_cp, (6, 7))
            ln_sqrt(s_ln4_var, s_ln4_sd)

        @block.vector
        def _(dve):
            v = nc.vector
            ch = Chain(dve, s_dve_chain)
            link = ch.link

            v.memset(empty, 0.0).then_inc(s_empty_ok, 1)
            dve.wait_ge(s_empty_ok, 1)
            v.memset(empty[:, :, 0:1], -1.0).then_inc(s_empty_ok, 1)
            v.memset(blk, 0.0)
            v.memset(h4[:, :, :, C:C + 1], 1.0)
            v.memset(posf, 0.0)
            dve.wait_ge(s_dst_in, 16)
            link(v.tensor_copy(dstf, dsti))
            for b in range(1, NB):
                link(v.scalar_tensor_tensor(blk, dstf, float(b * NP), blk, ALU.is_ge, ALU.add))
            dve.wait_ge(s_consts, 1)
            for b in range(NB):
                link(v.tensor_scalar(mask[:, b, :], blk, float(b), None, ALU.is_equal))
                ins = v.tensor_tensor_scan(cum[:, b, :], ones[:NP, 0:EC], mask[:, b, :], 0.0, ALU.mult, ALU.add)
            link(ins)
            v.tensor_copy(tot, cum[:, :, EC - 1]).then_inc(s_tot_ok, 1)
            dve.wait_ge(s_rec_in, 48)
            v.scalar_tensor_tensor(rec[:, :, R_DL], blk, float(-NP), dstf, ALU.mult, ALU.add)
            v.tensor_copy(rec[:, :, R_SRCF], srci)
            v.tensor_copy(rec[:, :, R_SRCI].bitcast(i32), srci)
            v.memset(rec[:, :, 3], 0.0)
            v.tensor_copy(rec[:, :, R_Y:R_Y + 4], a4)
            v.tensor_copy(rec[:, :, R_F:R_F + 8], a8)
            dve.wait_ge(s_prefix_ps, 1)
            link(v.tensor_scalar(ngi, PS[:, 5, 16:16 + NB], float(GS - 1), None, ALU.add))
            link(v.tensor_scalar(ngi, ngi, GS.bit_length() - 1, None, ALU.arith_shift_right))
            link(v.tensor_copy(ngf, ngi))
            link(v.tensor_tensor_scan(gend, ones[:, :NB], ngf, 0.0, ALU.mult, ALU.add))
            link(v.tensor_tensor(gbase, gend, ngf, ALU.subtract))
            link(v.tensor_scalar(ngf, gbase, float(GS), -1.0, ALU.mult, ALU.add))
            ins = v.tensor_tensor(base, PS[:NP, 5, 0:NB], ngf[:NP], ALU.add)
            ins.then_inc(s_prefix_cp, 1)
            dve.wait_ge(s_prefix_cp, 1)
            for b in range(NB):
                link(v.scalar_tensor_tensor(ge, cum[:, b, :], base[:, b:b + 1], mask[:, b, :], ALU.add, ALU.mult))
                link(v.tensor_tensor(posf, posf, ge, ALU.add))
            v.tensor_copy(pos, posf).then_inc(s_rec_ok, 1)
            v.memset(gbf, 0.0)
            link(v.tensor_copy(gf, gi))
            for b in range(1, NB):
                link(v.scalar_tensor_tensor(gbf, gf, gbase[0:1, b:b + 1], gbf, ALU.is_ge, ALU.add))
            link(v.tensor_copy(gblk[:], gbf))

            dve.wait_ge(s_wg_in, 48)
            ptmp = at(12512, [128, 488])
            for k in range(KT):
                for q in range(2):
                    for hh in range(2):
                        c0 = hh * 256
                        link(v.tensor_tensor(ptmp[:, 0:256], w_gat[:, k, c0:c0 + 256], att_b[:, q, c0:c0 + 256], ALU.mult))
                        link(v.tensor_reduce(wa[:, k, q * H + hh * 4:q * H + hh * 4 + 4],
                                             ptmp[:, 0:256].rearrange("p (h c) -> p h c", h=4), X, ALU.add))
            dve.sem_inc(s_wa_ok, 1)
            dve.wait_ge(s_wk_in, 32)
            for b in range(NB):
                dve.wait_ge(s_skip_ps, b + 1)
                ins = v.tensor_tensor(x_sb[:, b, :], x_sb[:, b, :], PS[:NP, 6 + b % 2, :], ALU.add)
                ins.then_inc(s_skip_cp, 1)
                dve.wait_ge(s_skip_cp, b + 1)
                v.tensor_tensor(x_sb[:, b, :], x_sb[:, b, :], b_skip_b, ALU.add)

            dve.sem_inc(s_cnt_flushed, 2)
            link(v.memset(cnt_d[:], 0))
            dve.wait_ge(s_recs_in, 16)

            def onehots(g, par):
                link(v.tensor_copy(rslot[:, par, :], rec_sb[:, bass.ds(g, 1), :].rearrange("p a k -> p (a k)")))
                for k in range(GT):
                    r = rslot[:, par, k * RW:(k + 1) * RW]
                    v.tensor_scalar(oh_src[:, par * GT + k, :], iota_src[:], r[:, R_SRCF:R_SRCF + 1], None, ALU.is_equal)
                    ins = v.tensor_scalar(oh_dst[:, par * GT + k, 0:NP], iota_dsth[:], r[:, R_DL:R_DL + 1], None, ALU.is_equal)
                ins.then_inc(s_oh_ok, 1)

            def flush_counts(g, par, ps_count):
                bv = dve.value_load(gblk[0:1, bass.ds(g, 1)], min_val=0, max_val=NB - 1)
                dve.wait_ge(s_cnt_ps, ps_count)
                dve.wait_ge(s_cnt_flushed, ps_count + 1)
                dstv = cnt_d[:, bass.ds(bv * N, N)]
                psv = PS[:NP, 3 * par:3 * par + 3, :].rearrange("p a n -> p (a n)")[:, 0:N]
                v.tensor_tensor(dstv, psv, dstv, ALU.add).then_inc(s_cnt_flushed, 1)
            onehots(0, 0)
            with dve.Fori(0, G // 2 - 1) as i:
                ch.enter(i, 2)
                onehots(i * 2 + 1, 1)
                flush_counts(i * 2, 0, i * 2 + 1)
                onehots(i * 2 + 2, 0)
                flush_counts(i * 2 + 1, 1, i * 2 + 2)
            ch.leave(G // 2 - 1)
            onehots(G - 1, 1)
            flush_counts(G - 2, 0, G - 1)
            flush_counts(G - 1, 1, G)
            dve.wait_ge(s_cnt_flushed, G + 2)
            cd = cnt_d[:].rearrange("p (b n) -> p b n", n=N)
            for b in range(NB):
                if b >= 2:
                    dve.wait_ge(s_cntt_ps, b - 1)
                v.tensor_copy(cnt_f[:, b % 2, :], cd[:, b, :]).then_inc(s_cntf_ok, 1)
            link(v.tensor_reduce(deg[:], cd, X, ALU.add))

            def make_mask(mk, cm, loops):
                link(v.tensor_scalar(mk, cm, 0.0, NEG, ALU.is_equal, ALU.mult))
                if loops:
                    for b in range(NB):
                        d = mk[:, b, b * NP:(b + 1) * NP]
                        ins = v.scalar_tensor_tensor(d, ident[:NP, :NP], 0.0, d, ALU.is_equal, ALU.mult)
                    link(ins)
            make_mask(nomask, cd, True)
            dve.wait_ge(s_cnts_cp, NB)

            def self_loops(op):
                for b in range(NB):
                    d = cnt_s[:, b, b * NP:(b + 1) * NP]
                    ins = v.tensor_tensor(d, d, ident[:NP, :NP], op)
                link(ins)
            self_loops(ALU.add)
            dve.sem_inc(s_asb_free, 2)
            dve.sem_inc(s_mask_ok, 1)

            with dve.Fori(0, H // 2) as i:
                ch.enter(i, 2 * NB)
                for par in range(2):
                    dve.wait_ge(s_asb_in0 if par == 0 else s_asb_in1, i * 16 + 16)
                    for b in range(NB):
                        dve.nop(nofuse=True)
                        link(v.tensor_tensor_reduce(out=junk, in0=nomask[:, b, :], in1=as_b[:, par, :], scale=1.0,
                                                    scalar=NEG, op0=ALU.add, op1=ALU.max, accum_out=mx1[:, b:b + 1]))
                    v.tensor_copy(mxh[:, bass.ds(i * 2 + par, 1), :].rearrange("p a b -> p (a b)"), mx1[:]).then_inc(s_asb_free, 1)
                    dve.wait_ge(s_asb_free, i * 2 + (par + 3))
            ch.leave(H // 2)
            dve.wait_ge(s_asb_free, 2 + H)
            dve.sem_inc(s_max_done, 1)

            def softmax_terms(nh, center, neigh, mxv, guard):
                mt = at(18200, [NP, NB * nh]) if nh > 1 else at(27000, [NP, NB])
                mt3 = mt.rearrange("p (b h) -> p b h", h=nh)
                link(v.tensor_tensor(mt3, mxv, center, ALU.add))
                link(v.scalar_tensor_tensor(mt, mt, SLOPE, mt, ALU.mult, ALU.max))
                link(v.tensor_tensor(uv[:, :, 0:nh], center, mt3, ALU.subtract))
                link(v.scalar_tensor_tensor(uv[:, :, nh:2 * nh], center, SLOPE, mt3, ALU.mult, ALU.subtract))
                v.tensor_scalar(sc8[:, 0:nh, :], neigh, 1.0 - SLOPE, None, ALU.mult)
                link(v.tensor_scalar(sc2[:, 0:nh, :], neigh, SLOPE, None, ALU.mult))
            softmax_terms(H, sc[:, :, H:2 * H], sc[:, :, 0:H].rearrange("p b h -> p h b"),
                          mxh[:].rearrange("p h b -> p b h"), False)
            dve.sem_inc(s_uv_ok, 1)
            dve.sem_inc(s_uv_free, 2)
            dve.sem_inc(s_head_free, 2)
            dve.sem_inc(s_p_ok, 2)
            dve.sem_inc(s_pv_done, 2)

            def t_tile(dst, U, V, cc, ok):
                v.scalar_tensor_tensor(dst, U, cc, V, ALU.add, ALU.max).then_inc(ok, 1)

            def p_tile(dst, e, cm, ok):
                v.scalar_tensor_tensor(dst, e, 1.0, cm, ALU.min, ALU.mult).then_inc(ok, 1)
            with dve.Fori(0, H // 2) as i:
                ch.enter(i, 4)
                for par in range(2):
                    hh = i * 2 + par
                    v.tensor_copy(c8[:, par, :], sc8[:, bass.ds(hh, 1), :].rearrange("p a b -> p (a b)"))
                    link(v.tensor_copy(c2[:, par, :], sc2[:, bass.ds(hh, 1), :].rearrange("p a b -> p (a b)")))
                    dve.wait_ge(s_uv_in0 if par == 0 else s_uv_in1, i * 32 + 32)
                    t_tile(tt[:, 0, :], UV[:, par, 0, :], UV[:, par, 1, :], c8[:, par, 0:1], s_t_ok)
                    for sblk in range(NB):
                        n0 = par * NB + sblk
                        if sblk < NB - 1:
                            t_tile(tt[:, (sblk + 1) % 2, :], UV[:, par, 0, :], UV[:, par, 1, :], c8[:, par, sblk + 1:sblk + 2], s_t_ok)
                        dve.wait_ge(s_e_ok, i * (2 * NB) + (n0 + 1))
                        dve.wait_ge(s_pv_done, i * (2 * NB) + (n0 + 1))
                        p_tile(pp[:, sblk % 2, :], ee[:, sblk % 2, :], cnt_s[:, sblk, :], s_p_ok)
                    dve.wait_ge(s_pv_done, i * (2 * NB) + (par * NB + NB + 2))
                    pv = PS[:NP, 2 * par:2 * par + 2, 0:5 * (C + 1)].rearrange("p q (d c) -> p q d c", c=C + 1)
                    r4 = rden[:].rearrange("p (q d) -> p q d", q=2)
                    link(v.reciprocal(r4, pv[:, :, :, C]))
                    O5 = O[:, :, bass.ds(hh * C, C)]
                    for q in range(2):
                        ins = v.tensor_tensor(O5[:, 5 * q:5 * q + 5, :], pv[:, q, :, 0:C],
                                              rden[:, 5 * q:5 * q + 5].unsqueeze(2).to_broadcast([NP, 5, C]), ALU.mult)
                    ins.then_inc(s_head_free, 1)
                    dve.wait_ge(s_head_free, i * 2 + (par + 3))
                    dve.sem_inc(s_uv_free, 1)
            ch.leave(H // 2)
            self_loops(ALU.subtract)

            dve.wait_ge(s_bn_in, 48)
            for b in range(NB):
                ins = v.tensor_tensor(O[:, b, :], O[:, b, :], bias_b, ALU.add)
            link(ins)
            dve.sem_inc(s_o_ok, 1)
            dve.wait_ge(s_bn_ps, 1)
            link(v.tensor_scalar(mean_b, PS[:NP, 4, :], 1.0 / N, None, ALU.mult))
            for b in range(NB):
                v.tensor_tensor(O[:, b, :], O[:, b, :], mean_b, ALU.subtract).then_inc(s_cen_ok, 1)
            dve.wait_ge(s_sq_used, NB)
            v.tensor_scalar(mean_b, PS[:NP, 5, :], 1.0 / N, None, ALU.mult).then_inc(s_var_ok, 1)
            dve.wait_ge(s_bnsd_ok, 1)
            link(v.reciprocal(scl_b, scl_b))
            link(v.tensor_tensor(scl_b, scl_b, gam_b, ALU.mult))
            for b in range(NB):
                link(v.tensor_tensor(O[:, b, :], O[:, b, :], scl_b, ALU.mult))
                v.tensor_tensor(O[:, b, :], O[:, b, :], bet_b, ALU.add).then_inc(s_bn_ok, 1)
            for b in range(NB):
                dve.wait_ge(s_gelu_ok, b + 1)
                ins = v.tensor_tensor(x_sb[:, b, :], x_sb[:, b, :], O[:, b, :], ALU.add)
            link(ins)

            def layernorm(var_ok, sd_ok, ok, last=False):
                for b in range(NB):
                    link(v.bn_stats(bst[:, b, :], x_sb[:, b, :]))
                    ins = v.bn_aggr(mv[:, b, :], bst[:, b, :])
                ins.then_inc(var_ok, 1)
                dve.wait_ge(sd_ok, 1)
                link(v.reciprocal(rstd[:], rstd[:]))
                for b in range(NB):
                    ins = v.tensor_scalar(x_sb[:, b, :], x_sb[:, b, :], mv[:, b, 0:1], rstd[:, b:b + 1], ALU.subtract, ALU.mult)
                ins.then_inc(ok, 1)
                dve.wait_ge(ok, 1)
                if last:
                    dve.sem_inc(s_final_ok, 1)
            layernorm(s_ln1_var, s_ln1_sd, s_x1_ok, False)

            v.memset(acc, 0.0).then_inc(s_acc_zero, 1)
            dve.wait_ge(s_acc_zero, 1)
            dve.wait_ge(s_xup_cp, NB)
            dve.sem_inc(s_prod_ok, 1)
            dve.sem_inc(s_scat_done, GT)
            dve.sem_inc(s_acc_free, 2)

            def products(par, k, T, gath):
                dve.wait_ge(s_tpw_ps, T(1))
                dve.wait_ge(s_gath[par * GT + k], gath)
                dve.wait_ge(s_scat_done, T(1))
                w = PS[:, k % 2, :].rearrange("p (q n) -> p q n", q=4)
                xg = ring[:, par * GT + k, :].rearrange("p (q n) -> p q n", q=4)
                pr = prod[:, k, :].rearrange("p (j q n) -> p j q n", j=2, q=4)
                v.tensor_tensor(pr[:, :, 0, :], w[:, 0:2, :], xg[:, 0:1, :].to_broadcast([128, 2, MUL]), ALU.mult)
                v.tensor_tensor(pr[:, :, 1:4, :], w[:, 2:4, :].unsqueeze(2).to_broadcast([128, 2, 3, MUL]),
                                xg[:, 1:4, :].unsqueeze(1).to_broadcast([128, 2, 3, MUL]), ALU.mult).then_inc(s_prod_ok, 1)

            def flush(g, par, n_scat):
                bv = dve.value_load(gblk[0:1, bass.ds(g, 1)], min_val=0, max_val=NB - 1)
                dve.wait_ge(s_scat_done, n_scat)
                dve.wait_ge(s_acc_free, g + 2)
                d = acc[:, bass.ds(bv * 1024, 1024)]
                psv = PS[:NP, 2 + 2 * par:4 + 2 * par, :].rearrange("p a n -> p (a n)")
                v.tensor_tensor(d, psv, d, ALU.add).then_inc(s_acc_free, 1)
            for k in range(GT):
                products(0, k, lambda m, k=k: k + m, 16)
            with dve.Fori(0, G // 2 - 1) as i:
                for par in (1, 0):
                    g = i * 2 + (2 - par)
                    off = 4 * (2 - par)
                    for k in range(GT):
                        products(par, k, lambda m, k=k: i * 8 + (off + k + m), i * 16 + (16 if par else 32))
                        if k == 1:
                            flush(i * 2 + (1 - par), 1 - par, i * 8 + (off + GT))
            for k in range(GT):
                products(1, k, lambda m, k=k: (G - 1) * GT + k + m, 16 * (G // 2))
                if k == 1:
                    flush(G - 2, 0, (G - 1) * GT + GT)
            flush(G - 1, 1, G * GT + GT)
            dve.wait_ge(s_acc_free, G + 2)
            dve.sem_inc(s_acc_done, 1)
            oscale = SILU2 * HID ** -0.5 * (2 * MUL) ** -0.5 / 10.0
            for b in range(NB):
                dve.wait_ge(s_y1_ps, b + 1)
                v.scalar_tensor_tensor(x_sb[:, b, 0:MUL], PS[:NP, 4 + b % 2, 0:MUL], oscale, x_sb[:, b, 0:MUL], ALU.mult, ALU.add)
                xv = x_sb[:, b, MUL:D].rearrange("p (u m) -> p m u", m=3)
                v.scalar_tensor_tensor(xv, PS[:NP, 4 + b % 2, MUL:D].rearrange("p (m u) -> p m u", m=3), oscale, xv,
                                       ALU.mult, ALU.add).then_inc(s_y1_cp, 1)
            dve.wait_ge(s_y1_cp, NB)
            layernorm(s_ln2_var, s_ln2_sd, s_x2_ok, False)

            dve.wait_ge(s_wl2_in, 48)
            for k in range(KT):
                for q in range(2):
                    link(v.tensor_tensor(tmp2, w_l2[:, k, :], a_b[:, q, :], ALU.mult))
                    link(v.tensor_reduce(wa[:, k, q:q + 1], tmp2, X, ALU.add))
            dve.sem_inc(s_wa2_ok, 1)
            make_mask(nomask2, cnt_s[:], False)
            dve.wait_ge(s_st_in, 16)
            for b in range(NB):
                link(v.tensor_tensor_reduce(out=junk2, in0=nomask2[:, b, :], in1=st_b, scale=1.0, scalar=NEG,
                                            op0=ALU.add, op1=ALU.max, accum_out=mx1[:, b:b + 1]))
            link(v.scalar_tensor_tensor(mx1[:], mx1[:], 0.5 * NEG, mx1[:], ALU.is_gt, ALU.mult))
            dve.wait_ge(s_cols2_cp, 1)
            softmax_terms(1, sc[:, :, 0:1], sc[:, :, 1:2].rearrange("p b h -> p h b"), mx1[:].unsqueeze(2), True)
            v.tensor_copy(c8[:, 0, :], sc8[:, 0, :])
            link(v.tensor_copy(c2[:, 0, :], sc2[:, 0, :]))
            dve.sem_inc(s_uv2_ok, 1)
            dve.wait_ge(s_uv2_in, 32)
            for k in range(NB + 1):
                if k < NB:
                    t_tile(t2[:, k % 2, :], UV2[:, 0, :], UV2[:, 1, :], c8[:, 0, k:k + 1], s_t2_ok)
                if k >= 1:
                    dve.wait_ge(s_e2_ok, k)
                    p_tile(P50[:, k - 1, :], e2[:, (k - 1) % 2, :], cd[:, k - 1, :], s_p2_ok)
            for b in range(NB):
                dve.wait_ge(s_l2_agg, b + 1)
                link(v.tensor_scalar(rden[:, b:b + 1], PS[:NP, 6 + b % 2, 0:1], 0.5, None, ALU.max))
                link(v.reciprocal(rden[:, b:b + 1], rden[:, b:b + 1]))
                v.tensor_scalar(agg[:, b, :], PS[:NP, 4 + b % 2, :], rden[:, b:b + 1], None, ALU.mult).then_inc(s_l2_cp, 1)
            link(v.tensor_scalar(cen[:], cen[:], -KAPPA, KAPPA * (1.0 + 1.0 / STEP), ALU.mult, ALU.add))
            dve.wait_ge(s_at_cp, NB)
            dve.sem_inc(s_aggT_ok, 1)
            dve.sem_inc(s_sp_free, 2)
            for half in range(2):
                with dve.Fori(0, NSPL // 2) as i:
                    ch.enter(i, 4)
                    for par in range(2):
                        slot = 1 - par
                        v.tensor_copy(cslot[:, par:par + 1], cen[:, bass.ds(i * 2 + par, 1)]).then_inc(s_cslot_ok, 1)
                        dve.wait_ge(s_sv_ok, i * 2 + (8 * half + par + 1))
                        v.tensor_scalar(sa, sv, 2 * KAPPA, 2 * KAPPA, ALU.min, ALU.subtract).then_inc(s_sa_ok, 1)
                        v.tensor_scalar(sbb, sv, KAPPA, KAPPA, ALU.min, ALU.subtract).then_inc(s_sa_ok, 1)
                        dve.wait_ge(s_sq2_ok, i * 4 + (16 * half + 2 * par + 1))
                        link(v.tensor_tensor(sa2, sa2, sa, ALU.mult))
                        dve.wait_ge(s_sq2_ok, i * 4 + (16 * half + 2 * par + 2))
                        link(v.tensor_tensor(sb2, sb2, sbb, ALU.mult))
                        dve.wait_ge(s_sp_free, i * 2 + (9 * half + par + 2))
                        v.scalar_tensor_tensor(basis[:, slot, :], sb2, 4.0, sa2, ALU.mult, ALU.subtract).then_inc(s_basis_ok, 1)
                ch.leave(NSPL // 2)
                dve.wait_ge(s_sp_free, 9 * half + 11)
                for b in range(HB):
                    bb = half * HB + b
                    v.tensor_tensor(x_sb[:, bb, :], x_sb[:, bb, :], PS[:NP, b, :], ALU.add).then_inc(s_y2_cp, 1)
            dve.wait_ge(s_y2_cp, NB)
            layernorm(s_ln3_var, s_ln3_sd, s_x3_ok, False)

            for k in range(NB):
                v.tensor_copy(P50[:, k, :], cnt_s[:, k, :]).then_inc(s_p3_ok, 1)
            link(v.tensor_scalar(deg[:], deg[:], 1.0, None, ALU.max))
            link(v.reciprocal(deg[:], deg[:]))
            for b in range(NB):
                dve.wait_ge(s_l3_agg, b + 1)
                v.tensor_scalar(nm[:, b, :], PS[:NP, b % 2, :], deg[:, b:b + 1], None, ALU.mult).then_inc(s_l3_cp, 1)
            for b in range(NB):
                dve.wait_ge(s_y3_ps, b + 1)
                v.scalar_tensor_tensor(x_sb[:, b, :], PS[:NP, 4 + b % 2, :], 0.0, x_sb[:, b, :], ALU.max, ALU.add)\
                    .then_inc(s_y3_cp, 1)
            dve.wait_ge(s_y3_cp, NB)
            layernorm(s_ln4_var, s_ln4_sd, s_x4_ok, True)


_INS = ("x", "src", "dst", "edge_attr_4", "edge_attr_8", "L0_gnn_W_gat", "L0_gnn_att_src", "L0_gnn_att_dst",
        "L0_gnn_gat_bias", "L0_gnn_bn_gamma", "L0_gnn_bn_beta", "L0_gnn_W_skip", "L0_gnn_b_skip",
        "L1_gnn_W_up0", "L1_gnn_W_up1", "L1_gnn_W_mlp1", "L1_gnn_W_mlp2", "L1_gnn_W_mlp3", "L1_gnn_W_mlp4",
        "L1_gnn_W_out0", "L1_gnn_W_out1", "L2_gnn_W", "L2_gnn_a")


def kernel(**inputs):
    import numpy as _np
    import concourse.bacc as _bacc
    from concourse import mybir as _mybir
    from concourse.bass_utils import run_bass_kernel_spmd as _run

    nc = _bacc.Bacc("TRN2", target_bir_lowering=False, num_devices=1)
    laid = {name: _np.asarray(inputs[name]) for name in _INS}
    laid["base_wT"] = _np.asarray(inputs["L2_gnn_base_w"]).T
    laid["spline_wT"] = _np.asarray(inputs["L2_gnn_spline_w"]).transpose(2, 1, 0)
    laid["w_l3T"] = _np.asarray(inputs["L3_gnn_w"]).T
    arrays, args = {}, {}
    for name, v in laid.items():
        v = _np.ascontiguousarray(v)
        arrays[f"in_{name}"] = v
        args[name] = nc.dram_tensor(f"in_{name}", v.shape, _mybir.dt.from_np(v.dtype), kind="ExternalInput").ap()
    out = nc.dram_tensor("out", (N, D), _mybir.dt.float32, kind="ExternalOutput").ap()
    build(nc, args, out)
    r = _run(nc, [arrays], core_ids=[0])
    return r.results[0]["out"]
```

```python
import numpy as np
import concourse.bass as bass
from concourse import mybir
from contextlib import ExitStack

N, D, E = 1250, 512, 21250
H, C = 8, 64
MUL, HID = 128, 64
NP, NB = 125, 10
KT = D // 128
EC = E // NP
GT = 4
GS = GT * 128
G = (E + NB * (GS - 1)) // GS
G += G % 2
RW = 16
R_DL, R_SRCF, R_SRCI, R_Y, R_F = 0, 1, 2, 4, 8
NEG = -1.0e30
SLOPE = 0.2
EPS = 1e-5
SB = 10
NSPL = 8
STEP = 2.0 / 5
KAPPA = (1.0 / 6.0) ** (1.0 / 3.0)
SILU2 = 1.679177
WR = 5
LEAD = 2
POOL_P = (3, 7)
assert NB % WR == 0
HB = NB // 2
assert NP * NB == N and NP * EC == E and EC % SB == 0


class Chain:

    def __init__(self, eng, sem):
        self.eng, self.sem, self.n, self.i, self.per, self.at = eng, sem, 0, None, 0, 0

    def link(self, ins):
        ins.then_inc(self.sem, 1)
        self.at += 1
        if self.i is None:
            self.n, self.at = self.n + self.at, 0
            self.eng.wait_ge(self.sem, self.n)
        else:
            self.eng.wait_ge(self.sem, self.i * self.per + (self.n + self.at))

    def enter(self, i, per):
        self.i, self.per, self.at = i, per, 0

    def leave(self, times):
        assert self.at == self.per, (self.at, self.per)
        self.n += times * self.per
        self.i, self.at = None, 0


def build(nc, a, out):
    f32, i32, u32 = mybir.dt.float32, mybir.dt.int32, mybir.dt.uint32
    bf16, f16, u16 = mybir.dt.bfloat16, mybir.dt.float16, mybir.dt.uint16
    ALU = mybir.AluOpType
    ACT = mybir.ActivationFunctionType
    X = mybir.AxisListType.X
    ctx = ExitStack()
    with ctx:
        def sb(name, shape, dt=f32):
            return ctx.enter_context(nc.sbuf_tensor(name, shape, dt))

        def dram(name, shape, dt=f32):
            return nc.dram_tensor(name, shape, dt, kind="Internal").ap()

        def sem(name):
            return ctx.enter_context(nc.semaphore(name))

        recs = dram("recs", ((G + 2) * GS, RW))
        as_rows = dram("as_rows", (2 * H, N))
        uv_rows = dram("uv_rows", (2 * H, N))
        st_rows = dram("st_rows", (2, N))
        uv2_rows = dram("uv2_rows", (2, N))
        h3_rows = dram("h3_rows", (G // 2, 128, GS))
        xup = dram("xup", (N, D))

        x_sb = sb("x_sb", [NP, NB, D])
        cnt_d = sb("cnt_d", [NP, NB * N], u16)
        cnt_s = sb("cnt_s", [NP, NB, N], u16)
        rec_sb = sb("rec_sb", [128, G + 2, GT * RW])
        ident = sb("ident", [128, 128])
        upper = sb("upper", [128, 128])
        ones = sb("ones", [128, 192])
        iota_src = sb("iota_src", [128, N], f16)
        iota_dst = sb("iota_dst", [128, NP], f32)
        gblk = sb("gblk", [1, G + 2], i32)
        epsc = sb("epsc", [128, 1])
        mv = sb("mv", [NP, NB, 2])
        bst = sb("bst", [NP, NB, 6])
        rstd = sb("rstd", [NP, NB])
        deg = sb("deg", [NP, NB])
        ARENA = 28300
        arena = sb("arena", [128, ARENA])

        def at(off, shape, dt=f32):
            size = int(np.prod(shape[1:]))
            words = size if dt in (f32, i32, u32) else (size + 1) // 2
            assert off + words <= ARENA
            v = arena[:shape[0], off:off + words]
            if dt != f32:
                v = v.bitcast(dt)
            if len(shape) == 3:
                v = v.rearrange("p (a b) -> p a b", a=shape[1])
            if len(shape) == 4:
                v = v.rearrange("p (a b c) -> p a b c", a=shape[1], b=shape[2])
            return v

        PS = ctx.enter_context(nc.psum_tensor("PS", [128, 8, 512], f32))

        o = [0]

        def nxt(shape, dt=f32):
            v = at(o[0], shape, dt)
            o[0] += int(np.prod(shape[1:]))
            return v
        srci, dsti = nxt([NP, EC], i32), nxt([NP, EC], i32)
        dstf, blk, ge, posf = (nxt([NP, EC]) for _ in range(4))
        pos = nxt([NP, EC], u32)
        mask, cum = nxt([NP, NB, EC]), nxt([NP, NB, EC])
        a4, a8, rec = nxt([NP, EC, 4]), nxt([NP, EC, 8]), nxt([NP, EC, RW])
        EMP = 54
        assert (G + 2) * GS % (128 * EMP) == 0
        empty = nxt([128, EMP, RW])
        tot, base = nxt([NP, NB]), nxt([NP, NB])
        ngi, ngf, gend, gbase = nxt([128, NB], i32), nxt([128, NB]), nxt([128, NB]), nxt([128, NB])
        gi, gf, gbf = nxt([1, G + 2], i32), nxt([1, G + 2]), nxt([1, G + 2])
        stage_rec, stage_pos = nxt([NP, SB, RW]), nxt([NP, SB], u32)
        assert o[0] <= 12000
        b_skip_b = at(12000, [NP, D])
        xT = at(13000, [128, KT, N])
        w_gat, w_skip = at(18000, [128, KT, D]), at(20048, [128, KT, D])
        att_b = at(22096, [128, 2, D])
        h_sb = at(23120, [NP, NB, D])
        wa = sb("wa", [128, KT, 2 * H])
        sc = sb("sc", [NP, NB, 2 * H])
        rows16 = cnt_s[0:2 * H, 0:2, :].rearrange("p a n -> p (a n)").bitcast(f32)
        mx1 = sb("mx1", [NP, NB])
        mxh = sb("mxh", [NP, H, NB])
        uv = sb("uv", [NP, NB, 2 * H])
        c8 = sb("c8", [NP, 2, NB])
        c2 = sb("c2", [NP, 2, NB])
        sc8 = sb("sc8", [NP, H, NB])
        sc2 = sb("sc2", [NP, H, NB])
        rden = sb("rden", [NP, NB])
        oh_src = at(0, [128, 2 * GT, N], bf16)
        oh_dst = at(5000, [128, 2 * GT, NP + 1], bf16)
        cnt_f = at(5600, [NP, 2, N])
        rslot = sb("rslot", [128, 2, GT * RW])
        pslot = sb("pslot", [128, 2, GT * RW])
        nslot = sb("nslot", [128, 2])
        ohtmp = at(8100, [128, N], bf16)
        nomask = at(13000, [NP, NB, N], bf16)
        as_b = at(2000, [NP, 2, N])
        junk = at(4600, [NP, N])
        uvrow_sb = at(8000, [2 * H, N])
        UV = at(0, [NP, 2, 2, N])
        wt = at(5000, [NP, WR, N])
        cnt_pool = (at(11400, [NP, N]), at(18020, [NP, N]))
        OT = at(13000, [128, KT, N])
        hs = at(19300, [NP, NB, 3 * C])
        rrow = at(21400, [128, N])
        fT = at(9300, [2 * 8, 2, GS])
        hid = at(19300, [128, 2, 3, GS])
        w_m1, w_m2, w_m3 = sb("w_m1", [2 * 8, 128]), sb("w_m2", [128, 128]), sb("w_m3", [128, 128])
        fsl = sb("fsl", [128, 2, GT, 2 * 8])
        bnp = sb("bnp", [128, 3, KT])
        bst1 = sb("bst1", [128, KT, 5, 6])
        mv1 = sb("mv1", [128, KT, 2])
        scl1 = sb("scl1", [128, KT])
        shf1 = sb("shf1", [128, KT])
        acc = at(0, [NP, NB * 1024])
        ring = at(10240, [128, 2 * GT, D])
        xT1 = at(14336, [128, KT, N])
        xup_st = at(19500, [NP, 2, D])
        prod = at(14336, [128, GT, 8 * MUL])
        sel = at(18432, [128, 2 * GT, NP])
        ws = at(19500, [128, GT, 5 * MUL])
        q4 = at(22100, [128, 3, MUL])
        h3 = at(23456, [128, GS])
        w_up0, w_up1 = at(25504, [128, MUL]), at(25632, [128, MUL])
        w_m4 = at(25952, [128, 4 * MUL])
        w_o0, w_o1 = at(26464, [128, 2, MUL]), at(26720, [128, 2, MUL])
        msgT = at(18432, [128, 2, 8 * NP])
        gidx = sb("gidx", [128, 2, GT], u32)
        gslot = sb("gslot", [128, 2, GT * RW])
        P50 = at(0, [NP, NB, N])
        UV2 = at(12500, [NP, 2, N])
        t2, e2 = at(15000, [NP, 2, N]), at(17500, [NP, 2, N])
        agg = at(20000, [NP, NB, D])
        w_l2 = at(0, [128, KT, D])
        a_b = at(2048, [128, 2, D])
        xT2 = at(3100, [128, KT, N])
        tmp2 = at(25200, [128, D])
        rows2 = at(8200, [2, N])
        uvrow2 = at(9500, [2, N])
        st_b = at(10800, [NP, N])
        nomask2 = at(13000, [NP, NB, N], bf16)
        junk2 = at(19300, [NP, N], bf16)
        aggT = at(0, [128, KT, N])
        basis = at(5000, [128, 2, KT * HB * NP])
        sv, sa, sbb, sa2, sb2 = (at(10000 + 2500 * k, [128, KT * HB * NP]) for k in range(5))
        w_sp = at(22500, [128, 2, KT * D])
        cen = sb("cen", [128, NSPL])
        cslot = sb("cslot", [128, 2])
        w_l3 = at(0, [128, 2 * KT, D])
        nm = at(12500, [NP, NB, D])
        nmT, xT3 = at(17620, [128, KT, N]), at(22620, [128, KT, N])
        fin = at(5000, [NP, 2, D])

        s_acc_done = sem("s_acc_done")
        s_acc_free = sem("s_acc_free")
        s_acc_zero = sem("s_acc_zero")
        s_aggT_ok = sem("s_aggT_ok")
        s_asb_free = sem("s_asb_free")
        s_asb_in0 = sem("s_asb_in0")
        s_asb_in1 = sem("s_asb_in1")
        s_at_cp = sem("s_at_cp")
        s_at_ps = sem("s_at_ps")
        s_basis_ok = sem("s_basis_ok")
        s_bn_in = sem("s_bn_in")
        s_bn_ok = sem("s_bn_ok")
        s_bnsd_ok = sem("s_bnsd_ok")
        s_cnt_flushed = sem("s_cnt_flushed")
        s_cnt_ps = sem("s_cnt_ps")
        s_cntf_ok = sem("s_cntf_ok")
        s_cnts_cp = sem("s_cnts_cp")
        s_cntt_ps = sem("s_cntt_ps")
        s_cols2_cp = sem("s_cols2_cp")
        s_cols2_ps = sem("s_cols2_ps")
        s_cols_cp = sem("s_cols_cp")
        s_cols_ps = sem("s_cols_ps")
        s_const0 = sem("s_const0")
        s_consts = sem("s_consts")
        s_cslot_ok = sem("s_cslot_ok")
        s_dst_in = sem("s_dst_in")
        s_dve_chain = sem("s_dve_chain")
        s_e2_ok = sem("s_e2_ok")
        s_e_ok = sem("s_e_ok")
        s_empty_ok = sem("s_empty_ok")
        s_final_ok = sem("s_final_ok")
        s_fs_ok = sem("s_fs_ok")
        s_ft_cp = sem("s_ft_cp")
        s_ft_ps = sem("s_ft_ps")
        s_gelu_ok = sem("s_gelu_ok")
        s_gidx_ok = sem("s_gidx_ok")
        s_h3_in0 = sem("s_h3_in0")
        s_h3_in1 = sem("s_h3_in1")
        s_h3_out0 = sem("s_h3_out0")
        s_h3_out1 = sem("s_h3_out1")
        s_h_cp = sem("s_h_cp")
        s_h_ps = sem("s_h_ps")
        s_head_free = sem("s_head_free")
        s_hid_ok = sem("s_hid_ok")
        s_hs_ok = sem("s_hs_ok")
        s_l2_agg = sem("s_l2_agg")
        s_l2_cp = sem("s_l2_cp")
        s_l3_agg = sem("s_l3_agg")
        s_l3_cp = sem("s_l3_cp")
        s_ln_sd = sem("s_ln_sd")
        s_ln_var = sem("s_ln_var")
        s_mask_ok = sem("s_mask_ok")
        s_max_done = sem("s_max_done")
        s_min_ok = sem("s_min_ok")
        s_mlp_done = sem("s_mlp_done")
        s_mlp_ps = sem("s_mlp_ps")
        s_mt_cp = sem("s_mt_cp")
        s_mt_ps = sem("s_mt_ps")
        s_norm_ok = sem("s_norm_ok")
        s_nslot_ok = sem("s_nslot_ok")
        s_nt_cp = sem("s_nt_cp")
        s_nt_ps = sem("s_nt_ps")
        s_o_cp = sem("s_o_cp")
        s_o_ps = sem("s_o_ps")
        s_oh_ok = sem("s_oh_ok")
        s_oha_ok = sem("s_oha_ok")
        s_ohd_ok = sem("s_ohd_ok")
        s_out_done = sem("s_out_done")
        s_p2_ok = sem("s_p2_ok")
        s_p3_ok = sem("s_p3_ok")
        s_p_ok = sem("s_p_ok")
        s_pp_ok = sem("s_pp_ok")
        s_prefix_cp = sem("s_prefix_cp")
        s_prefix_ps = sem("s_prefix_ps")
        s_prod_ok = sem("s_prod_ok")
        s_pslot_ok = sem("s_pslot_ok")
        s_pv_done = sem("s_pv_done")
        s_q_ok = sem("s_q_ok")
        s_rec_in = sem("s_rec_in")
        s_rec_ok = sem("s_rec_ok")
        s_recs_clear = sem("s_recs_clear")
        s_recs_in = sem("s_recs_in")
        s_rows2_cp = sem("s_rows2_cp")
        s_rows2_out = sem("s_rows2_out")
        s_rows2_ps = sem("s_rows2_ps")
        s_rows_cp = sem("s_rows_cp")
        s_rows_out = sem("s_rows_out")
        s_rows_ps = sem("s_rows_ps")
        s_rrow_ok = sem("s_rrow_ok")
        s_sa_ok = sem("s_sa_ok")
        s_scat_done = sem("s_scat_done")
        s_scattered = sem("s_scattered")
        s_sel_ok = sem("s_sel_ok")
        s_silu_ok = sem("s_silu_ok")
        s_skip_cp = sem("s_skip_cp")
        s_skip_ps = sem("s_skip_ps")
        s_sp_free = sem("s_sp_free")
        s_sq2_ok = sem("s_sq2_ok")
        s_st_in = sem("s_st_in")
        s_staged = sem("s_staged")
        s_sv_ok = sem("s_sv_ok")
        s_t2_ok = sem("s_t2_ok")
        s_t_ok = sem("s_t_ok")
        s_tot_ok = sem("s_tot_ok")
        s_tpw_ps = sem("s_tpw_ps")
        s_uv2_in = sem("s_uv2_in")
        s_uv2_ok = sem("s_uv2_ok")
        s_uv_free = sem("s_uv_free")
        s_uv_in0 = sem("s_uv_in0")
        s_uv_in1 = sem("s_uv_in1")
        s_uv_ok = sem("s_uv_ok")
        s_uvrow2_ok = sem("s_uvrow2_ok")
        s_uvrow_ok = sem("s_uvrow_ok")
        s_uvt2_ps = sem("s_uvt2_ps")
        s_uvt_ps = sem("s_uvt_ps")
        s_var_ok = sem("s_var_ok")
        s_w1_in = sem("s_w1_in")
        s_wa2_ok = sem("s_wa2_ok")
        s_wa_ok = sem("s_wa_ok")
        s_wdiag_zero = sem("s_wdiag_zero")
        s_wg_in = sem("s_wg_in")
        s_wk_in = sem("s_wk_in")
        s_wl2_in = sem("s_wl2_in")
        s_wl3_in = sem("s_wl3_in")
        s_wm_in = sem("s_wm_in")
        s_ws_ok = sem("s_ws_ok")
        s_wsp_in0 = sem("s_wsp_in0")
        s_wsp_in1 = sem("s_wsp_in1")
        s_x_in = sem("s_x_in")
        s_x_ok = sem("s_x_ok")
        s_xt1_cp = sem("s_xt1_cp")
        s_xt1_ps = sem("s_xt1_ps")
        s_xt2_cp = sem("s_xt2_cp")
        s_xt2_ps = sem("s_xt2_ps")
        s_xt3_cp = sem("s_xt3_cp")
        s_xt3_ps = sem("s_xt3_ps")
        s_xt_cp = sem("s_xt_cp")
        s_xt_ps = sem("s_xt_ps")
        s_xup_cp = sem("s_xup_cp")
        s_xup_out0 = sem("s_xup_out0")
        s_xup_out1 = sem("s_xup_out1")
        s_xup_ps = sem("s_xup_ps")
        s_y1_cp = sem("s_y1_cp")
        s_y1_ps = sem("s_y1_ps")
        s_y2_cp = sem("s_y2_cp")
        s_y3_cp = sem("s_y3_cp")
        s_y3_ps = sem("s_y3_ps")
        s_gath = [sem(f"s_gath{k}") for k in range(2 * GT)]
        block = ctx.enter_context(nc.Block())

        def kview(w):
            return w.rearrange("(k p) n -> p k n", p=128)

        def bass_row(v, p):
            return v.rearrange("(a n) -> a n", a=1).to_broadcast([p, v.shape[0]])

        @block.sync
        def _(sp):
            sp.dma_start(dsti, a["dst"].rearrange("(p e) -> p e", p=NP)).then_inc(s_dst_in, 16)
            sp.dma_start(srci, a["src"].rearrange("(p e) -> p e", p=NP)).then_inc(s_rec_in, 16)
            sp.dma_start(a4, a["edge_attr_4"].rearrange("(p e) k -> p e k", p=NP)).then_inc(s_rec_in, 16)
            sp.dma_start(a8, a["edge_attr_8"].rearrange("(p e) k -> p e k", p=NP)).then_inc(s_rec_in, 16)
            sp.dma_start(x_sb[:], a["x"].rearrange("(b p) n -> p b n", p=NP)).then_inc(s_x_in, 16)
            sp.dma_start(w_gat, kview(a["L0_gnn_W_gat"])).then_inc(s_wg_in, 16)
            sp.dma_start(att_b[:, 0, :], bass_row(a["L0_gnn_att_src"].rearrange("h c -> (h c)"), 128)).then_inc(s_wg_in, 16)
            sp.dma_start(att_b[:, 1, :], bass_row(a["L0_gnn_att_dst"].rearrange("h c -> (h c)"), 128)).then_inc(s_wg_in, 16)
            sp.dma_start(w_skip, kview(a["L0_gnn_W_skip"])).then_inc(s_wk_in, 16)
            sp.dma_start(b_skip_b, bass_row(a["L0_gnn_b_skip"], NP)).then_inc(s_wk_in, 16)
            sp.wait_ge(s_wdiag_zero, 1)
            for q in range(2):
                sp.dma_start(w_m1[q * 8:q * 8 + 8, q * HID:(q + 1) * HID], a["L1_gnn_W_mlp1"]).then_inc(s_wm_in, 16)
                sp.dma_start(w_m2[q * HID:(q + 1) * HID, q * HID:(q + 1) * HID], a["L1_gnn_W_mlp2"]).then_inc(s_wm_in, 16)
                sp.dma_start(w_m3[q * HID:(q + 1) * HID, q * HID:(q + 1) * HID], a["L1_gnn_W_mlp3"]).then_inc(s_wm_in, 16)
            for q, name in enumerate(("L0_gnn_gat_bias", "L0_gnn_bn_gamma", "L0_gnn_bn_beta")):
                sp.dma_start(bnp[:, q, :], a[name]).then_inc(s_bn_in, 16)
            sp.wait_ge(s_empty_ok, 2)
            flat = recs.rearrange("(q p e) k -> q p (e k)", p=128, e=EMP)
            nq = (G + 2) * GS // (128 * EMP)
            for q in range(nq):
                sp.dma_start(flat[q], empty.rearrange("p e k -> p (e k)")).then_inc(s_recs_clear, 16)
            sp.wait_ge(s_scattered, 16 * EC)
            sp.dma_start(rec_sb[:], recs.rearrange("(g p t) k -> p g (t k)", p=128, t=GT)).then_inc(s_recs_in, 16)

            sp.wait_ge(s_rows_cp, 3)
            sp.dma_start(as_rows, rows16).then_inc(s_rows_out, 16)
            sp.wait_ge(s_rows_out, 16)
            sp.wait_ge(s_mask_ok, 1)
            with sp.Fori(0, H // 2) as i:
                for par in range(2):
                    sp.wait_ge(s_asb_free, i * 2 + (par + 1))
                    sp.dma_start(as_b[:, par, :], as_rows[bass.ds(i * 2 + par, 1), :].to_broadcast([NP, N]))\
                      .then_inc(s_asb_in0 if par == 0 else s_asb_in1, 16)
            sp.wait_ge(s_uvrow_ok, 1)
            sp.dma_start(uv_rows, uvrow_sb).then_inc(s_rows_out, 16)
            sp.wait_ge(s_rows_out, 32)
            sp.wait_ge(s_max_done, 1)
            with sp.Fori(0, H // 2) as i:
                for par in range(2):
                    sp.wait_ge(s_uv_free, i * 2 + (par + 1))
                    for q in range(2):
                        sp.dma_start(UV[:, par, q, :], uv_rows[bass.ds(i * 2 + (par + q * H), 1), :].to_broadcast([NP, N]))\
                          .then_inc(s_uv_in0 if par == 0 else s_uv_in1, 16)

            sp.wait_ge(s_x_ok, 1)
            sp.dma_start(w_up0, a["L1_gnn_W_up0"]).then_inc(s_w1_in, 16)
            sp.dma_start(w_up1, a["L1_gnn_W_up1"]).then_inc(s_w1_in, 16)
            sp.dma_start(w_m4[0:HID, :], a["L1_gnn_W_mlp4"]).then_inc(s_w1_in, 16)
            sp.dma_start(w_m4[HID:128, :], a["L1_gnn_W_mlp4"]).then_inc(s_w1_in, 16)
            sp.dma_start(w_o0, kview(a["L1_gnn_W_out0"])).then_inc(s_w1_in, 16)
            sp.dma_start(w_o1, kview(a["L1_gnn_W_out1"])).then_inc(s_w1_in, 16)
            for b in range(NB):
                sp.wait_ge(s_xup_cp, b + 1)
                sp.dma_start(xup[b * NP:(b + 1) * NP, :], xup_st[:, b % 2, :]).then_inc(s_xup_out0 if b % 2 == 0 else s_xup_out1, 16)
            for par in range(2):
                sp.dma_start(h3[par * HID:(par + 1) * HID, :], h3_rows[0, par * HID:(par + 1) * HID, :])\
                  .then_inc(s_h3_in0 if par == 0 else s_h3_in1, 16)
            with sp.Fori(0, G // 2 - 1) as i:
                for par in range(2):
                    sp.wait_ge(s_tpw_ps, i * 8 + 4 * (par + 1))
                    sp.dma_start(h3[par * HID:(par + 1) * HID, :],
                                 h3_rows[bass.ds(i + 1, 1), par * HID:(par + 1) * HID, :].rearrange("q p n -> (q p) n"))\
                      .then_inc(s_h3_in0 if par == 0 else s_h3_in1, 16)
            sp.wait_ge(s_tpw_ps, (G - 1) * GT)
            sp.dma_start(h3[0:HID, :], h3_rows[G // 2 - 1, 0:HID, :]).then_inc(s_h3_in0, 16)

            sp.wait_ge(s_x_ok, 2)
            sp.dma_start(w_l2, kview(a["L2_gnn_W"])).then_inc(s_wl2_in, 16)
            av = a["L2_gnn_a"].rearrange("(q n) k -> q (n k)", q=2)
            sp.dma_start(a_b[:, 0, :], av[0:1, :].to_broadcast([128, D])).then_inc(s_wl2_in, 16)
            sp.dma_start(a_b[:, 1, :], av[1:2, :].to_broadcast([128, D])).then_inc(s_wl2_in, 16)
            sp.wait_ge(s_rows2_cp, 3)
            sp.dma_start(st_rows, rows2).then_inc(s_rows2_out, 16)
            sp.wait_ge(s_rows2_out, 16)
            sp.dma_start(st_b, st_rows[1:2, :].to_broadcast([NP, N])).then_inc(s_st_in, 16)
            sp.wait_ge(s_uvrow2_ok, 1)
            sp.dma_start(uv2_rows, uvrow2).then_inc(s_rows2_out, 16)
            sp.wait_ge(s_rows2_out, 32)
            for q in range(2):
                sp.dma_start(UV2[:, q, :], uv2_rows[q:q + 1, :].to_broadcast([NP, N])).then_inc(s_uv2_in, 16)
            sp.wait_ge(s_aggT_ok, 1)
            spl = a["spline_wT"].rearrange("q (k p) n -> q p k n", p=128)
            for half in range(2):
                sp.wait_ge(s_sp_free, 10 * half + 1)
                sp.dma_start(w_sp[:, 0, :].rearrange("p (k n) -> p k n", k=KT), kview(a["base_wT"])).then_inc(s_wsp_in0, 16)
                with sp.Fori(0, NSPL // 2) as i:
                    for par in range(2):
                        slot = 1 - par
                        sp.wait_ge(s_sp_free, i * 2 + (9 * half + par + 2))
                        sp.dma_start(w_sp[:, slot, :].rearrange("p (k n) -> p k n", k=KT),
                                     spl[bass.ds(i * 2 + par, 1), :, :, :].rearrange("q p k n -> (q p) k n"))\
                          .then_inc(s_wsp_in0 if slot == 0 else s_wsp_in1, 16)
            sp.wait_ge(s_l3_agg, NB)
            sp.dma_start(w_l3, kview(a["w_l3T"])).then_inc(s_wl3_in, 16)

            sp.wait_ge(s_final_ok, 1)
            sp.dma_start(out.rearrange("(b p) n -> p b n", p=NP), x_sb[:]).then_inc(s_out_done, 16)
            sp.wait_ge(s_out_done, 16)

        @block.gpsimd
        def _(pool):
            pool.memset(upper[:], 1.0)
            pool.memset(ident[:], 0.0)
            pool.memset(ones[:], 1.0)
            pool.memset(epsc[:], EPS)
            pool.memset(w_m1[:], 0.0)
            pool.memset(w_m2[:], 0.0)
            pool.memset(w_m3[:], 0.0).then_inc(s_wdiag_zero, 1)
            pool.memset(gidx[:], 0).then_inc(s_const0, 1)
            pool.iota(gi, pattern=[[1, G + 2]], base=0, channel_multiplier=0)
            pool.iota(iota_src[:], pattern=[[1, N]], base=0, channel_multiplier=0, allow_small_or_imprecise_dtypes=True)
            pool.iota(iota_dst[:], pattern=[[1, NP]], base=0, channel_multiplier=0, allow_small_or_imprecise_dtypes=True)
            pool.iota(cen[:], pattern=[[1, NSPL]], base=0, channel_multiplier=0, allow_small_or_imprecise_dtypes=True)
            pool.wait_ge(s_const0, 1)
            pool.affine_select(out=upper[:], in_=upper[:], compare_op=ALU.is_gt, fill=0.0, base=0,
                               pattern=[[1, 128]], channel_multiplier=-1)
            pool.affine_select(out=ident[:], in_=ident[:], compare_op=ALU.not_equal, fill=1.0, base=0,
                               pattern=[[-1, 128]], channel_multiplier=1).then_inc(s_consts, 1)
            nq = (G + 2) * GS // (128 * EMP)
            pool.wait_ge(s_recs_clear, 16 * nq)
            pool.wait_ge(s_rec_ok, 1)

            def scatter_round(j, n_staged):
                pool.tensor_copy(stage_pos, pos[:, bass.ds(j * SB, SB)])
                pool.tensor_copy(stage_rec, rec[:, bass.ds(j * SB, SB), :]).then_inc(s_staged, 1)
                pool.wait_ge(s_staged, n_staged)
                pool.nop(nofuse=True)
                for k in range(SB):
                    pool.indirect_dma_start(out=recs, out_offset=bass.IndirectOffsetOnAxis(stage_pos[:, k:k + 1], 0),
                                            in_=stage_rec[:, k, :], in_offset=None).then_inc(s_scattered, 16)
            scatter_round(0, 1)
            with pool.Fori(1, EC // SB) as j:
                pool.wait_ge(s_scattered, j * (16 * SB))
                scatter_round(j, j + 1)

            pool.wait_ge(s_recs_in, 16)
            with pool.Fori(0, G // 2) as i:
                for par in range(2):
                    pool.wait_ge(s_cnt_ps, i * 2 + (par + 1))
                    pool.tensor_copy(pslot[:, par, :], rec_sb[:, bass.ds(i * 2 + par, 1), :].rearrange("p a k -> p (a k)"))\
                        .then_inc(s_pslot_ok, 1)
                    pool.wait_ge(s_pslot_ok, i * 2 + (par + 1))
                    pool.nop(nofuse=True)
                    for k in range(GT):
                        ins = pool.tensor_scalar(oh_dst[:, par * GT + k, 0:NP], iota_dst[:],
                                                 pslot[:, par, k * RW + R_DL:k * RW + R_DL + 1], None, ALU.is_equal)
                    ins.then_inc(s_ohd_ok, 1)
            with pool.Fori(0, G // 4) as i:
                for q in range(2):
                    pool.wait_ge(s_ft_ps, i * 2 + (q + 1))
                    for hf in range(2):
                        ins = pool.tensor_copy(fsl[:, q, :, hf * 8:hf * 8 + 8],
                                               rec_sb[:, bass.ds(i * 4 + (2 * q + hf), 1), :]
                                               .rearrange("p a (t k) -> p (a t) k", k=RW)[:, :, R_F:R_F + 8])
                    ins.then_inc(s_fs_ok, 1)
            pool.wait_ge(s_mlp_done, 1)
            pool.memset(hs[:, :, C:2 * C], 1.0)
            h5 = h_sb.rearrange("p b (h c) -> p b h c", h=H)
            for par in range(2):
                pool.tensor_copy(hs[:, :, par * 2 * C:par * 2 * C + C], h5[:, :, par, :]).then_inc(s_hs_ok, 1)

            def pool_head(h, par, fill, norm):
                for n, sblk in enumerate(POOL_P):
                    pool.wait_ge(s_e_ok, h * NB + (sblk + 1))
                    pool.nop(nofuse=True)
                    w = wt[:, sblk % WR, :]
                    pool.tensor_scalar(w, w, 1.0, None, ALU.min).then_inc(s_min_ok, 1)
                    pool.wait_ge(s_min_ok, h * len(POOL_P) + (n + 1))
                    pool.tensor_tensor(w, w, cnt_pool[n], ALU.mult).then_inc(s_pp_ok, 1)
                    if fill and n == 0:
                        pool.wait_ge(s_pv_done, h * NB + WR)
                        c0 = (1 - par) * 2 * C
                        pool.tensor_copy(hs[:, :, c0:c0 + C],
                                         h5[:, :, bass.ds(h + 1, 1), :].rearrange("p b h c -> p b (h c)")).then_inc(s_hs_ok, 1)
                if norm is not None:
                    normalise(norm)

            def normalise(i):
                pool.wait_ge(s_rrow_ok, i + 1)
                pool.nop(nofuse=True)
                o_i = OT[:, bass.ds(i, 1), :].rearrange("p a n -> p (a n)")
                nc.gpsimd.tensor_tensor(o_i, o_i, rrow, ALU.mult).then_inc(s_norm_ok, 1)
            pool_head(0, 0, False, None)
            with pool.Fori(0, H // 2 - 1) as i:
                pool_head(i * 2 + 1, 1, True, None)
                pool_head(i * 2 + 2, 0, True, i)
            pool_head(H - 1, 1, False, None)
            normalise(H // 2 - 1)

            pool.wait_ge(s_recs_in, 16)
            for sl in range(2):
                pool.wait_ge(s_xup_out0 if sl == 0 else s_xup_out1, 16 * NB // 2)

            pool.wait_ge(s_acc_zero, 1)

            def gathers(g, par, n):
                pool.tensor_copy(gidx[:, par, :], rec_sb[:, bass.ds(g, 1), :].bitcast(u32)
                                 .rearrange("p a (t k) -> p (a t) k", k=RW)[:, :, R_SRCI])
                pool.tensor_copy(gslot[:, par, :], rec_sb[:, bass.ds(g, 1), :].rearrange("p a k -> p (a k)"))\
                    .then_inc(s_gidx_ok, 1)
                pool.wait_ge(s_gidx_ok, n)
                pool.nop(nofuse=True)
                for k in range(GT):
                    pool.indirect_dma_start(out=ring[:, par * GT + k, :], out_offset=None, in_=xup,
                                            in_offset=bass.IndirectOffsetOnAxis(gidx[:, par, k:k + 1], 0))\
                        .then_inc(s_gath[par * GT + k], 16)

            def selectors(par):
                for k in range(GT):
                    ins = pool.tensor_scalar(sel[:, par * GT + k, :], iota_dst[:],
                                             gslot[:, par, k * RW + R_DL:k * RW + R_DL + 1], None, ALU.is_equal)
                    ins.then_inc(s_sel_ok, 1)
            for g in range(2):
                gathers(g, g, g + 1)
                selectors(g)
            with pool.Fori(0, G // 2 - 1) as i:
                for par in range(2):
                    pool.wait_ge(s_prod_ok, i * 8 + (4 * par + 4 + GT))
                    pool.wait_ge(s_scat_done, i * 8 + (4 * par + 4 + GT))
                    gathers(i * 2 + (2 + par), par, i * 2 + (3 + par))
                    selectors(par)

        @block.tensor
        def _(pe):
            t = nc.tensor

            def transposes(src, ready, done, copied, banks, copied0=0):
                for b in range(NB):
                    if ready is not None:
                        pe.wait_ge(*ready(b))
                    if b >= 2:
                        pe.wait_ge(copied, copied0 + b - 1)
                    for k in range(KT):
                        ins = t.transpose(PS[:, banks[b % 2], k * 128:k * 128 + NP], src(b, k), ident[:NP, :NP])
                    ins.then_inc(done, 1)

            def node_product(lhs, rhs, nk, done, copied, banks, cols=D):
                for b in range(NB):
                    if b >= 2:
                        pe.wait_ge(copied, b - 1)
                    for k in range(nk):
                        ins = t.matmul(PS[:NP, banks[b % 2], 0:cols], lhs(b, k), rhs(k), start=(k == 0), stop=(k == nk - 1))
                    ins.then_inc(done, 1)

            def blk_of(v):
                return lambda b, k: v[:, k, b * NP:(b + 1) * NP]

            def rows_product(w, nr, xt, done, b0):
                for q in range(3):
                    n0, n1 = q * 512, min(N, (q + 1) * 512)
                    for k in range(KT):
                        ins = t.matmul(PS[:nr, b0 + q, 0:n1 - n0], w[:, k, 0:nr], xt[:, k, n0:n1], start=(k == 0), stop=(k == KT - 1))
                    ins.then_inc(done, 1)

            def cols_product(w, nr, xt, done, bank):
                for b in range(NB):
                    for k in range(KT):
                        ins = t.matmul(PS[:NP, bank, b * nr:(b + 1) * nr], xt[:, k, b * NP:(b + 1) * NP], w[:, k, 0:nr],
                                       start=(k == 0), stop=(k == KT - 1))
                ins.then_inc(done, 1)

            def uv_transposes(src, nr, done, b0):
                for b in range(NB):
                    ins = t.transpose(PS[:nr, b0 + b // 4, (b % 4) * NP:(b % 4 + 1) * NP], src[:, b, 0:nr], ident[:NP, :NP])
                ins.then_inc(done, 1)

            pe.wait_ge(s_consts, 1)
            pe.wait_ge(s_x_in, 16)
            transposes(lambda b, k: x_sb[:, b, k * 128:(k + 1) * 128], None, s_xt_ps, s_xt_cp, (6, 7))
            pe.wait_ge(s_tot_ok, 1)
            t.matmul(PS[:NP, 5, 0:NB], upper[:NP, :NP], tot, start=True, stop=True)
            t.matmul(PS[:, 5, 16:16 + NB], ones[:NP, 0:128], tot, start=True, stop=True).then_inc(s_prefix_ps, 1)
            pe.wait_ge(s_wg_in, 48)
            pe.wait_ge(s_xt_cp, NB)
            node_product(blk_of(xT), lambda k: w_gat[:, k, :], KT, s_h_ps, s_h_cp, (6, 7))
            pe.wait_ge(s_wa_ok, 1)
            rows_product(wa, 2 * H, xT, s_rows_ps, 0)
            cols_product(wa, 2 * H, xT, s_cols_ps, 3)
            pe.wait_ge(s_wk_in, 32)
            pe.wait_ge(s_h_cp, NB)
            node_product(blk_of(xT), lambda k: w_skip[:, k, :], KT, s_skip_ps, s_skip_cp, (6, 7))
            pe.wait_ge(s_rows_cp, 3)
            pe.wait_ge(s_cols_cp, 1)
            pe.wait_ge(s_prefix_cp, 1)

            with pe.Fori(0, G // 2) as i:
                for par in range(2):
                    pe.wait_ge(s_oh_ok, i * 2 + (par + 1))
                    pe.wait_ge(s_ohd_ok, i * 2 + (par + 1))
                    pe.wait_ge(s_oha_ok, i * 2 + (par + 1))
                    pe.wait_ge(s_cnt_flushed, i * 2 + (par + 1))
                    for k in range(GT):
                        for q in range(3):
                            n0, n1 = q * 512, min(N, (q + 1) * 512)
                            ins = t.matmul(PS[:NP, 3 * par + q, 0:n1 - n0], oh_dst[:, par * GT + k, 0:NP],
                                           oh_src[:, par * GT + k, n0:n1], start=(k == 0), stop=(k == GT - 1))
                    ins.then_inc(s_cnt_ps, 1)
            pe.wait_ge(s_cnt_flushed, G + 2)
            for b in range(NB):
                pe.wait_ge(s_cntf_ok, b + 1)
                if b >= 2:
                    pe.wait_ge(s_cnts_cp, b - 1)
                for j in range(NB):
                    ins = t.transpose(PS[:NP, 3 * (b % 2) + j // 4, (j % 4) * NP:(j % 4 + 1) * NP],
                                      cnt_f[:, b % 2, j * NP:(j + 1) * NP], ident[:NP, :NP])
                ins.then_inc(s_cntt_ps, 1)
            pe.wait_ge(s_cnts_cp, NB)
            pe.wait_ge(s_wm_in, 16 * 6)
            with pe.Fori(0, G // 4) as i:
                for q in range(2):
                    pe.wait_ge(s_fs_ok, i * 2 + (q + 1))
                    for k in range(GT):
                        ins = t.transpose(PS[:16, 6 + q, k * 128:(k + 1) * 128],
                                          fsl[:, q, k, :], ident[:])
                    ins.then_inc(s_ft_ps, 1)
                for l, w in enumerate((w_m1, w_m2, w_m3)):
                    for q in range(2):
                        if l == 0:
                            pe.wait_ge(s_ft_cp, i * 2 + (q + 1))
                        else:
                            pe.wait_ge(s_hid_ok, i * 6 + (2 * (l - 1) + q + 1))
                        t.matmul(PS[:, 4 + q, :], w[:], fT[:, q, :] if l == 0 else hid[:, q, l - 1, :], start=True, stop=True)\
                            .then_inc(s_mlp_ps, 1)
                for q in range(2):
                    pe.wait_ge(s_hid_ok, i * 6 + (4 + q + 1))
            pe.wait_ge(s_uv_ok, 1)
            uv_transposes(uv, 2 * H, s_uvt_ps, 0)
            pe.wait_ge(s_uvrow_ok, 1)
            with pe.Fori(0, H // 2) as i:
                for par in range(2):
                    pe.wait_ge(s_hs_ok, i * 2 + (par + 1))
                    pe.wait_ge(s_head_free, i * 2 + (par + 1))
                    for sblk in range(NB):
                        if sblk in POOL_P:
                            n_p = len(POOL_P)
                            pe.wait_ge(s_pp_ok, i * (2 * n_p) + (par * n_p + POOL_P.index(sblk) + 1))
                        else:
                            n_p = NB - len(POOL_P)
                            pe.wait_ge(s_p_ok, i * (2 * n_p) + (par * n_p + len([b for b in range(sblk) if b not in POOL_P]) + 1))
                        for q in range(3):
                            n0, n1 = q * 512, min(N, (q + 1) * 512)
                            ins = t.matmul(PS[:, 3 * par + q, 0:n1 - n0], hs[:, sblk, par * C:par * C + 2 * C],
                                           wt[:, sblk % WR, n0:n1], start=(sblk == 0), stop=(sblk == NB - 1))
                        ins.then_inc(s_pv_done, 1)
            for b in range(NB):
                if b == 0:
                    pe.wait_ge(s_gelu_ok, 1)
                if b >= 2:
                    pe.wait_ge(s_o_cp, b - 1)
                for k in range(KT):
                    ins = t.transpose(PS[:NP, 6 + b % 2, k * 128:(k + 1) * 128], OT[:, k, b * NP:(b + 1) * NP], ident[:])
                ins.then_inc(s_o_ps, 1)

            pe.wait_ge(s_x_ok, 1)
            pe.wait_ge(s_w1_in, 16 * 6)

            def src1(b, k):
                return x_sb[:, b, 0:MUL] if k == 0 else x_sb[:, b, MUL + k - 1:D:3]
            transposes(src1, None, s_xt1_ps, s_xt1_cp, (6, 7))
            pe.wait_ge(s_xt1_cp, NB)
            for b in range(NB):
                if b >= 2:
                    pe.wait_ge(s_xup_cp, b - 1)
                for k in range(4):
                    ins = t.matmul(PS[:NP, 6 + b % 2, k * MUL:(k + 1) * MUL], xT1[:, k, b * NP:(b + 1) * NP],
                                   w_up0 if k == 0 else w_up1, start=True, stop=True)
                ins.then_inc(s_xup_ps, 1)
            pe.wait_ge(s_xup_cp, NB)

            tpw_bank = (0, 1, 6, 7)

            def tpw(k, par):
                t.matmul(PS[:, tpw_bank[k], :], h3[par * HID:(par + 1) * HID, k * 128:(k + 1) * 128],
                         w_m4[par * HID:(par + 1) * HID, :], start=True, stop=True).then_inc(s_tpw_ps, 1)

            def scat(par, k):
                for q in range(2):
                    ins = t.matmul(PS[:NP, 2 + 2 * par + q, :], sel[:, par * GT + k, :], prod[:, k, q * 512:(q + 1) * 512],
                                   start=(k == 0), stop=(k == GT - 1))
                ins.then_inc(s_scat_done, 1)
            pe.wait_ge(s_h3_in0, 16)
            for k in range(GT - 1):
                tpw(k, 0)
            with pe.Fori(0, G // 2) as i:
                for par in range(2):
                    pe.wait_ge(s_acc_free, i * 2 + (par + 1))
                    for k in range(GT):
                        if k == 1:
                            pe.wait_ge(s_h3_in1 if par == 0 else s_h3_in0, i * 16 + 16 * (par + 1))
                        tpw((k + GT - 1) % GT, par if k == 0 else 1 - par)
                        pe.wait_ge(s_sel_ok, i * 8 + (4 * par + k + 1))
                        pe.wait_ge(s_prod_ok, i * 8 + (4 * par + k + 1 + GT))
                        scat(par, k)
            pe.wait_ge(s_acc_done, 1)
            for b in range(NB):
                if b >= 2:
                    pe.wait_ge(s_mt_cp, 2 * (b - 1))
                for c in range(8):
                    ins = t.transpose(PS[:, 2 * (b % 2) + c // 4, (c % 4) * 128:(c % 4) * 128 + NP],
                                      acc[:, b * 1024 + c * 128:b * 1024 + (c + 1) * 128], ident[:NP, :NP])
                    if c % 4 == 3:
                        ins.then_inc(s_mt_ps, 1)
                pe.wait_ge(s_mt_cp, 2 * (b + 1))
                if b >= 2:
                    pe.wait_ge(s_y1_cp, b - 1)
                for q in range(4):
                    pair = ((0, w_o0[:, 0, :]), (7, w_o0[:, 1, :])) if q == 0 else \
                           ((q, w_o1[:, 0, :]), (3 + q, w_o1[:, 1, :]))
                    for n, (c, w) in enumerate(pair):
                        ins = t.matmul(PS[:NP, 4 + b % 2, q * MUL:(q + 1) * MUL], msgT[:, b % 2, c * NP:(c + 1) * NP], w,
                                       start=(n == 0), stop=(n == 1))
                ins.then_inc(s_y1_ps, 1)

            def aggregate(done, copied, den, banks, ready):
                for b in range(NB):
                    if ready is not None and b == 0:
                        pe.wait_ge(*ready)
                    if b >= 2:
                        pe.wait_ge(copied, b - 1)
                    for k in range(NB):
                        ins = t.matmul(PS[:NP, banks[b % 2], :], P50[:, k, b * NP:(b + 1) * NP], x_sb[:, k, :],
                                       start=(k == 0), stop=(k == NB - 1))
                    if den:
                        for k in range(NB):
                            ins = t.matmul(PS[:NP, banks[b % 2] + 2, 0:2], P50[:, k, b * NP:(b + 1) * NP], ones[:NP, 0:2],
                                           start=(k == 0), stop=(k == NB - 1))
                    ins.then_inc(done, 1)

            pe.wait_ge(s_x_ok, 2)
            transposes(lambda b, k: x_sb[:, b, k * 128:(k + 1) * 128], None, s_xt2_ps, s_xt2_cp, (6, 7))
            pe.wait_ge(s_wa2_ok, 1)
            pe.wait_ge(s_xt2_cp, NB)
            rows_product(wa, 2, xT2, s_rows2_ps, 0)
            cols_product(wa, 2, xT2, s_cols2_ps, 3)
            pe.wait_ge(s_uv2_ok, 1)
            pe.wait_ge(s_rows2_cp, 3)
            uv_transposes(uv, 2, s_uvt2_ps, 0)
            pe.wait_ge(s_uvrow2_ok, 1)
            aggregate(s_l2_agg, s_l2_cp, True, (4, 5), (s_p2_ok, NB))
            pe.wait_ge(s_l2_cp, NB)
            transposes(lambda b, k: agg[:, b, k * 128:(k + 1) * 128], None, s_at_ps, s_at_cp, (6, 7))
            pe.wait_ge(s_at_cp, NB)

            def spline_step(slot, first, last):
                for b in range(HB):
                    for k in range(KT):
                        ins = t.matmul(PS[:NP, b, :], basis[:, slot, (k * HB + b) * NP:(k * HB + b + 1) * NP],
                                       w_sp[:, slot, k * D:(k + 1) * D], start=(first and k == 0), stop=(last and k == KT - 1),
                                       skip_group_check=True)
                ins.then_inc(s_sp_free, 1)
            for half in range(2):
                if half:
                    pe.wait_ge(s_y2_cp, HB)
                pe.wait_ge(s_wsp_in0, 16 * (5 * half + 1))
                pe.wait_ge(s_silu_ok, half + 1)
                spline_step(0, True, False)
                with pe.Fori(0, NSPL // 2) as i:
                    for par in range(2):
                        slot = 1 - par
                        if slot == 0:
                            pe.wait_ge(s_wsp_in0, i * 16 + 16 * (5 * half + 2))
                        else:
                            pe.wait_ge(s_wsp_in1, i * 16 + 16 * (4 * half + 1))
                        pe.wait_ge(s_basis_ok, i * 2 + (8 * half + par + 1))
                        spline_step(slot, False, False)
            pe.wait_ge(s_x_ok, 3)
            aggregate(s_l3_agg, s_l3_cp, False, (0, 1), (s_p3_ok, NB))
            transposes(lambda b, k: x_sb[:, b, k * 128:(k + 1) * 128], None, s_xt3_ps, s_xt3_cp, (6, 7))
            pe.wait_ge(s_xt3_cp, NB)
            transposes(lambda b, k: nm[:, b, k * 128:(k + 1) * 128], lambda b: (s_l3_cp, b + 1), s_nt_ps, s_nt_cp, (6, 7))
            pe.wait_ge(s_nt_cp, NB)
            pe.wait_ge(s_wl3_in, 16)
            node_product(lambda b, k: (xT3 if k < KT else nmT)[:, k % KT, b * NP:(b + 1) * NP],
                         lambda k: w_l3[:, k, :], 2 * KT, s_y3_ps, s_y3_cp, (4, 5))

        @block.scalar
        def _(act):
            A = nc.scalar.activation

            def evac_T(dst, done, copied, banks):
                for b in range(NB):
                    act.wait_ge(done, b + 1)
                    A(dst[:, :, b * NP:(b + 1) * NP],
                      PS[:, banks[b % 2], :].rearrange("p (k n) -> p k n", k=KT)[:, :, 0:NP], ACT.Copy).then_inc(copied, 1)

            def evac_rows(dst, nr, done, copied, b0):
                for q in range(3):
                    n0, n1 = q * 512, min(N, (q + 1) * 512)
                    act.wait_ge(done, q + 1)
                    A(dst[:, n0:n1], PS[:nr, b0 + q, 0:n1 - n0], ACT.Copy).then_inc(copied, 1)

            def evac_uv(dst, nr, b0, ok, done):
                act.wait_ge(done, 1)
                for q in range(3):
                    n0, n1 = q * 4 * NP, min(N, (q + 1) * 4 * NP)
                    ins = A(dst[:, n0:n1], PS[:nr, b0 + q, 0:n1 - n0], ACT.Copy)
                ins.then_inc(ok, 1)

            evac_T(xT, s_xt_ps, s_xt_cp, (6, 7))
            for b in range(NB):
                act.wait_ge(s_h_ps, b + 1)
                A(h_sb[:, b, :], PS[:NP, 6 + b % 2, :], ACT.Copy).then_inc(s_h_cp, 1)
            evac_rows(rows16, 2 * H, s_rows_ps, s_rows_cp, 0)
            act.wait_ge(s_cols_ps, 1)
            A(sc[:].rearrange("p b n -> p (b n)"), PS[:NP, 3, 0:NB * 2 * H], ACT.Copy).then_inc(s_cols_cp, 1)
            act.wait_ge(s_recs_in, 16)
            with act.Fori(0, G // 2) as i:
                for par in range(2):
                    act.wait_ge(s_cnt_ps, i * 2 + (par + 1))
                    r = rec_sb[:, bass.ds(i * 2 + par, 1), :].rearrange("p a k -> p (a k)")
                    A(nslot[:, par:par + 1], r[:, 3 * RW + R_SRCF:3 * RW + R_SRCF + 1], ACT.Copy, scale=-1.0).then_inc(s_nslot_ok, 1)
                    act.wait_ge(s_nslot_ok, i * 4 + (2 * par + 1))
                    A(ohtmp, iota_src[:], ACT.Abs, bias=nslot[:, par:par + 1]).then_inc(s_nslot_ok, 1)
                    act.wait_ge(s_nslot_ok, i * 4 + (2 * par + 2))
                    A(oh_src[:, par * GT + 3, :], ohtmp, ACT.Relu, scale=-1.0, bias=1.0).then_inc(s_oha_ok, 1)
                    act.wait_ge(s_oha_ok, i * 2 + (par + 1))
            act.wait_ge(s_rows_out, 16)
            for b in range(NB):
                act.wait_ge(s_cntt_ps, b + 1)
                for q in range(3):
                    j0, j1 = 4 * q, min(NB, 4 * q + 4)
                    ins = A(cnt_s[:, j0:j1, b * NP:(b + 1) * NP],
                            PS[:NP, 3 * (b % 2) + q, 0:(j1 - j0) * NP].rearrange("p (j n) -> p j n", n=NP), ACT.Copy)
                ins.then_inc(s_cnts_cp, 1)
            sc0 = 8.0 ** -0.5
            sc1 = SILU2 * float(HID) ** -0.5
            with act.Fori(0, G // 4) as i:
                for q in range(2):
                    act.wait_ge(s_ft_ps, i * 2 + (q + 3))
                    A(fT[:, q, :], PS[:16, 6 + q, :], ACT.Copy).then_inc(s_ft_cp, 1)
                for l in range(3):
                    for q in range(2):
                        act.wait_ge(s_mlp_ps, i * 6 + (2 * l + q + 1))
                        if l == 2:
                            act.wait_ge(s_h3_out0 if q == 0 else s_h3_out1, i * 16 + 16)
                        A(hid[:, q, l, :], PS[:, 4 + q, :], ACT.Silu, scale=sc0 if l == 0 else sc1).then_inc(s_hid_ok, 1)
                for q in range(2):
                    act.wait_ge(s_hid_ok, i * 6 + (4 + q + 1))
                    act.dma_start(h3_rows[bass.ds(i * 2 + q, 1), :, :].rearrange("q p n -> (q p) n"), hid[:, q, 2, :])\
                       .then_inc(s_h3_out0 if q == 0 else s_h3_out1, 16)
            act.wait_ge(s_h3_out0, 16 * (G // 4 + 1))
            act.wait_ge(s_h3_out1, 16 * (G // 4 + 1))
            act.sem_inc(s_mlp_done, 2)
            evac_uv(uvrow_sb, 2 * H, 0, s_uvrow_ok, s_uvt_ps)
            def evac_head(h, i, par):
                act.wait_ge(s_pv_done, h * NB + (NB + WR))
                num, den = par * C, C - par * C
                pv = PS[:, 3 * par:3 * par + 3, :].rearrange("p a n -> p (a n)")[:, 0:N]
                if par == 0:
                    act.wait_ge(s_norm_ok, i + 1)
                A(rrow[num:num + C, :], pv[den:den + C, :], ACT.Copy)
                A(OT[num:num + C, bass.ds(i, 1), :].rearrange("p a n -> p (a n)"), pv[num:num + C, :], ACT.Copy)\
                    .then_inc(s_head_free, 1)

            def act_head(h, par, before):
                for sblk in range(NB):
                    act.wait_ge(s_t_ok, h * NB + (sblk + 1))
                    A(wt[:, sblk % WR, :], wt[:, sblk % WR, :], ACT.Exp, bias=c2[:, par, sblk:sblk + 1]).then_inc(s_e_ok, 1)
                    if sblk == 2 and before is not None:
                        evac_head(*before)
            act_head(0, 0, None)
            with act.Fori(0, H // 2 - 1) as i:
                act_head(i * 2 + 1, 1, (i * 2, i, 0))
                act_head(i * 2 + 2, 0, (i * 2 + 1, i, 1))
            act_head(H - 1, 1, (H - 2, H // 2 - 1, 0))
            evac_head(H - 1, H // 2 - 1, 1)
            act.wait_ge(s_var_ok, 1)
            A(scl1[:], mv1[:, :, 1], ACT.Sqrt, bias=epsc[:, :]).then_inc(s_bnsd_ok, 1)
            act.wait_ge(s_bn_ok, 1)
            for k in range(KT):
                ins = A(OT[:, k, :], OT[:, k, :], ACT.Gelu, scale=scl1[:, k:k + 1], bias=shf1[:, k:k + 1])
            ins.then_inc(s_gelu_ok, 1)

            def ln_sqrt(layer):
                act.wait_ge(s_ln_var, layer)
                A(rstd[:], mv[:, :, 1], ACT.Sqrt, bias=epsc[:NP, :]).then_inc(s_ln_sd, 1)
            ln_sqrt(1)

            evac_T(xT1, s_xt1_ps, s_xt1_cp, (6, 7))
            for b in range(NB):
                act.wait_ge(s_xup_ps, b + 1)
                if b >= 2:
                    act.wait_ge(s_xup_out0 if b % 2 == 0 else s_xup_out1, 16 * (b // 2))
                A(xup_st[:, b % 2, :], PS[:NP, 6 + b % 2, :], ACT.Copy, scale=float(MUL) ** -0.5).then_inc(s_xup_cp, 1)

            with act.Fori(0, G // 2) as i:
                for par in range(2):
                    act.wait_ge(s_gidx_ok, i * 2 + (par + 1))
                    for k in range(GT):
                        act.wait_ge(s_tpw_ps, i * 8 + (4 * par + k + 1))
                        act.wait_ge(s_prod_ok, i * 8 + (4 * par + k + 1))
                        w = PS[:, (0, 1, 6, 7)[k], :].rearrange("p (q n) -> p q n", q=4)
                        y = gslot[:, par, k * RW + R_Y:k * RW + R_Y + 4]
                        wk = ws[:, k, :].rearrange("p (q n) -> p q n", q=5)
                        A(wk[:, 0:5:4, :], w[:, 0:2, :], ACT.Copy, scale=y[:, 0:1])
                        for m in range(3):
                            ins = A(wk[:, 1 + m, :], w[:, 2, :], ACT.Copy, scale=y[:, 1 + m:2 + m])
                        ins.then_inc(s_ws_ok, 1)

            for b in range(NB):
                for q in range(2):
                    act.wait_ge(s_mt_ps, 2 * b + q + 1)
                    if b >= 2 and q == 0:
                        act.wait_ge(s_y1_ps, b - 1)
                    v = PS[:, 2 * (b % 2) + q, :].rearrange("p (k n) -> p k n", k=4)[:, :, 0:NP]
                    dstv = msgT[:, b % 2, q * 4 * NP:(q + 1) * 4 * NP].rearrange("p (k n) -> p k n", k=4)
                    if q == 0:
                        ins = A(dstv, v, ACT.Copy)
                    else:
                        A(dstv[:, 0:3, :], v[:, 0:3, :], ACT.Copy)
                        ins = A(dstv[:, 3, :], v[:, 3, :], ACT.Copy, scale=3.0 ** -0.5)
                    ins.then_inc(s_mt_cp, 1)
            ln_sqrt(2)

            evac_T(xT2, s_xt2_ps, s_xt2_cp, (6, 7))
            evac_rows(rows2, 2, s_rows2_ps, s_rows2_cp, 0)
            act.wait_ge(s_cols2_ps, 1)
            A(sc[:, :, 0:2], PS[:NP, 3, 0:NB * 2].rearrange("p (b n) -> p b n", n=2), ACT.Copy).then_inc(s_cols2_cp, 1)
            evac_uv(uvrow2, 2, 0, s_uvrow2_ok, s_uvt2_ps)
            for k in range(NB):
                act.wait_ge(s_t2_ok, k + 1)
                if k >= 2:
                    act.wait_ge(s_p2_ok, k - 1)
                A(e2[:, k % 2, :], t2[:, k % 2, :], ACT.Exp, bias=c2[:, 0, k:k + 1]).then_inc(s_e2_ok, 1)
            evac_T(aggT, s_at_ps, s_at_cp, (6, 7))

            HW = HB * NP
            for half in range(2):
                av = aggT[:, :, half * HW:(half + 1) * HW]

                def as3(v):
                    return v.rearrange("p (k n) -> p k n", k=KT)
                if half == 0:
                    act.wait_ge(s_at_cp, NB)
                act.wait_ge(s_sp_free, 10 * half + 1)
                A(as3(basis[:, 0, :]), av, ACT.Silu).then_inc(s_silu_ok, 1)
                with act.Fori(0, NSPL // 2) as i:
                    for par in range(2):
                        act.wait_ge(s_cslot_ok, i * 2 + (8 * half + par + 1))
                        A(as3(sv), av, ACT.Abs, scale=KAPPA / STEP, bias=cslot[:, par:par + 1]).then_inc(s_sv_ok, 1)
                        act.wait_ge(s_sa_ok, i * 4 + (16 * half + 2 * par + 1))
                        A(sa2, sa, ACT.Square).then_inc(s_sq2_ok, 1)
                        act.wait_ge(s_sa_ok, i * 4 + (16 * half + 2 * par + 2))
                        A(sb2, sbb, ACT.Square).then_inc(s_sq2_ok, 1)
            ln_sqrt(3)
            evac_T(xT3, s_xt3_ps, s_xt3_cp, (6, 7))
            evac_T(nmT, s_nt_ps, s_nt_cp, (6, 7))
            ln_sqrt(4)

        @block.vector
        def _(dve):
            v = nc.vector
            ch = Chain(dve, s_dve_chain)
            link = ch.link

            v.memset(empty, 0.0).then_inc(s_empty_ok, 1)
            dve.wait_ge(s_empty_ok, 1)
            v.memset(empty[:, :, 0:1], -1.0).then_inc(s_empty_ok, 1)
            v.memset(blk, 0.0)
            v.memset(posf, 0.0)
            dve.wait_ge(s_dst_in, 16)
            link(v.tensor_copy(dstf, dsti))
            for b in range(1, NB):
                link(v.scalar_tensor_tensor(blk, dstf, float(b * NP), blk, ALU.is_ge, ALU.add))
            dve.wait_ge(s_consts, 1)
            for b in range(NB):
                link(v.tensor_scalar(mask[:, b, :], blk, float(b), None, ALU.is_equal))
                ins = v.tensor_tensor_scan(cum[:, b, :], ones[:NP, 0:EC], mask[:, b, :], 0.0, ALU.mult, ALU.add)
            link(ins)
            v.tensor_copy(tot, cum[:, :, EC - 1]).then_inc(s_tot_ok, 1)
            dve.wait_ge(s_rec_in, 48)
            v.scalar_tensor_tensor(rec[:, :, R_DL], blk, float(-NP), dstf, ALU.mult, ALU.add)
            v.tensor_copy(rec[:, :, R_SRCF], srci)
            v.tensor_copy(rec[:, :, R_SRCI].bitcast(i32), srci)
            v.memset(rec[:, :, 3], 0.0)
            v.tensor_copy(rec[:, :, R_Y:R_Y + 4], a4)
            v.tensor_copy(rec[:, :, R_F:R_F + 8], a8)
            dve.wait_ge(s_prefix_ps, 1)
            link(v.tensor_scalar(ngi, PS[:, 5, 16:16 + NB], float(GS - 1), None, ALU.add))
            link(v.tensor_scalar(ngi, ngi, GS.bit_length() - 1, None, ALU.arith_shift_right))
            link(v.tensor_copy(ngf, ngi))
            link(v.tensor_tensor_scan(gend, ones[:, :NB], ngf, 0.0, ALU.mult, ALU.add))
            link(v.tensor_tensor(gbase, gend, ngf, ALU.subtract))
            link(v.tensor_scalar(ngf, gbase, float(GS), -1.0, ALU.mult, ALU.add))
            ins = v.tensor_tensor(base, PS[:NP, 5, 0:NB], ngf[:NP], ALU.add)
            ins.then_inc(s_prefix_cp, 1)
            dve.wait_ge(s_prefix_cp, 1)
            for b in range(NB):
                link(v.scalar_tensor_tensor(ge, cum[:, b, :], base[:, b:b + 1], mask[:, b, :], ALU.add, ALU.mult))
                link(v.tensor_tensor(posf, posf, ge, ALU.add))
            v.tensor_copy(pos, posf).then_inc(s_rec_ok, 1)
            v.memset(gbf, 0.0)
            link(v.tensor_copy(gf, gi))
            for b in range(1, NB):
                link(v.scalar_tensor_tensor(gbf, gf, gbase[0:1, b:b + 1], gbf, ALU.is_ge, ALU.add))
            link(v.tensor_copy(gblk[:], gbf))

            dve.wait_ge(s_wg_in, 48)
            ptmp = at(12512, [128, 488])
            for k in range(KT):
                for q in range(2):
                    for hh in range(2):
                        c0 = hh * 256
                        link(v.tensor_tensor(ptmp[:, 0:256], w_gat[:, k, c0:c0 + 256], att_b[:, q, c0:c0 + 256], ALU.mult))
                        link(v.tensor_reduce(wa[:, k, q * H + hh * 4:q * H + hh * 4 + 4],
                                             ptmp[:, 0:256].rearrange("p (h c) -> p h c", h=4), X, ALU.add))
            dve.sem_inc(s_wa_ok, 1)
            dve.wait_ge(s_wk_in, 32)
            for b in range(NB):
                dve.wait_ge(s_skip_ps, b + 1)
                ins = v.tensor_tensor(x_sb[:, b, :], x_sb[:, b, :], PS[:NP, 6 + b % 2, :], ALU.add)
                ins.then_inc(s_skip_cp, 1)
                dve.wait_ge(s_skip_cp, b + 1)
                v.tensor_tensor(x_sb[:, b, :], x_sb[:, b, :], b_skip_b, ALU.add)

            dve.sem_inc(s_cnt_flushed, 2)
            dve.sem_inc(s_cnt_ps, 2)
            dve.sem_inc(s_h3_out0, 16)
            dve.sem_inc(s_h3_out1, 16)
            dve.sem_inc(s_ft_ps, 2)
            link(v.memset(cnt_d[:], 0))
            dve.wait_ge(s_recs_in, 16)

            def onehots(g, par):
                link(v.tensor_copy(rslot[:, par, :], rec_sb[:, bass.ds(g, 1), :].rearrange("p a k -> p (a k)")))
                for k in range(GT - 1):
                    r = rslot[:, par, k * RW:(k + 1) * RW]
                    ins = v.tensor_scalar(oh_src[:, par * GT + k, :], iota_src[:], r[:, R_SRCF:R_SRCF + 1], None, ALU.is_equal)
                ins.then_inc(s_oh_ok, 1)

            def flush_counts(g, par, ps_count):
                bv = dve.value_load(gblk[0:1, bass.ds(g, 1)], min_val=0, max_val=NB - 1)
                dve.wait_ge(s_cnt_ps, ps_count + 2)
                dve.wait_ge(s_cnt_flushed, ps_count + 1)
                dstv = cnt_d[:, bass.ds(bv * N, N)]
                psv = PS[:NP, 3 * par:3 * par + 3, :].rearrange("p a n -> p (a n)")[:, 0:N]
                v.tensor_tensor(dstv, psv, dstv, ALU.add).then_inc(s_cnt_flushed, 1)
            onehots(0, 0)
            with dve.Fori(0, G // 2 - 1) as i:
                ch.enter(i, 2)
                onehots(i * 2 + 1, 1)
                flush_counts(i * 2, 0, i * 2 + 1)
                onehots(i * 2 + 2, 0)
                flush_counts(i * 2 + 1, 1, i * 2 + 2)
            ch.leave(G // 2 - 1)
            onehots(G - 1, 1)
            flush_counts(G - 2, 0, G - 1)
            flush_counts(G - 1, 1, G)
            dve.wait_ge(s_cnt_flushed, G + 2)
            cd = cnt_d[:].rearrange("p (b n) -> p b n", n=N)
            for b in range(NB):
                if b >= 2:
                    dve.wait_ge(s_cntt_ps, b - 1)
                v.tensor_copy(cnt_f[:, b % 2, :], cd[:, b, :]).then_inc(s_cntf_ok, 1)
            link(v.tensor_reduce(deg[:], cd, X, ALU.add))

            def make_mask(mk, cm, loops):
                link(v.tensor_scalar(mk, cm, 0.0, NEG, ALU.is_equal, ALU.mult))
                if loops:
                    for b in range(NB):
                        d = mk[:, b, b * NP:(b + 1) * NP]
                        ins = v.scalar_tensor_tensor(d, ident[:NP, :NP], 0.0, d, ALU.is_equal, ALU.mult)
                    link(ins)
            make_mask(nomask, cd, True)
            dve.wait_ge(s_cnts_cp, NB)

            def self_loops(op):
                for b in range(NB):
                    d = cnt_s[:, b, b * NP:(b + 1) * NP]
                    ins = v.tensor_tensor(d, d, ident[:NP, :NP], op)
                link(ins)
            self_loops(ALU.add)
            dve.sem_inc(s_asb_free, 2)
            dve.sem_inc(s_mask_ok, 1)

            with dve.Fori(0, H // 2) as i:
                ch.enter(i, 2 * NB)
                for par in range(2):
                    dve.wait_ge(s_asb_in0 if par == 0 else s_asb_in1, i * 16 + 16)
                    for b in range(NB):
                        dve.nop(nofuse=True)
                        link(v.tensor_tensor_reduce(out=junk, in0=nomask[:, b, :], in1=as_b[:, par, :], scale=1.0,
                                                    scalar=NEG, op0=ALU.add, op1=ALU.max, accum_out=mx1[:, b:b + 1]))
                    v.tensor_copy(mxh[:, bass.ds(i * 2 + par, 1), :].rearrange("p a b -> p (a b)"), mx1[:]).then_inc(s_asb_free, 1)
                    dve.wait_ge(s_asb_free, i * 2 + (par + 3))
            ch.leave(H // 2)
            dve.wait_ge(s_asb_free, 2 + H)
            dve.sem_inc(s_max_done, 1)

            def softmax_terms(nh, center, neigh, mxv, guard):
                mt = at(18200, [NP, NB * nh]) if nh > 1 else at(27000, [NP, NB])
                mt3 = mt.rearrange("p (b h) -> p b h", h=nh)
                link(v.tensor_tensor(mt3, mxv, center, ALU.add))
                link(v.scalar_tensor_tensor(mt, mt, SLOPE, mt, ALU.mult, ALU.max))
                link(v.tensor_tensor(uv[:, :, 0:nh], center, mt3, ALU.subtract))
                link(v.scalar_tensor_tensor(uv[:, :, nh:2 * nh], center, SLOPE, mt3, ALU.mult, ALU.subtract))
                v.tensor_scalar(sc8[:, 0:nh, :], neigh, 1.0 - SLOPE, None, ALU.mult)
                link(v.tensor_scalar(sc2[:, 0:nh, :], neigh, SLOPE, None, ALU.mult))
            dve.wait_ge(s_mlp_done, 1)
            softmax_terms(H, sc[:, :, H:2 * H], sc[:, :, 0:H].rearrange("p b h -> p h b"),
                          mxh[:].rearrange("p h b -> p b h"), False)
            for n, sblk in enumerate(POOL_P):
                ins = v.tensor_copy(cnt_pool[n], cnt_s[:, sblk, :])
            link(ins)
            dve.sem_inc(s_uv_ok, 1)
            dve.sem_inc(s_uv_free, 2)
            dve.sem_inc(s_head_free, 2)
            dve.sem_inc(s_norm_ok, 1)
            dve.sem_inc(s_pv_done, WR)

            def t_tile(dst, U, V, cc, ok):
                v.scalar_tensor_tensor(dst, U, cc, V, ALU.add, ALU.max).then_inc(ok, 1)

            def p_tile(dst, e, cm, ok):
                v.scalar_tensor_tensor(dst, e, 1.0, cm, ALU.min, ALU.mult).then_inc(ok, 1)

            def first_step(h, i, par, sblk):
                if sblk == 0:
                    v.tensor_copy(c8[:, par, :], sc8[:, bass.ds(h, 1), :].rearrange("p a b -> p (a b)"))
                    link(v.tensor_copy(c2[:, par, :], sc2[:, bass.ds(h, 1), :].rearrange("p a b -> p (a b)")))
                    dve.wait_ge(s_uv_in0 if par == 0 else s_uv_in1, i * 32 + 32)
                dve.wait_ge(s_pv_done, h * NB + (sblk + 1))
                t_tile(wt[:, sblk % WR, :], UV[:, par, 0, :], UV[:, par, 1, :], c8[:, par, sblk:sblk + 1], s_t_ok)

            def recip(i):
                dve.wait_ge(s_head_free, i * 2 + 4)
                v.reciprocal(rrow, rrow).then_inc(s_rrow_ok, 1)

            def dve_head(h, i, par, last=False, rec=None):
                for sblk in range(NB):
                    if sblk + LEAD < NB:
                        first_step(h, i, par, sblk + LEAD)
                    elif not last:
                        first_step(h + 1, i + par, 1 - par, sblk + LEAD - NB)
                    if sblk not in POOL_P:
                        dve.wait_ge(s_e_ok, h * NB + (sblk + 1))
                        p_tile(wt[:, sblk % WR, :], wt[:, sblk % WR, :], cnt_s[:, sblk, :], s_p_ok)
                    if sblk + LEAD == NB:
                        dve.wait_ge(s_t_ok, h * NB + NB)
                        dve.sem_inc(s_uv_free, 1)
                    if sblk == 4 and rec is not None:
                        recip(rec)
            for sblk in range(LEAD):
                first_step(0, 0, 0, sblk)
            dve_head(0, 0, 0)
            with dve.Fori(0, H // 2 - 1) as i:
                ch.enter(i, 2)
                dve_head(i * 2 + 1, i, 1)
                dve_head(i * 2 + 2, i + 1, 0, rec=i)
            ch.leave(H // 2 - 1)
            dve_head(H - 1, H // 2 - 1, 1, last=True)
            recip(H // 2 - 1)
            n_p = H * (NB - len(POOL_P))
            dve.wait_ge(s_p_ok, n_p)
            dve.wait_ge(s_pp_ok, H * len(POOL_P))
            dve.wait_ge(s_norm_ok, H // 2 + 1)
            self_loops(ALU.subtract)

            dve.wait_ge(s_bn_in, 48)
            for k in range(KT):
                for q in range(5):
                    ins = v.bn_stats(bst1[:, k, q, :], OT[:, k, q * (N // 5):(q + 1) * (N // 5)])
            link(ins)
            for k in range(KT):
                ins = v.bn_aggr(mv1[:, k, :], bst1[:, k, :, :].rearrange("p q n -> p (q n)"))
            ins.then_inc(s_var_ok, 1)
            dve.wait_ge(s_bnsd_ok, 1)
            link(v.reciprocal(scl1[:], scl1[:]))
            link(v.tensor_tensor(scl1[:], scl1[:], bnp[:, 1, :], ALU.mult))
            link(v.tensor_tensor(shf1[:], mv1[:, :, 0], bnp[:, 0, :], ALU.add))
            link(v.tensor_tensor(shf1[:], bnp[:, 0, :], shf1[:], ALU.subtract))
            link(v.tensor_tensor(shf1[:], shf1[:], scl1[:], ALU.mult))
            v.tensor_tensor(shf1[:], shf1[:], bnp[:, 2, :], ALU.add).then_inc(s_bn_ok, 1)
            for b in range(NB):
                dve.wait_ge(s_o_ps, b + 1)
                ins = v.tensor_tensor(x_sb[:, b, :], x_sb[:, b, :], PS[:NP, 6 + b % 2, :], ALU.add)
                ins.then_inc(s_o_cp, 1)
            dve.wait_ge(s_o_cp, NB)

            def layernorm(layer, last=False):
                for b in range(NB):
                    link(v.bn_stats(bst[:, b, :], x_sb[:, b, :]))
                    ins = v.bn_aggr(mv[:, b, :], bst[:, b, :])
                ins.then_inc(s_ln_var, 1)
                dve.wait_ge(s_ln_sd, layer)
                link(v.reciprocal(rstd[:], rstd[:]))
                for b in range(NB):
                    ins = v.tensor_scalar(x_sb[:, b, :], x_sb[:, b, :], mv[:, b, 0:1], rstd[:, b:b + 1], ALU.subtract, ALU.mult)
                ins.then_inc(s_x_ok, 1)
                dve.wait_ge(s_x_ok, layer)
                if last:
                    dve.sem_inc(s_final_ok, 1)
            layernorm(1, False)

            v.memset(acc, 0.0).then_inc(s_acc_zero, 1)
            dve.wait_ge(s_acc_zero, 1)
            dve.wait_ge(s_xup_cp, NB)
            dve.sem_inc(s_prod_ok, GT)
            dve.sem_inc(s_scat_done, GT)
            dve.sem_inc(s_acc_free, 2)

            def products(par, k, T, T3, gath):
                if k == 0:
                    dve.wait_ge(s_sel_ok, T(1))
                dve.wait_ge(s_gath[par * GT + k], gath)
                xg = ring[:, par * GT + k, :].rearrange("p (q n) -> p q n", q=4)
                y = gslot[:, par, k * RW + R_Y:k * RW + R_Y + 4]
                wk = ws[:, k, :].rearrange("p (q n) -> p q n", q=5)
                pr = prod[:, k, :].rearrange("p (q n) -> p q n", q=8)
                v.tensor_scalar(q4[:, 0, :], xg[:, 1, :], y[:, 1:2], None, ALU.mult).then_inc(s_q_ok, 1)
                dve.wait_ge(s_ws_ok, T(1))
                dve.wait_ge(s_scat_done, T(1))
                v.tensor_tensor(pr[:, 0:4, :], wk[:, 0:4, :], xg[:, 0:1, :].to_broadcast([128, 4, MUL]), ALU.mult)
                dve.wait_ge(s_q_ok, T3(1))
                v.scalar_tensor_tensor(q4[:, 1, :], xg[:, 2, :], y[:, 2:3], q4[:, 0, :], ALU.mult, ALU.add).then_inc(s_q_ok, 1)
                v.tensor_tensor(pr[:, 4:7, :], wk[:, 4:5, :].to_broadcast([128, 3, MUL]), xg[:, 1:4, :], ALU.mult)
                dve.wait_ge(s_q_ok, T3(2))
                v.scalar_tensor_tensor(q4[:, 2, :], xg[:, 3, :], y[:, 3:4], q4[:, 1, :], ALU.mult, ALU.add).then_inc(s_q_ok, 1)
                dve.wait_ge(s_q_ok, T3(3))
                v.tensor_tensor(pr[:, 7, :], PS[:, (0, 1, 6, 7)[k], 3 * MUL:4 * MUL], q4[:, 2, :], ALU.mult).then_inc(s_prod_ok, 1)

            def flush(g, par, n_scat):
                bv = dve.value_load(gblk[0:1, bass.ds(g, 1)], min_val=0, max_val=NB - 1)
                dve.wait_ge(s_scat_done, n_scat)
                dve.wait_ge(s_acc_free, g + 2)
                d = acc[:, bass.ds(bv * 1024, 1024)]
                psv = PS[:NP, 2 + 2 * par:4 + 2 * par, :].rearrange("p a n -> p (a n)")
                v.tensor_tensor(d, psv, d, ALU.add).then_inc(s_acc_free, 1)
            for k in range(GT):
                products(0, k, lambda m, k=k: k + m, lambda m, k=k: 3 * k + m, 16)
            with dve.Fori(0, G // 2 - 1) as i:
                for par in (1, 0):
                    g = i * 2 + (2 - par)
                    off = 4 * (2 - par)
                    for k in range(GT):
                        products(par, k, lambda m, k=k: i * 8 + (off + k + m), lambda m, k=k: i * 24 + (3 * (off + k) + m),
                                 i * 16 + (16 if par else 32))
                        if k == 1:
                            flush(i * 2 + (1 - par), 1 - par, i * 8 + (off + GT))
            for k in range(GT):
                products(1, k, lambda m, k=k: (G - 1) * GT + k + m, lambda m, k=k: 3 * ((G - 1) * GT + k) + m, 16 * (G // 2))
                if k == 1:
                    flush(G - 2, 0, (G - 1) * GT + GT)
            flush(G - 1, 1, G * GT + GT)
            dve.wait_ge(s_acc_free, G + 2)
            dve.sem_inc(s_acc_done, 1)
            oscale = SILU2 * HID ** -0.5 * (2 * MUL) ** -0.5 / 10.0
            for b in range(NB):
                dve.wait_ge(s_y1_ps, b + 1)
                v.scalar_tensor_tensor(x_sb[:, b, 0:MUL], PS[:NP, 4 + b % 2, 0:MUL], oscale, x_sb[:, b, 0:MUL], ALU.mult, ALU.add)
                xv = x_sb[:, b, MUL:D].rearrange("p (u m) -> p m u", m=3)
                v.scalar_tensor_tensor(xv, PS[:NP, 4 + b % 2, MUL:D].rearrange("p (m u) -> p m u", m=3), oscale, xv,
                                       ALU.mult, ALU.add).then_inc(s_y1_cp, 1)
            dve.wait_ge(s_y1_cp, NB)
            layernorm(2, False)

            dve.wait_ge(s_wl2_in, 48)
            for k in range(KT):
                for q in range(2):
                    link(v.tensor_tensor(tmp2, w_l2[:, k, :], a_b[:, q, :], ALU.mult))
                    link(v.tensor_reduce(wa[:, k, q:q + 1], tmp2, X, ALU.add))
            dve.sem_inc(s_wa2_ok, 1)
            make_mask(nomask2, cnt_s[:], False)
            dve.wait_ge(s_st_in, 16)
            for b in range(NB):
                link(v.tensor_tensor_reduce(out=junk2, in0=nomask2[:, b, :], in1=st_b, scale=1.0, scalar=NEG,
                                            op0=ALU.add, op1=ALU.max, accum_out=mx1[:, b:b + 1]))
            link(v.scalar_tensor_tensor(mx1[:], mx1[:], 0.5 * NEG, mx1[:], ALU.is_gt, ALU.mult))
            dve.wait_ge(s_cols2_cp, 1)
            softmax_terms(1, sc[:, :, 0:1], sc[:, :, 1:2].rearrange("p b h -> p h b"), mx1[:].unsqueeze(2), True)
            v.tensor_copy(c8[:, 0, :], sc8[:, 0, :])
            link(v.tensor_copy(c2[:, 0, :], sc2[:, 0, :]))
            dve.sem_inc(s_uv2_ok, 1)
            dve.wait_ge(s_uv2_in, 32)
            for k in range(NB + 1):
                if k < NB:
                    t_tile(t2[:, k % 2, :], UV2[:, 0, :], UV2[:, 1, :], c8[:, 0, k:k + 1], s_t2_ok)
                if k >= 1:
                    dve.wait_ge(s_e2_ok, k)
                    p_tile(P50[:, k - 1, :], e2[:, (k - 1) % 2, :], cd[:, k - 1, :], s_p2_ok)
            for b in range(NB):
                dve.wait_ge(s_l2_agg, b + 1)
                link(v.tensor_scalar(rden[:, b:b + 1], PS[:NP, 6 + b % 2, 0:1], 0.5, None, ALU.max))
                link(v.reciprocal(rden[:, b:b + 1], rden[:, b:b + 1]))
                v.tensor_scalar(agg[:, b, :], PS[:NP, 4 + b % 2, :], rden[:, b:b + 1], None, ALU.mult).then_inc(s_l2_cp, 1)
            link(v.tensor_scalar(cen[:], cen[:], -KAPPA, KAPPA * (1.0 + 1.0 / STEP), ALU.mult, ALU.add))
            dve.wait_ge(s_at_cp, NB)
            dve.sem_inc(s_aggT_ok, 1)
            dve.sem_inc(s_sp_free, 2)
            for half in range(2):
                with dve.Fori(0, NSPL // 2) as i:
                    ch.enter(i, 4)
                    for par in range(2):
                        slot = 1 - par
                        v.tensor_copy(cslot[:, par:par + 1], cen[:, bass.ds(i * 2 + par, 1)]).then_inc(s_cslot_ok, 1)
                        dve.wait_ge(s_sv_ok, i * 2 + (8 * half + par + 1))
                        v.tensor_scalar(sa, sv, 2 * KAPPA, 2 * KAPPA, ALU.min, ALU.subtract).then_inc(s_sa_ok, 1)
                        v.tensor_scalar(sbb, sv, KAPPA, KAPPA, ALU.min, ALU.subtract).then_inc(s_sa_ok, 1)
                        dve.wait_ge(s_sq2_ok, i * 4 + (16 * half + 2 * par + 1))
                        link(v.tensor_tensor(sa2, sa2, sa, ALU.mult))
                        dve.wait_ge(s_sq2_ok, i * 4 + (16 * half + 2 * par + 2))
                        link(v.tensor_tensor(sb2, sb2, sbb, ALU.mult))
                        dve.wait_ge(s_sp_free, i * 2 + (9 * half + par + 2))
                        v.scalar_tensor_tensor(basis[:, slot, :], sb2, 4.0, sa2, ALU.mult, ALU.subtract).then_inc(s_basis_ok, 1)
                ch.leave(NSPL // 2)
                dve.wait_ge(s_sp_free, 9 * half + 11)
                for b in range(HB):
                    bb = half * HB + b
                    v.tensor_tensor(x_sb[:, bb, :], x_sb[:, bb, :], PS[:NP, b, :], ALU.add).then_inc(s_y2_cp, 1)
            dve.wait_ge(s_y2_cp, NB)
            layernorm(3, False)

            for k in range(NB):
                v.tensor_copy(P50[:, k, :], cnt_s[:, k, :]).then_inc(s_p3_ok, 1)
            link(v.tensor_scalar(deg[:], deg[:], 1.0, None, ALU.max))
            link(v.reciprocal(deg[:], deg[:]))
            for b in range(NB):
                dve.wait_ge(s_l3_agg, b + 1)
                v.tensor_scalar(nm[:, b, :], PS[:NP, b % 2, :], deg[:, b:b + 1], None, ALU.mult).then_inc(s_l3_cp, 1)
            for b in range(NB):
                dve.wait_ge(s_y3_ps, b + 1)
                v.scalar_tensor_tensor(x_sb[:, b, :], PS[:NP, 4 + b % 2, :], 0.0, x_sb[:, b, :], ALU.max, ALU.add)\
                    .then_inc(s_y3_cp, 1)
            dve.wait_ge(s_y3_cp, NB)
            layernorm(4, True)


_INS = ("x", "src", "dst", "edge_attr_4", "edge_attr_8", "L0_gnn_W_gat", "L0_gnn_att_src", "L0_gnn_att_dst",
        "L0_gnn_gat_bias", "L0_gnn_bn_gamma", "L0_gnn_bn_beta", "L0_gnn_W_skip", "L0_gnn_b_skip",
        "L1_gnn_W_up0", "L1_gnn_W_up1", "L1_gnn_W_mlp1", "L1_gnn_W_mlp2", "L1_gnn_W_mlp3", "L1_gnn_W_mlp4",
        "L1_gnn_W_out0", "L1_gnn_W_out1", "L2_gnn_W", "L2_gnn_a")


def kernel(**inputs):
    import numpy as _np
    import concourse.bacc as _bacc
    from concourse import mybir as _mybir
    from concourse.bass_utils import run_bass_kernel_spmd as _run

    nc = _bacc.Bacc("TRN2", target_bir_lowering=False, num_devices=1)
    laid = {name: _np.asarray(inputs[name]) for name in _INS}
    for name in ("L0_gnn_gat_bias", "L0_gnn_bn_gamma", "L0_gnn_bn_beta"):
        laid[name] = laid[name].reshape(KT, 128).T
    laid["L1_gnn_W_mlp4"] = laid["L1_gnn_W_mlp4"].reshape(HID, 4, MUL)[:, [0, 2, 1, 3], :].reshape(HID, 4 * MUL)
    laid["base_wT"] = _np.asarray(inputs["L2_gnn_base_w"]).T
    laid["spline_wT"] = _np.asarray(inputs["L2_gnn_spline_w"]).transpose(2, 1, 0)
    laid["w_l3T"] = _np.asarray(inputs["L3_gnn_w"]).T
    arrays, args = {}, {}
    for name, v in laid.items():
        v = _np.ascontiguousarray(v)
        arrays[f"in_{name}"] = v
        args[name] = nc.dram_tensor(f"in_{name}", v.shape, _mybir.dt.from_np(v.dtype), kind="ExternalInput").ap()
    out = nc.dram_tensor("out", (N, D), _mybir.dt.float32, kind="ExternalOutput").ap()
    build(nc, args, out)
    r = _run(nc, [arrays], core_ids=[0])
    return r.results[0]["out"]
```

```python
import numpy as np
import concourse.bass as bass
from concourse import mybir
from contextlib import ExitStack

N, D, E = 1250, 512, 21250
H, C = 8, 64
MUL, HID = 128, 64
NP, NB = 125, 10
KT = D // 128
EC = E // NP
GT = 4
GS = GT * 128
G = (E + NB * (GS - 1)) // GS
G += G % 2
RW = 16
R_DL, R_SRCF, R_SRCI, R_Y, R_F = 0, 1, 2, 4, 8
NEG = -1.0e30
SLOPE = 0.2
EPS = 1e-5
SB = 10
ROUNDS = EC // SB
NSPL = 8
STEP = 2.0 / 5
KAPPA = (1.0 / 6.0) ** (1.0 / 3.0)
SILU2 = 1.679177
WR = 5
LEAD = 2
POOL_P = (1, 4, 7)
assert NB % WR == 0 and G % 4 == 0
HB = NB // 2
assert NP * NB == N and NP * EC == E and ROUNDS * SB == EC and ROUNDS % 2 == 1


class Chain:

    def __init__(self, eng, sem):
        self.eng, self.sem, self.n, self.i, self.per, self.at = eng, sem, 0, None, 0, 0

    def link(self, ins):
        ins.then_inc(self.sem, 1)
        self.at += 1
        if self.i is None:
            self.n, self.at = self.n + self.at, 0
            self.eng.wait_ge(self.sem, self.n)
        else:
            self.eng.wait_ge(self.sem, self.i * self.per + (self.n + self.at))

    def trail(self, ins):
        ins.then_inc(self.sem, 1)
        self.at += 1
        self.eng.wait_ge(self.sem, (0 if self.i is None else self.i * self.per) + (self.n + self.at - 1))

    def enter(self, i, per):
        self.i, self.per, self.at = i, per, 0

    def leave(self, times):
        assert self.at == self.per, (self.at, self.per)
        self.n += times * self.per
        self.i, self.at = None, 0


def build(nc, a, out):
    f32, i32, u32 = mybir.dt.float32, mybir.dt.int32, mybir.dt.uint32
    f32r = mybir.dt.float32r
    bf16, f16, u16 = mybir.dt.bfloat16, mybir.dt.float16, mybir.dt.uint16
    ALU = mybir.AluOpType
    ACT = mybir.ActivationFunctionType
    X = mybir.AxisListType.X
    ctx = ExitStack()
    with ctx:
        def sb(name, shape, dt=f32):
            return ctx.enter_context(nc.sbuf_tensor(name, shape, dt))

        def dram(name, shape, dt=f32):
            return nc.dram_tensor(name, shape, dt, kind="Internal").ap()

        def sem(name):
            return ctx.enter_context(nc.semaphore(name))

        recs = dram("recs", ((G + 2) * GS, RW))
        as_rows = dram("as_rows", (2 * H, N))
        uv_rows = dram("uv_rows", (2 * H, N))
        uv2_rows = dram("uv2_rows", (2, N))
        h3_rows = dram("h3_rows", (G // 2, 128, GS))
        xup = dram("xup", (N, D))

        x_sb = sb("x_sb", [NP, NB, D])
        cnt_d = sb("cnt_d", [NP, NB * N], u16)
        cnt_s = sb("cnt_s", [NP, NB, N], u16)
        gld = sb("gld", [128, 2, GT * RW])
        h3r = sb("h3r", [128, 2, GS], f32r)
        w4r = sb("w4r", [128, 2, 4 * MUL], f32r)
        ident = sb("ident", [128, 128])
        upper = sb("upper", [128, 128])
        ones = sb("ones", [128, 192])
        iota_src = sb("iota_src", [128, N], f16)
        iota_dst = sb("iota_dst", [128, NP], f32)
        gblk = sb("gblk", [1, G + 2], i32)
        epsc = sb("epsc", [128, 1])
        mv = sb("mv", [NP, NB, 2])
        bst = sb("bst", [NP, NB, 6])
        rstd = sb("rstd", [NP, NB])
        deg = sb("deg", [NP, NB])
        ARENA = 29550
        arena = sb("arena", [128, ARENA])

        def at(off, shape, dt=f32):
            size = int(np.prod(shape[1:]))
            words = size if dt in (f32, f32r, i32, u32) else (size + 1) // 2
            assert off + words <= ARENA
            v = arena[:shape[0], off:off + words]
            if dt != f32:
                v = v.bitcast(dt)
            if len(shape) == 3:
                v = v.rearrange("p (a b) -> p a b", a=shape[1])
            if len(shape) == 4:
                v = v.rearrange("p (a b c) -> p a b c", a=shape[1], b=shape[2])
            return v

        PS = ctx.enter_context(nc.psum_tensor("PS", [128, 8, 512], f32))

        o = [0]

        def nxt(shape, dt=f32):
            v = at(o[0], shape, dt)
            o[0] += int(np.prod(shape[1:]))
            return v
        srci, dsti = nxt([NP, EC], i32), nxt([NP, EC], i32)
        dstf, blk, posf = (nxt([NP, EC]) for _ in range(3))
        pos = nxt([NP, EC], u32)
        mask, cum = nxt([NP, NB, EC]), nxt([NP, NB, EC])
        a4, a8, rec = nxt([NP, EC, 4]), nxt([NP, EC, 8]), nxt([NP, EC, RW])
        EMP = 54
        assert (G + 2) * GS % (128 * EMP) == 0
        empty = nxt([128, EMP, RW])
        tot, base = nxt([NP, NB]), nxt([NP, NB])
        ngi, ngf, gend, gbase = nxt([128, NB], i32), nxt([128, NB]), nxt([128, NB]), nxt([128, NB])
        gi, gf, gbf = nxt([1, G + 2], i32), nxt([1, G + 2]), nxt([1, G + 2])
        stage_rec, stage_pos = nxt([NP, 2, SB, RW]), nxt([NP, 2, SB], u32)
        assert o[0] <= 12000
        b_skip_b = at(12000, [NP, D])
        xT = at(13000, [128, KT, N])
        w_gat, w_skip = at(18000, [128, KT, D]), at(20048, [128, KT, D])
        att_b = at(22096, [128, 2, D])
        h_sb = at(23120, [NP, NB, D])
        wa = sb("wa", [128, KT, 2 * H])
        sc = sb("sc", [NP, NB, 2 * H])
        rows16 = cnt_s[0:2 * H, 0:2, :].rearrange("p a n -> p (a n)").bitcast(f32)
        mx1 = sb("mx1", [NP, NB])
        mxh = sb("mxh", [NP, H, NB])
        uv = sb("uv", [NP, NB, 2 * H])
        c8 = sb("c8", [NP, 2, NB])
        c2 = sb("c2", [NP, 2, NB])
        sc8 = sb("sc8", [NP, H, NB])
        sc2 = sb("sc2", [NP, H, NB])
        rden = sb("rden", [NP, NB])
        oh_src = at(0, [128, 2 * GT, N], bf16)
        oh_dst = at(5000, [128, 2 * GT, NP + 1], bf16)
        cnt_f = at(5600, [NP, 2, N])
        rec_sb = at(9300, [128, G + 2, GT * RW])
        pslot = sb("pslot", [128, 2, GT * RW])
        nslot = sb("nslot", [128, 2])
        ohtmp = sb("ohtmp", [128, NP])
        cnt_ev = at(5600, [NP, 2, N], u16)
        nomask = at(13000, [NP, NB, N], bf16)
        as_b = at(2000, [NP, 2, N])
        junk = at(4600, [NP, 2, N], bf16)
        uvrow_sb = at(8000, [2 * H, N])
        UV = at(0, [NP, 2, 2, N])
        wt = at(5000, [NP, WR, N])
        cnt_pool = (at(11400, [NP, N]), at(18020, [NP, N]), at(28300, [NP, N]))
        OT = at(13000, [128, KT, N])
        hs = at(19300, [NP, NB, 3 * C])
        rrow = at(21400, [128, N])
        fT = at(5900, [2 * 8, 2, GS])
        hid = at(19300, [128, 2, 3, GS])
        w_m1, w_m2, w_m3 = sb("w_m1", [2 * 8, 128]), sb("w_m2", [128, 128]), sb("w_m3", [128, 128])
        fsl = sb("fsl", [128, 2, GT, 2 * 8])
        bnp = sb("bnp", [128, 3, KT])
        bst1 = sb("bst1", [128, KT, 5, 6])
        mv1 = sb("mv1", [128, KT, 2])
        scl1 = sb("scl1", [128, KT])
        shf1 = sb("shf1", [128, KT])
        acc = at(0, [NP, NB * 1024])
        ring = at(10240, [128, 2 * GT, D])
        xT1 = at(14336, [128, KT, N])
        xup_st = at(19500, [NP, 2, D])
        prod = at(14336, [128, GT, 8 * MUL])
        sel = at(18432, [128, 2 * GT, NP])
        ws = at(19500, [128, GT, 5 * MUL])
        q4 = at(22100, [128, 2, MUL])
        qa = at(24560, [128, GT, MUL])
        h3 = at(23530, [128, 2, GS])
        gsum = at(27000, [NP, 2, 1024])
        w_up0, w_up1 = at(25504, [128, MUL]), at(25632, [128, MUL])
        w_m4 = at(25952, [128, 4 * MUL])
        w_o0, w_o1 = at(26464, [128, 2, MUL]), at(26720, [128, 2, MUL])
        msgT = at(18432, [128, 2, 8 * NP])
        gidx = sb("gidx", [128, 2, GT], u32)
        gslot = sb("gslot", [128, 2, GT * RW])
        P50 = at(0, [NP, NB, N])
        UV2 = at(12500, [NP, 2, N])
        t2, e2 = at(15000, [NP, 2, N]), at(17500, [NP, 2, N])
        wa2 = sb("wa2", [128, KT, 2])
        w_l2, a_b, tmp2 = at(18000, [128, KT, D]), at(22096, [128, 2, D]), at(20048, [128, D])
        xT2 = at(20440, [128, KT, N])
        w_rep = at(0, [128, KT, NP])
        uvrow2 = at(9500, [2, N])
        st_b = at(10800, [NP, N])
        nomask2 = at(12100, [NP, NB, N], bf16)
        junk2 = at(18800, [NP, 2, N], bf16)
        aggr = at(16600, [128, KT, N])
        rden2 = at(21700, [128, N])
        aggT = at(0, [128, KT, N])
        basis = at(5000, [128, 2, KT * HB * NP])
        w_sp = at(12500, [128, 2, KT * D])
        sv, sa, sbb, sa2, sb2 = (at(o, [128, KT * HB * NP]) for o in (10000, 16600, 19100, 21600, 24100))
        cen = sb("cen", [128, NSPL])
        cslot = sb("cslot", [128, 2])
        w_l3 = at(0, [128, 2 * KT, D])
        cnt50 = at(4100, [NP, NB, N])
        z_sb = at(16700, [NP, NB, D])
        fin = at(21900, [NP, 2, D])
        xT3 = at(23200, [128, KT, N])

        s_acc_done = sem("s_acc_done")
        s_acc_free = sem("s_acc_free")
        s_acc_zero = sem("s_acc_zero")
        s_aggT_ok = sem("s_aggT_ok")
        s_asb_free = sem("s_asb_free")
        s_asb_in0 = sem("s_asb_in0")
        s_asb_in1 = sem("s_asb_in1")
        s_basis_ok = sem("s_basis_ok")
        s_bn_in = sem("s_bn_in")
        s_bn_ok = sem("s_bn_ok")
        s_bnsd_ok = sem("s_bnsd_ok")
        s_cnt_flushed = sem("s_cnt_flushed")
        s_cnt_left = sem("s_cnt_left")
        s_cnt_ps = sem("s_cnt_ps")
        s_cntf_ok = sem("s_cntf_ok")
        s_cnts_cp = sem("s_cnts_cp")
        s_cntt_ps = sem("s_cntt_ps")
        s_cols2_cp = sem("s_cols2_cp")
        s_cols2_ps = sem("s_cols2_ps")
        s_cols_cp = sem("s_cols_cp")
        s_cols_ps = sem("s_cols_ps")
        s_const0 = sem("s_const0")
        s_consts = sem("s_consts")
        s_cslot_ok = sem("s_cslot_ok")
        s_dst_in = sem("s_dst_in")
        s_dve_chain = sem("s_dve_chain")
        s_e2_ok = sem("s_e2_ok")
        s_e_ok = sem("s_e_ok")
        s_empty_ok = sem("s_empty_ok")
        s_fin_ok = sem("s_fin_ok")
        s_fs_ok = sem("s_fs_ok")
        s_ft_cp = sem("s_ft_cp")
        s_ft_ps = sem("s_ft_ps")
        s_gelu_ok = sem("s_gelu_ok")
        s_gidx_ok = sem("s_gidx_ok")
        s_gld_in0 = sem("s_gld_in0")
        s_gld_in1 = sem("s_gld_in1")
        s_gsum_ok = sem("s_gsum_ok")
        s_h3_in0 = sem("s_h3_in0")
        s_h3_in1 = sem("s_h3_in1")
        s_h3_ok = sem("s_h3_ok")
        s_h3_out0 = sem("s_h3_out0")
        s_h3_out1 = sem("s_h3_out1")
        s_h3hi_ok = sem("s_h3hi_ok")
        s_h_cp = sem("s_h_cp")
        s_h_ps = sem("s_h_ps")
        s_head_free = sem("s_head_free")
        s_hid_ok = sem("s_hid_ok")
        s_hs_ok = sem("s_hs_ok")
        s_l2_agg = sem("s_l2_agg")
        s_l2_cp = sem("s_l2_cp")
        s_ln_sd = sem("s_ln_sd")
        s_ln_var = sem("s_ln_var")
        s_max_stage = sem("s_max_stage")
        s_min_ok = sem("s_min_ok")
        s_mlp_done = sem("s_mlp_done")
        s_mlp_ps = sem("s_mlp_ps")
        s_mt_cp = sem("s_mt_cp")
        s_mt_ps = sem("s_mt_ps")
        s_norm_ok = sem("s_norm_ok")
        s_nslot_ok = sem("s_nslot_ok")
        s_o_cp = sem("s_o_cp")
        s_o_ps = sem("s_o_ps")
        s_oh_ok = sem("s_oh_ok")
        s_oha_ok = sem("s_oha_ok")
        s_ohd_ok = sem("s_ohd_ok")
        s_out_done = sem("s_out_done")
        s_p2_ok = sem("s_p2_ok")
        s_p3_ok = sem("s_p3_ok")
        s_p_ok = sem("s_p_ok")
        s_pp_ok = sem("s_pp_ok")
        s_prefix_cp = sem("s_prefix_cp")
        s_prefix_ps = sem("s_prefix_ps")
        s_prod_ok = sem("s_prod_ok")
        s_pslot_ok = sem("s_pslot_ok")
        s_pv_done = sem("s_pv_done")
        s_q_ok = sem("s_q_ok")
        s_rec_in = sem("s_rec_in")
        s_rec_ok = sem("s_rec_ok")
        s_recs_clear = sem("s_recs_clear")
        s_recs_in = sem("s_recs_in")
        s_rows2_out = sem("s_rows2_out")
        s_rows_cp = sem("s_rows_cp")
        s_rows_out = sem("s_rows_out")
        s_rows_ps = sem("s_rows_ps")
        s_rrow_ok = sem("s_rrow_ok")
        s_sa_ok = sem("s_sa_ok")
        s_scat_done = sem("s_scat_done")
        s_scattered0 = sem("s_scattered0")
        s_scattered1 = sem("s_scattered1")
        s_silu_ok = sem("s_silu_ok")
        s_skip_cp = sem("s_skip_cp")
        s_skip_ps = sem("s_skip_ps")
        s_sp_free = sem("s_sp_free")
        s_sq2_ok = sem("s_sq2_ok")
        s_st_ok = sem("s_st_ok")
        s_st_ps = sem("s_st_ps")
        s_staged = sem("s_staged")
        s_sv_ok = sem("s_sv_ok")
        s_t2_ok = sem("s_t2_ok")
        s_t_ok = sem("s_t_ok")
        s_tot_ok = sem("s_tot_ok")
        s_tpw_ps = sem("s_tpw_ps")
        s_uv2_in = sem("s_uv2_in")
        s_uv2_ok = sem("s_uv2_ok")
        s_uv_free = sem("s_uv_free")
        s_uv_in0 = sem("s_uv_in0")
        s_uv_in1 = sem("s_uv_in1")
        s_uv_ok = sem("s_uv_ok")
        s_uvrow2_ok = sem("s_uvrow2_ok")
        s_uvrow_ok = sem("s_uvrow_ok")
        s_uvt2_ps = sem("s_uvt2_ps")
        s_uvt_ps = sem("s_uvt_ps")
        s_var_ok = sem("s_var_ok")
        s_w1_in = sem("s_w1_in")
        s_w4_ok = sem("s_w4_ok")
        s_wa_ok = sem("s_wa_ok")
        s_wdiag_zero = sem("s_wdiag_zero")
        s_wg_in = sem("s_wg_in")
        s_wk_in = sem("s_wk_in")
        s_wl2_in = sem("s_wl2_in")
        s_wl3_in = sem("s_wl3_in")
        s_wm_in = sem("s_wm_in")
        s_wrep_ok = sem("s_wrep_ok")
        s_ws_ok = sem("s_ws_ok")
        s_wsp_in0 = sem("s_wsp_in0")
        s_wsp_in1 = sem("s_wsp_in1")
        s_x_in = sem("s_x_in")
        s_x_ok = sem("s_x_ok")
        s_xt1_cp = sem("s_xt1_cp")
        s_xt1_ps = sem("s_xt1_ps")
        s_xt2_cp = sem("s_xt2_cp")
        s_xt2_ps = sem("s_xt2_ps")
        s_xt3_cp = sem("s_xt3_cp")
        s_xt3_ps = sem("s_xt3_ps")
        s_xt_cp = sem("s_xt_cp")
        s_xt_ps = sem("s_xt_ps")
        s_xup_cp = sem("s_xup_cp")
        s_xup_out0 = sem("s_xup_out0")
        s_xup_out1 = sem("s_xup_out1")
        s_xup_ps = sem("s_xup_ps")
        s_y1_cp = sem("s_y1_cp")
        s_y1_ps = sem("s_y1_ps")
        s_y2_cp = sem("s_y2_cp")
        s_y3_cp = sem("s_y3_cp")
        s_y3_ps = sem("s_y3_ps")
        s_z_cp = sem("s_z_cp")
        s_z_ps = sem("s_z_ps")
        s_gath = [sem(f"s_gath{k}") for k in range(2 * GT)]
        block = ctx.enter_context(nc.Block())

        def kview(w):
            return w.rearrange("(k p) n -> p k n", p=128)

        def bass_row(v, p):
            return v.rearrange("(a n) -> a n", a=1).to_broadcast([p, v.shape[0]])

        @block.sync
        def _(sp):
            sp.dma_start(dsti, a["dst"].rearrange("(p e) -> p e", p=NP)).then_inc(s_dst_in, 16)
            sp.dma_start(srci, a["src"].rearrange("(p e) -> p e", p=NP)).then_inc(s_rec_in, 16)
            sp.dma_start(a4, a["edge_attr_4"].rearrange("(p e) k -> p e k", p=NP)).then_inc(s_rec_in, 16)
            sp.dma_start(a8, a["edge_attr_8"].rearrange("(p e) k -> p e k", p=NP)).then_inc(s_rec_in, 16)
            sp.wait_ge(s_empty_ok, 2)
            flat = recs.rearrange("(q p e) k -> q p (e k)", p=128, e=EMP)
            nq = (G + 2) * GS // (128 * EMP)
            for q in range(nq):
                sp.dma_start(flat[q], empty.rearrange("p e k -> p (e k)")).then_inc(s_recs_clear, 16)
            sp.dma_start(x_sb[:], a["x"].rearrange("(b p) n -> p b n", p=NP)).then_inc(s_x_in, 16)
            sp.dma_start(w_gat, kview(a["L0_gnn_W_gat"])).then_inc(s_wg_in, 16)
            sp.dma_start(att_b[:, 0, :], bass_row(a["L0_gnn_att_src"].rearrange("h c -> (h c)"), 128)).then_inc(s_wg_in, 16)
            sp.dma_start(att_b[:, 1, :], bass_row(a["L0_gnn_att_dst"].rearrange("h c -> (h c)"), 128)).then_inc(s_wg_in, 16)
            sp.dma_start(w_skip, kview(a["L0_gnn_W_skip"])).then_inc(s_wk_in, 16)
            sp.dma_start(b_skip_b, bass_row(a["L0_gnn_b_skip"], NP)).then_inc(s_wk_in, 16)
            sp.wait_ge(s_wdiag_zero, 1)
            for q in range(2):
                sp.dma_start(w_m1[q * 8:q * 8 + 8, q * HID:(q + 1) * HID], a["L1_gnn_W_mlp1"]).then_inc(s_wm_in, 16)
                sp.dma_start(w_m2[q * HID:(q + 1) * HID, q * HID:(q + 1) * HID], a["L1_gnn_W_mlp2"]).then_inc(s_wm_in, 16)
                sp.dma_start(w_m3[q * HID:(q + 1) * HID, q * HID:(q + 1) * HID], a["L1_gnn_W_mlp3"]).then_inc(s_wm_in, 16)
            for q, name in enumerate(("L0_gnn_gat_bias", "L0_gnn_bn_gamma", "L0_gnn_bn_beta")):
                sp.dma_start(bnp[:, q, :], a[name]).then_inc(s_bn_in, 16)
            sp.wait_ge(s_h_ps, NB)
            sp.wait_ge(s_wa_ok, 1)
            sp.dma_start(w_l2, kview(a["L2_gnn_W"])).then_inc(s_wl2_in, 16)
            av = a["L2_gnn_a"].rearrange("(q n) k -> q (n k)", q=2)
            for q in range(2):
                sp.dma_start(a_b[:, q, :], av[q:q + 1, :].to_broadcast([128, D])).then_inc(s_wl2_in, 16)
            sp.wait_ge(s_scattered0, 16 * SB * (ROUNDS // 2 + 1))
            sp.wait_ge(s_scattered1, 16 * SB * (ROUNDS // 2))
            sp.wait_ge(s_wa_ok, 2)
            sp.dma_start(rec_sb[:], recs.rearrange("(g p t) k -> p g (t k)", p=128, t=GT)).then_inc(s_recs_in, 16)

            sp.wait_ge(s_rows_cp, 3)
            sp.dma_start(as_rows, rows16).then_inc(s_rows_out, 16)
            sp.wait_ge(s_rows_out, 16)
            sp.wait_ge(s_max_stage, 1)
            with sp.Fori(0, H // 2) as i:
                for par in range(2):
                    sp.wait_ge(s_asb_free, i * 2 + (par + 1))
                    sp.dma_start(as_b[:, par, :], as_rows[bass.ds(i * 2 + par, 1), :].to_broadcast([NP, N]))\
                      .then_inc(s_asb_in0 if par == 0 else s_asb_in1, 16)
            sp.wait_ge(s_uvrow_ok, 1)
            sp.dma_start(uv_rows, uvrow_sb).then_inc(s_rows_out, 16)
            sp.wait_ge(s_rows_out, 32)
            sp.wait_ge(s_max_stage, 2)
            with sp.Fori(0, H // 2) as i:
                for par in range(2):
                    sp.wait_ge(s_uv_free, i * 2 + (par + 1))
                    for q in range(2):
                        sp.dma_start(UV[:, par, q, :], uv_rows[bass.ds(i * 2 + (par + q * H), 1), :].to_broadcast([NP, N]))\
                          .then_inc(s_uv_in0 if par == 0 else s_uv_in1, 16)

            sp.wait_ge(s_norm_ok, H // 2 + 1)
            sp.dma_start(w_up0, a["L1_gnn_W_up0"]).then_inc(s_w1_in, 16)
            sp.dma_start(w_up1, a["L1_gnn_W_up1"]).then_inc(s_w1_in, 16)
            sp.dma_start(w_m4[0:HID, :], a["L1_gnn_W_mlp4"]).then_inc(s_w1_in, 16)
            sp.dma_start(w_m4[HID:128, :], a["L1_gnn_W_mlp4"]).then_inc(s_w1_in, 16)
            sp.dma_start(w_o0, kview(a["L1_gnn_W_out0"])).then_inc(s_w1_in, 16)
            sp.dma_start(w_o1, kview(a["L1_gnn_W_out1"])).then_inc(s_w1_in, 16)
            for b in range(NB):
                sp.wait_ge(s_xup_cp, b + 1)
                sp.dma_start(xup[b * NP:(b + 1) * NP, :], xup_st[:, b % 2, :]).then_inc(s_xup_out0 if b % 2 == 0 else s_xup_out1, 16)
            def load_h3(pair, par):
                for q in range(2):
                    sp.dma_start(h3[q * HID:(q + 1) * HID, par, :],
                                 h3_rows[bass.ds(pair, 1), par * HID:(par + 1) * HID, :].rearrange("q p n -> (q p) n"))\
                      .then_inc(s_h3_in0 if par == 0 else s_h3_in1, 16)

            def load_recs(pair, par):
                sp.dma_start(gld[:, par, :], recs.rearrange("(i g p t) k -> i g p (t k)", g=2, p=128, t=GT)
                             [bass.ds(pair, 1), par, :, :].rearrange("i p k -> (i p) k"))\
                  .then_inc(s_gld_in0 if par == 0 else s_gld_in1, 16)
            for par in range(2):
                load_h3(0, par)
                load_recs(0, par)
            with sp.Fori(0, G // 2 - 1) as i:
                for par in range(2):
                    sp.wait_ge(s_h3_ok, i * 2 + (par + 1))
                    load_h3(i + 1, par)
                    sp.wait_ge(s_gidx_ok, i * 2 + (par + 1))
                    load_recs(i + 1, par)

            sp.wait_ge(s_uvrow2_ok, 1)
            sp.dma_start(uv2_rows, uvrow2).then_inc(s_rows2_out, 16)
            sp.wait_ge(s_rows2_out, 16)
            for q in range(2):
                sp.dma_start(UV2[:, q, :], uv2_rows[q:q + 1, :].to_broadcast([NP, N])).then_inc(s_uv2_in, 16)
            sp.wait_ge(s_p2_ok, NB)
            spl = a["spline_wT"].rearrange("q (k p) n -> q p k n", p=128)
            for half in range(2):
                sp.wait_ge(s_sp_free, 10 * half + 1)
                sp.dma_start(w_sp[:, 0, :].rearrange("p (k n) -> p k n", k=KT), kview(a["base_wT"])).then_inc(s_wsp_in0, 16)
                with sp.Fori(0, NSPL // 2) as i:
                    for par in range(2):
                        slot = 1 - par
                        sp.wait_ge(s_sp_free, i * 2 + (9 * half + par + 2))
                        sp.dma_start(w_sp[:, slot, :].rearrange("p (k n) -> p k n", k=KT),
                                     spl[bass.ds(i * 2 + par, 1), :, :, :].rearrange("q p k n -> (q p) k n"))\
                          .then_inc(s_wsp_in0 if slot == 0 else s_wsp_in1, 16)
            sp.wait_ge(s_silu_ok, 2)
            sp.wait_ge(s_sv_ok, 2 * NSPL)
            sp.dma_start(w_l3, kview(a["w_l3T"])).then_inc(s_wl3_in, 16)

            for b in range(NB):
                sp.wait_ge(s_x_ok, 3 * NB + b + 1)
                sp.dma_start(out[b * NP:(b + 1) * NP, :], x_sb[:, b, :]).then_inc(s_out_done, 16)
            sp.wait_ge(s_out_done, 16 * NB)

        @block.gpsimd
        def _(pool):
            pool.memset(upper[:], 1.0)
            pool.memset(ident[:], 0.0)
            pool.memset(ones[:], 1.0)
            pool.memset(epsc[:], EPS)
            pool.memset(w_m1[:], 0.0)
            pool.memset(w_m2[:], 0.0)
            pool.memset(w_m3[:], 0.0).then_inc(s_wdiag_zero, 1)
            pool.memset(gidx[:], 0).then_inc(s_const0, 1)
            pool.iota(gi, pattern=[[1, G + 2]], base=0, channel_multiplier=0)
            pool.iota(iota_src[:], pattern=[[1, N]], base=0, channel_multiplier=0, allow_small_or_imprecise_dtypes=True)
            pool.iota(iota_dst[:], pattern=[[1, NP]], base=0, channel_multiplier=0, allow_small_or_imprecise_dtypes=True)
            pool.iota(cen[:], pattern=[[1, NSPL]], base=0, channel_multiplier=0, allow_small_or_imprecise_dtypes=True)
            pool.wait_ge(s_const0, 1)
            pool.affine_select(out=upper[:], in_=upper[:], compare_op=ALU.is_gt, fill=0.0, base=0,
                               pattern=[[1, 128]], channel_multiplier=-1)
            pool.affine_select(out=ident[:], in_=ident[:], compare_op=ALU.not_equal, fill=1.0, base=0,
                               pattern=[[-1, 128]], channel_multiplier=1).then_inc(s_consts, 1)
            nq = (G + 2) * GS // (128 * EMP)
            pool.wait_ge(s_recs_clear, 16 * nq)
            pool.wait_ge(s_rec_ok, 1)

            def scatter_round(j, sl, n_staged, n_out):
                sent = s_scattered0 if sl == 0 else s_scattered1
                if n_out is not None:
                    pool.wait_ge(sent, n_out)
                    pool.nop(nofuse=True)
                pool.tensor_copy(stage_pos[:, sl, :], pos[:, bass.ds(j * SB, SB)])
                pool.tensor_copy(stage_rec[:, sl, :, :], rec[:, bass.ds(j * SB, SB), :]).then_inc(s_staged, 1)
                pool.wait_ge(s_staged, n_staged)
                pool.nop(nofuse=True)
                for k in range(SB):
                    pool.indirect_dma_start(out=recs, out_offset=bass.IndirectOffsetOnAxis(stage_pos[:, sl, k:k + 1], 0),
                                            in_=stage_rec[:, sl, k, :], in_offset=None).then_inc(sent, 16)
            scatter_round(0, 0, 1, None)
            scatter_round(1, 1, 2, None)
            scatter_round(2, 0, 3, 16 * SB)
            with pool.Fori(0, (ROUNDS - 3) // 2) as j:
                scatter_round(j * 2 + 3, 1, j * 2 + 4, j * (16 * SB) + 16 * SB)
                scatter_round(j * 2 + 4, 0, j * 2 + 5, j * (16 * SB) + 2 * 16 * SB)

            pool.wait_ge(s_recs_in, 16)
            with pool.Fori(0, G // 2) as i:
                for par in range(2):
                    pool.wait_ge(s_cnt_ps, i * 2 + (par + 1))
                    pool.tensor_copy(pslot[:, par, :], rec_sb[:, bass.ds(i * 2 + par, 1), :].rearrange("p a k -> p (a k)"))\
                        .then_inc(s_pslot_ok, 1)
                    pool.wait_ge(s_pslot_ok, i * 2 + (par + 1))
                    pool.nop(nofuse=True)
                    for k in range(GT - 1):
                        ins = pool.tensor_scalar(oh_dst[:, par * GT + k, 0:NP], iota_dst[:],
                                                 pslot[:, par, k * RW + R_DL:k * RW + R_DL + 1], None, ALU.is_equal)
                    ins.then_inc(s_ohd_ok, 1)
            with pool.Fori(0, G // 4) as i:
                for q in range(2):
                    pool.wait_ge(s_ft_ps, i * 2 + (q + 1))
                    for hf in range(2):
                        ins = pool.tensor_copy(fsl[:, q, :, hf * 8:hf * 8 + 8],
                                               rec_sb[:, bass.ds(i * 4 + (2 * q + hf), 1), :]
                                               .rearrange("p a (t k) -> p (a t) k", k=RW)[:, :, R_F:R_F + 8])
                    ins.then_inc(s_fs_ok, 1)
            pool.wait_ge(s_mlp_done, 1)
            pool.memset(hs[:, :, C:2 * C], 1.0)
            h5 = h_sb.rearrange("p b (h c) -> p b h c", h=H)
            for par in range(2):
                pool.tensor_copy(hs[:, :, par * 2 * C:par * 2 * C + C], h5[:, :, par, :]).then_inc(s_hs_ok, 1)

            def pool_head(h, par, fill, norm):
                for n, sblk in enumerate(POOL_P):
                    pool.wait_ge(s_e_ok, h * NB + (sblk + 1))
                    pool.nop(nofuse=True)
                    w = wt[:, sblk % WR, :]
                    pool.tensor_scalar(w, w, 1.0, None, ALU.min).then_inc(s_min_ok, 1)
                    pool.wait_ge(s_min_ok, h * len(POOL_P) + (n + 1))
                    pool.tensor_tensor(w, w, cnt_pool[n], ALU.mult).then_inc(s_pp_ok, 1)
                    if fill and n == 0:
                        pool.wait_ge(s_pv_done, h * NB + WR)
                        c0 = (1 - par) * 2 * C
                        pool.tensor_copy(hs[:, :, c0:c0 + C],
                                         h5[:, :, bass.ds(h + 1, 1), :].rearrange("p b h c -> p b (h c)")).then_inc(s_hs_ok, 1)
                if norm is not None:
                    normalise(norm)

            def normalise(i):
                pool.wait_ge(s_rrow_ok, i + 1)
                pool.nop(nofuse=True)
                o_i = OT[:, bass.ds(i, 1), :].rearrange("p a n -> p (a n)")
                nc.gpsimd.tensor_tensor(o_i, o_i, rrow, ALU.mult).then_inc(s_norm_ok, 1)
            pool_head(0, 0, False, None)
            with pool.Fori(0, H // 2 - 1) as i:
                pool_head(i * 2 + 1, 1, True, None)
                pool_head(i * 2 + 2, 0, True, i)
            pool_head(H - 1, 1, False, None)
            normalise(H // 2 - 1)

            for sl in range(2):
                pool.wait_ge(s_xup_out0 if sl == 0 else s_xup_out1, 16 * NB // 2)

            pool.wait_ge(s_acc_zero, 1)

            def gathers(par, n, n_in):
                pool.wait_ge(s_gld_in0 if par == 0 else s_gld_in1, n_in)
                pool.nop(nofuse=True)
                pool.tensor_copy(gidx[:, par, :], gld[:, par, :].bitcast(u32).rearrange("p (t k) -> p t k", k=RW)[:, :, R_SRCI])
                pool.tensor_copy(gslot[:, par, :], gld[:, par, :])\
                    .then_inc(s_gidx_ok, 1)
                pool.wait_ge(s_gidx_ok, n)
                pool.nop(nofuse=True)
                for k in range(GT):
                    pool.indirect_dma_start(out=ring[:, par * GT + k, :], out_offset=None, in_=xup,
                                            in_offset=bass.IndirectOffsetOnAxis(gidx[:, par, k:k + 1], 0))\
                        .then_inc(s_gath[par * GT + k], 16)

            def add_group(g, par):
                bv = pool.value_load(gblk[0:1, bass.ds(g, 1)], min_val=0, max_val=NB - 1)
                pool.wait_ge(s_gsum_ok, g + 3)
                pool.wait_ge(s_acc_free, g + 2)
                pool.nop(nofuse=True)
                d = acc[:, bass.ds(bv * 1024, 1024)]
                pool.tensor_tensor(d, gsum[:, par, :], d, ALU.add).then_inc(s_acc_free, 1)
            gathers(0, 1, 16)
            gathers(1, 2, 16)
            pool.wait_ge(s_prod_ok, 2 * GT)
            gathers(0, 3, 32)
            with pool.Fori(0, G // 2 - 2) as i:
                for par in range(2):
                    pool.wait_ge(s_prod_ok, i * 8 + GT * (par + 3))
                    gathers(1 - par, i * 2 + (4 + par), i * 16 + 16 * (2 + par))
                    add_group(i * 2 + par, par)
            pool.wait_ge(s_prod_ok, (G - 2) * GT + GT)
            gathers(1, G, 16 * (G // 2))
            for g in range(G - 4, G):
                add_group(g, g % 2)

            pool.wait_ge(s_sp_free, 2 + 2 * (NSPL + 1))
            for k in range(NB):
                pool.tensor_copy(cnt50[:, k, :], cnt_s[:, k, :]).then_inc(s_p3_ok, 1)

        @block.tensor
        def _(pe):
            t = nc.tensor

            def transposes(src, ready, done, copied, banks, copied0=0):
                for b in range(NB):
                    if ready is not None:
                        pe.wait_ge(*ready(b))
                    if b >= 2:
                        pe.wait_ge(copied, copied0 + b - 1)
                    for k in range(KT):
                        ins = t.transpose(PS[:, banks[b % 2], k * 128:k * 128 + NP], src(b, k), ident[:NP, :NP])
                    ins.then_inc(done, 1)

            def node_product(lhs, rhs, nk, done, copied, banks, cols=D):
                for b in range(NB):
                    if b >= 2:
                        pe.wait_ge(copied, b - 1)
                    for k in range(nk):
                        ins = t.matmul(PS[:NP, banks[b % 2], 0:cols], lhs(b, k), rhs(k), start=(k == 0), stop=(k == nk - 1))
                    ins.then_inc(done, 1)

            def blk_of(v):
                return lambda b, k: v[:, k, b * NP:(b + 1) * NP]

            def rows_product(w, nr, xt, done, b0):
                for q in range(3):
                    n0, n1 = q * 512, min(N, (q + 1) * 512)
                    for k in range(KT):
                        ins = t.matmul(PS[:nr, b0 + q, 0:n1 - n0], w[:, k, 0:nr], xt[:, k, n0:n1], start=(k == 0), stop=(k == KT - 1))
                    ins.then_inc(done, 1)

            def cols_product(w, nr, xt, done, bank):
                for b in range(NB):
                    for k in range(KT):
                        ins = t.matmul(PS[:NP, bank, b * nr:(b + 1) * nr], xt[:, k, b * NP:(b + 1) * NP], w[:, k, 0:nr],
                                       start=(k == 0), stop=(k == KT - 1))
                ins.then_inc(done, 1)

            def uv_transposes(src, nr, done, b0):
                for b in range(NB):
                    ins = t.transpose(PS[:nr, b0 + b // 4, (b % 4) * NP:(b % 4 + 1) * NP], src[:, b, 0:nr], ident[:NP, :NP])
                ins.then_inc(done, 1)

            pe.wait_ge(s_consts, 1)
            pe.wait_ge(s_tot_ok, 1)
            t.matmul(PS[:NP, 5, 0:NB], upper[:NP, :NP], tot, start=True, stop=True)
            t.matmul(PS[:, 5, 16:16 + NB], ones[:NP, 0:128], tot, start=True, stop=True).then_inc(s_prefix_ps, 1)
            pe.wait_ge(s_x_in, 16)
            transposes(lambda b, k: x_sb[:, b, k * 128:(k + 1) * 128], None, s_xt_ps, s_xt_cp, (6, 7))
            pe.wait_ge(s_wg_in, 48)
            pe.wait_ge(s_xt_cp, NB)
            node_product(blk_of(xT), lambda k: w_gat[:, k, :], KT, s_h_ps, s_h_cp, (6, 7))
            pe.wait_ge(s_wa_ok, 1)
            rows_product(wa, 2 * H, xT, s_rows_ps, 0)
            cols_product(wa, 2 * H, xT, s_cols_ps, 3)
            pe.wait_ge(s_wk_in, 32)
            pe.wait_ge(s_h_cp, NB)
            node_product(blk_of(xT), lambda k: w_skip[:, k, :], KT, s_skip_ps, s_skip_cp, (6, 7))
            pe.wait_ge(s_rows_cp, 3)
            pe.wait_ge(s_cols_cp, 1)
            pe.wait_ge(s_prefix_cp, 1)

            with pe.Fori(0, G // 2) as i:
                for par in range(2):
                    pe.wait_ge(s_oh_ok, i * 2 + (par + 1))
                    pe.wait_ge(s_ohd_ok, i * 2 + (par + 1))
                    pe.wait_ge(s_oha_ok, i * 2 + (par + 1))
                    pe.wait_ge(s_cnt_left, i * 2 + (par + 1))
                    for k in range(GT):
                        for q in range(3):
                            n0, n1 = q * 512, min(N, (q + 1) * 512)
                            ins = t.matmul(PS[:NP, 3 * par + q, 0:n1 - n0], oh_dst[:, par * GT + k, 0:NP],
                                           oh_src[:, par * GT + k, n0:n1], start=(k == 0), stop=(k == GT - 1))
                    ins.then_inc(s_cnt_ps, 1)
            pe.wait_ge(s_cnt_flushed, G + 2)
            for b in range(NB):
                pe.wait_ge(s_cntf_ok, b + 1)
                if b >= 2:
                    pe.wait_ge(s_cnts_cp, b - 1)
                for j in range(NB):
                    ins = t.transpose(PS[:NP, 3 * (b % 2) + j // 4, (j % 4) * NP:(j % 4 + 1) * NP],
                                      cnt_f[:, b % 2, j * NP:(j + 1) * NP], ident[:NP, :NP])
                ins.then_inc(s_cntt_ps, 1)
            pe.wait_ge(s_cnts_cp, NB)
            pe.wait_ge(s_wm_in, 16 * 6)
            def feat_transposes(n):
                for q in range(2):
                    pe.wait_ge(s_fs_ok, n + (q + 1))
                    for k in range(GT):
                        ins = t.transpose(PS[:16, 6 + q, k * 128:(k + 1) * 128], fsl[:, q, k, :], ident[:])
                    ins.then_inc(s_ft_ps, 1)

            def edge_layer(l, w, n, n3):
                for q in range(2):
                    if l == 0:
                        pe.wait_ge(s_ft_cp, n + (q + 1))
                    else:
                        pe.wait_ge(s_hid_ok, n3 + (2 * (l - 1) + q + 1))
                    t.matmul(PS[:, 4 + q, :], w[:], fT[:, q, :] if l == 0 else hid[:, q, l - 1, :], start=True, stop=True)\
                        .then_inc(s_mlp_ps, 1)

            def edge_layers(n, n3, ahead):
                edge_layer(0, w_m1, n, n3)
                edge_layer(1, w_m2, n, n3)
                if ahead:
                    feat_transposes(n + 2)
                edge_layer(2, w_m3, n, n3)
                for q in range(2):
                    pe.wait_ge(s_hid_ok, n3 + (4 + q + 1))
            feat_transposes(0)
            with pe.Fori(0, G // 4 - 1) as i:
                edge_layers(i * 2, i * 6, True)
            edge_layers(G // 2 - 2, (G // 2 - 2) * 3, False)
            pe.wait_ge(s_uv_ok, 1)
            uv_transposes(uv, 2 * H, s_uvt_ps, 0)
            pe.wait_ge(s_uvrow_ok, 1)
            with pe.Fori(0, H // 2) as i:
                for par in range(2):
                    pe.wait_ge(s_hs_ok, i * 2 + (par + 1))
                    pe.wait_ge(s_head_free, i * 2 + (par + 1))
                    for sblk in range(NB):
                        if sblk in POOL_P:
                            n_p = len(POOL_P)
                            pe.wait_ge(s_pp_ok, i * (2 * n_p) + (par * n_p + POOL_P.index(sblk) + 1))
                        else:
                            n_p = NB - len(POOL_P)
                            pe.wait_ge(s_p_ok, i * (2 * n_p) + (par * n_p + len([b for b in range(sblk) if b not in POOL_P]) + 1))
                        for q in range(3):
                            n0, n1 = q * 512, min(N, (q + 1) * 512)
                            ins = t.matmul(PS[:, 3 * par + q, 0:n1 - n0], hs[:, sblk, par * C:par * C + 2 * C],
                                           wt[:, sblk % WR, n0:n1], start=(sblk == 0), stop=(sblk == NB - 1))
                        ins.then_inc(s_pv_done, 1)
            def back(b):
                if b >= 2:
                    pe.wait_ge(s_o_cp, b - 1)
                for k in range(KT):
                    ins = t.transpose(PS[:NP, 6 + b % 2, k * 128:(k + 1) * 128], OT[:, k, b * NP:(b + 1) * NP], ident[:])
                ins.then_inc(s_o_ps, 1)

            def x1_transposes(b):
                pe.wait_ge(s_x_ok, b + 1)
                if b >= 2:
                    pe.wait_ge(s_xt1_cp, b - 1)
                for k in range(4):
                    src = x_sb[:, b, 0:MUL] if k == 0 else x_sb[:, b, MUL + k - 1:D:3]
                    ins = t.transpose(PS[:, 4 + b % 2, k * 128:k * 128 + NP], src, ident[:NP, :NP])
                ins.then_inc(s_xt1_ps, 1)
            def linear_up(b):
                pe.wait_ge(s_xt1_cp, b + 1)
                if b == 0:
                    pe.wait_ge(s_w1_in, 16 * 6)
                if b >= 2:
                    pe.wait_ge(s_xup_cp, b - 1)
                for k in range(4):
                    ins = t.matmul(PS[:NP, 2 + b % 2, k * MUL:(k + 1) * MUL], xT1[:, k, b * NP:(b + 1) * NP],
                                   w_up0 if k == 0 else w_up1, start=True, stop=True)
                ins.then_inc(s_xup_ps, 1)
            pe.wait_ge(s_gelu_ok, 1)
            for b in range(NB + 3):
                if b < NB:
                    back(b)
                if 2 <= b < NB + 2:
                    x1_transposes(b - 2)
                if b >= 3:
                    linear_up(b - 3)

            pe.wait_ge(s_xup_cp, NB)

            tpw_bank = (0, 1, 6, 7)

            def tpw(k, par):
                cols = slice(k * 128, (k + 1) * 128)
                t.matmul(PS[:, tpw_bank[k], :], h3r[:, par, cols], w4r[:, 0, :], start=True, stop=False)
                t.matmul(PS[:, tpw_bank[k], :], h3r[0:HID, par, cols], w4r[0:HID, 1, :], start=False, stop=True).then_inc(s_tpw_ps, 1)

            def scat(par, k):
                for q in range(2):
                    ins = t.matmul(PS[:NP, 2 + 2 * par + q, :], sel[:, par * GT + k, :], prod[:, k, q * 512:(q + 1) * 512],
                                   start=(k == 0), stop=(k == GT - 1))
                ins.then_inc(s_scat_done, 1)
            pe.wait_ge(s_w4_ok, 2)
            pe.wait_ge(s_h3_ok, 1)
            for k in range(GT - 1):
                tpw(k, 0)
            with pe.Fori(0, G // 2) as i:
                for par in range(2):
                    pe.wait_ge(s_gsum_ok, i * 2 + (par + 1))
                    for k in range(GT):
                        if k == 1:
                            pe.wait_ge(s_h3_ok, i * 2 + (par + 2))
                        tpw((k + GT - 1) % GT, par if k == 0 else 1 - par)
                        pe.wait_ge(s_prod_ok, i * 8 + (4 * par + k + 1 + GT))
                        scat(par, k)
            pe.wait_ge(s_acc_done, 1)

            def x2_transposes(b):
                pe.wait_ge(s_x_ok, NB + b + 1)
                if b >= 2:
                    pe.wait_ge(s_xt2_cp, b - 1)
                for k in range(KT):
                    ins = t.transpose(PS[:, 6 + b % 2, k * 128:k * 128 + NP], x_sb[:, b, k * 128:(k + 1) * 128], ident[:NP, :NP])
                ins.then_inc(s_xt2_ps, 1)

            def msg_transposes(b):
                if b >= 2:
                    pe.wait_ge(s_mt_cp, 2 * (b - 1))
                for c in range(8):
                    ins = t.transpose(PS[:, 2 * (b % 2) + c // 4, (c % 4) * 128:(c % 4) * 128 + NP],
                                      acc[:, b * 1024 + c * 128:b * 1024 + (c + 1) * 128], ident[:NP, :NP])
                    if c % 4 == 3:
                        ins.then_inc(s_mt_ps, 1)
            msg_transposes(0)
            for b in range(NB):
                if b + 1 < NB:
                    msg_transposes(b + 1)
                pe.wait_ge(s_mt_cp, 2 * (b + 1))
                if b >= 2:
                    pe.wait_ge(s_y1_cp, b - 1)
                for q in range(4):
                    pair = ((0, w_o0[:, 0, :]), (7, w_o0[:, 1, :])) if q == 0 else \
                           ((q, w_o1[:, 0, :]), (3 + q, w_o1[:, 1, :]))
                    for n, (c, w) in enumerate(pair):
                        ins = t.matmul(PS[:NP, 4 + b % 2, q * MUL:(q + 1) * MUL], msgT[:, b % 2, c * NP:(c + 1) * NP], w,
                                       start=(n == 0), stop=(n == 1))
                ins.then_inc(s_y1_ps, 1)
                if b >= 2:
                    x2_transposes(b - 2)

            for b in range(NB - 2, NB):
                x2_transposes(b)
            pe.wait_ge(s_xt2_cp, NB)
            pe.wait_ge(s_wrep_ok, 1)
            rows_product(w_rep, NP, xT2, s_st_ps, 0)
            cols_product(wa2, 2, xT2, s_cols2_ps, 3)
            pe.wait_ge(s_uv2_ok, 1)
            pe.wait_ge(s_st_ok, 3)
            uv_transposes(uv, 2, s_uvt2_ps, 0)
            pe.wait_ge(s_uvrow2_ok, 1)

            def agg_part(w, b0, k):
                for q in range(3):
                    n0, n1 = q * 512, min(N, (q + 1) * 512)
                    ins = t.matmul(PS[:, b0 + q, 0:n1 - n0], w, P50[:, k, n0:n1], start=(k == 0), stop=(k == NB - 1))
                return ins

            def x_feat(k, f):
                return x_sb[:, k, f * 128:(f + 1) * 128]
            for k in range(NB):
                pe.wait_ge(s_p2_ok, k + 1)
                for f in range(2):
                    ins = agg_part(x_feat(k, f), 3 * f, k)
                    if k == NB - 1:
                        ins.then_inc(s_l2_agg, 1)
            for n, (b0, f) in enumerate(((0, 2), (3, None), (0, 3))):
                pe.wait_ge(s_l2_cp, n + 1)
                for k in range(NB):
                    ins = agg_part(ones[:NP, 0:128] if f is None else x_feat(k, f), b0, k)
                ins.then_inc(s_l2_agg, 1)

            def spline_step(slot, first, last):
                for b in range(HB):
                    for k in range(KT):
                        ins = t.matmul(PS[:NP, b, :], basis[:, slot, (k * HB + b) * NP:(k * HB + b + 1) * NP],
                                       w_sp[:, slot, k * D:(k + 1) * D], start=(first and k == 0), stop=(last and k == KT - 1),
                                       skip_group_check=True)
                ins.then_inc(s_sp_free, 1)
            for half in range(2):
                if half:
                    pe.wait_ge(s_y2_cp, HB)
                pe.wait_ge(s_wsp_in0, 16 * (5 * half + 1))
                pe.wait_ge(s_silu_ok, half + 1)
                spline_step(0, True, False)
                with pe.Fori(0, NSPL // 2) as i:
                    for par in range(2):
                        slot = 1 - par
                        if slot == 0:
                            pe.wait_ge(s_wsp_in0, i * 16 + 16 * (5 * half + 2))
                        else:
                            pe.wait_ge(s_wsp_in1, i * 16 + 16 * (4 * half + 1))
                        pe.wait_ge(s_basis_ok, i * 2 + (8 * half + par + 1))
                        spline_step(slot, False, False)
            for b in range(NB + 1):
                if b < NB:
                    pe.wait_ge(s_x_ok, 2 * NB + b + 1)
                    if b >= 1:
                        pe.wait_ge(s_xt3_cp, b)
                    for k in range(KT):
                        ins = t.transpose(PS[:, 7, k * 128:k * 128 + NP], x_sb[:, b, k * 128:(k + 1) * 128], ident[:NP, :NP])
                    ins.then_inc(s_xt3_ps, 1)
                if b >= 1:
                    c = b - 1
                    pe.wait_ge(s_xt3_cp, c + 1)
                    if c == 0:
                        pe.wait_ge(s_wl3_in, 16)
                    if c >= 2:
                        pe.wait_ge(s_z_cp, c - 1)
                    for k in range(KT):
                        ins = t.matmul(PS[:NP, 5 + c % 2, :], xT3[:, k, c * NP:(c + 1) * NP], w_l3[:, KT + k, :],
                                       start=(k == 0), stop=(k == KT - 1))
                    ins.then_inc(s_z_ps, 1)
            pe.wait_ge(s_z_cp, NB)
            for b in range(NB):
                if b >= 2:
                    pe.wait_ge(s_y3_cp, b - 1)
                for k in range(KT):
                    t.matmul(PS[:NP, 4 + b % 2, :], xT3[:, k, b * NP:(b + 1) * NP], w_l3[:, k, :], start=(k == 0), stop=(k == KT - 1))
                for k in range(NB):
                    if b == 0:
                        pe.wait_ge(s_p3_ok, k + 1)
                    ins = t.matmul(PS[:NP, b % 2, :], cnt50[:, k, b * NP:(b + 1) * NP], z_sb[:, k, :],
                                   start=(k == 0), stop=(k == NB - 1))
                ins.then_inc(s_y3_ps, 1)

        @block.scalar
        def _(act):
            A = nc.scalar.activation

            def ln_sqrt(layer, b):
                act.wait_ge(s_ln_var, (layer - 1) * NB + b + 1)
                A(rstd[:, b:b + 1], mv[:, b, 1:2], ACT.Sqrt, bias=epsc[:NP, :]).then_inc(s_ln_sd, 1)

            def evac_T(dst, done, copied, banks, layer=0, then=None):
                if layer:
                    ln_sqrt(layer, 0)
                for b in range(NB):
                    if layer and b + 1 < NB:
                        ln_sqrt(layer, b + 1)
                    act.wait_ge(done, b + 1)
                    A(dst[:, :, b * NP:(b + 1) * NP],
                      PS[:, banks[b % 2], :].rearrange("p (k n) -> p k n", k=KT)[:, :, 0:NP], ACT.Copy).then_inc(copied, 1)
                    if then and b >= 1:
                        then(b - 1)
                if then:
                    then(NB - 1)

            def evac_rows(dst, nr, done, copied, b0):
                for q in range(3):
                    n0, n1 = q * 512, min(N, (q + 1) * 512)
                    act.wait_ge(done, q + 1)
                    A(dst[:, n0:n1], PS[:nr, b0 + q, 0:n1 - n0], ACT.Copy).then_inc(copied, 1)

            def evac_uv(dst, nr, b0, ok, done):
                act.wait_ge(done, 1)
                for q in range(3):
                    n0, n1 = q * 4 * NP, min(N, (q + 1) * 4 * NP)
                    ins = A(dst[:, n0:n1], PS[:nr, b0 + q, 0:n1 - n0], ACT.Copy)
                ins.then_inc(ok, 1)

            evac_T(xT, s_xt_ps, s_xt_cp, (6, 7))
            for b in range(NB):
                act.wait_ge(s_h_ps, b + 1)
                A(h_sb[:, b, :], PS[:NP, 6 + b % 2, :], ACT.Copy).then_inc(s_h_cp, 1)
            evac_rows(rows16, 2 * H, s_rows_ps, s_rows_cp, 0)
            act.wait_ge(s_cols_ps, 1)
            A(sc[:].rearrange("p b n -> p (b n)"), PS[:NP, 3, 0:NB * 2 * H], ACT.Copy).then_inc(s_cols_cp, 1)
            def last_onehot(par, n, n3):
                act.wait_ge(s_pslot_ok, n)
                A(nslot[:, par:par + 1], pslot[:, par, 3 * RW + R_DL:3 * RW + R_DL + 1], ACT.Copy, scale=-1.0).then_inc(s_nslot_ok, 1)
                act.wait_ge(s_nslot_ok, n3 + 1)
                A(ohtmp[:], iota_dst[:], ACT.Abs, bias=nslot[:, par:par + 1]).then_inc(s_nslot_ok, 1)
                act.wait_ge(s_nslot_ok, n3 + 2)
                A(oh_dst[:, par * GT + GT - 1, 0:NP], ohtmp[:], ACT.Relu, scale=-1.0, bias=1.0).then_inc(s_oha_ok, 1)
                act.wait_ge(s_oha_ok, n)

            def counts_out(par, n):
                act.wait_ge(s_cnt_ps, n + 2)
                act.wait_ge(s_cnt_flushed, n)
                psv = PS[:NP, 3 * par:3 * par + 3, :].rearrange("p a n -> p (a n)")[:, 0:N]
                A(cnt_ev[:, par, :], psv, ACT.Copy).then_inc(s_cnt_left, 1)
            last_onehot(0, 1, 0)
            last_onehot(1, 2, 2)
            with act.Fori(0, G // 2 - 1) as i:
                for par in range(2):
                    counts_out(par, i * 2 + (par + 1))
                    last_onehot(par, i * 2 + (par + 3), i * 4 + (2 * par + 4))
            counts_out(0, G - 1)
            counts_out(1, G)
            act.wait_ge(s_rows_out, 16)
            for b in range(NB):
                act.wait_ge(s_cntt_ps, b + 1)
                for q in range(3):
                    j0, j1 = 4 * q, min(NB, 4 * q + 4)
                    ins = A(cnt_s[:, j0:j1, b * NP:(b + 1) * NP],
                            PS[:NP, 3 * (b % 2) + q, 0:(j1 - j0) * NP].rearrange("p (j n) -> p j n", n=NP), ACT.Copy)
                ins.then_inc(s_cnts_cp, 1)
            sc0 = 8.0 ** -0.5
            sc1 = SILU2 * float(HID) ** -0.5
            def feat_in(n):
                for q in range(2):
                    act.wait_ge(s_ft_ps, n + (q + 3))
                    A(fT[:, q, :], PS[:16, 6 + q, :], ACT.Copy).then_inc(s_ft_cp, 1)

            def edge_silu(n, n3, n8, ahead):
                for l in range(3):
                    if l == 2 and ahead:
                        feat_in(n + 2)
                    for q in range(2):
                        act.wait_ge(s_mlp_ps, n3 + (2 * l + q + 1))
                        if l == 2:
                            act.wait_ge(s_h3_out0 if q == 0 else s_h3_out1, n8 + 16)
                        A(hid[:, q, l, :], PS[:, 4 + q, :], ACT.Silu, scale=sc0 if l == 0 else sc1).then_inc(s_hid_ok, 1)
                for q in range(2):
                    act.wait_ge(s_hid_ok, n3 + (4 + q + 1))
                    act.dma_start(h3_rows[bass.ds(n + q, 1), :, :].rearrange("q p n -> (q p) n"), hid[:, q, 2, :])\
                       .then_inc(s_h3_out0 if q == 0 else s_h3_out1, 16)
            feat_in(0)
            with act.Fori(0, G // 4 - 1) as i:
                edge_silu(i * 2, i * 6, i * 16, True)
            edge_silu(G // 2 - 2, (G // 2 - 2) * 3, 16 * (G // 4 - 1), False)
            act.wait_ge(s_h3_out0, 16 * (G // 4 + 1))
            act.wait_ge(s_h3_out1, 16 * (G // 4 + 1))
            act.sem_inc(s_mlp_done, 2)
            evac_uv(uvrow_sb, 2 * H, 0, s_uvrow_ok, s_uvt_ps)
            def evac_head(h, i, par):
                act.wait_ge(s_pv_done, h * NB + (NB + WR))
                num, den = par * C, C - par * C
                pv = PS[:, 3 * par:3 * par + 3, :].rearrange("p a n -> p (a n)")[:, 0:N]
                if par == 0:
                    act.wait_ge(s_norm_ok, i + 1)
                A(rrow[num:num + C, :], pv[den:den + C, :], ACT.Copy)
                A(OT[num:num + C, bass.ds(i, 1), :].rearrange("p a n -> p (a n)"), pv[num:num + C, :], ACT.Copy)\
                    .then_inc(s_head_free, 1)

            def act_head(h, par, before):
                for sblk in range(NB):
                    act.wait_ge(s_t_ok, h * NB + (sblk + 1))
                    A(wt[:, sblk % WR, :], wt[:, sblk % WR, :], ACT.Exp, bias=c2[:, par, sblk:sblk + 1]).then_inc(s_e_ok, 1)
                    if sblk == 2 and before is not None:
                        evac_head(*before)
            act_head(0, 0, None)
            with act.Fori(0, H // 2 - 1) as i:
                act_head(i * 2 + 1, 1, (i * 2, i, 0))
                act_head(i * 2 + 2, 0, (i * 2 + 1, i, 1))
            act_head(H - 1, 1, (H - 2, H // 2 - 1, 0))
            evac_head(H - 1, H // 2 - 1, 1)
            act.wait_ge(s_var_ok, 1)
            A(scl1[:], mv1[:, :, 1], ACT.Sqrt, bias=epsc[:, :]).then_inc(s_bnsd_ok, 1)
            act.wait_ge(s_bn_ok, 1)
            for k in range(KT):
                ins = A(OT[:, k, :], OT[:, k, :], ACT.Gelu, scale=scl1[:, k:k + 1], bias=shf1[:, k:k + 1])
            ins.then_inc(s_gelu_ok, 1)

            def xup_out(b):
                act.wait_ge(s_xup_ps, b + 1)
                if b >= 2:
                    act.wait_ge(s_xup_out0 if b % 2 == 0 else s_xup_out1, 16 * (b // 2))
                A(xup_st[:, b % 2, :], PS[:NP, 2 + b % 2, :], ACT.Copy, scale=float(MUL) ** -0.5).then_inc(s_xup_cp, 1)
            evac_T(xT1, s_xt1_ps, s_xt1_cp, (4, 5), 1, xup_out)

            def round_hidden(par, n):
                act.wait_ge(s_h3_in0 if par == 0 else s_h3_in1, n)
                A(h3r[:, par, :], h3[:, par, :], ACT.Copy).then_inc(s_h3hi_ok, 1)

            def scale_weights(i, par):
                act.wait_ge(s_gidx_ok, i * 2 + (par + 1))
                for k in range(GT):
                    act.wait_ge(s_gath[par * GT + k], i * 16 + 16)
                    act.wait_ge(s_prod_ok, i * 8 + (4 * par + k + 1))
                    y = gslot[:, par, k * RW + R_Y:k * RW + R_Y + 4]
                    A(qa[:, k, :], ring[:, par * GT + k, MUL:2 * MUL], ACT.Copy, scale=y[:, 1:2])
                    act.wait_ge(s_tpw_ps, i * 8 + (4 * par + k + 1))
                    w = PS[:, (0, 1, 6, 7)[k], :].rearrange("p (q n) -> p q n", q=4)
                    wk = ws[:, k, :].rearrange("p (q n) -> p q n", q=5)
                    A(wk[:, 0:5:4, :], w[:, 0:2, :], ACT.Copy, scale=y[:, 0:1])
                    for m in range(3):
                        ins = A(wk[:, 1 + m, :], w[:, 2, :], ACT.Copy, scale=y[:, 1 + m:2 + m])
                    ins.then_inc(s_ws_ok, 1)
            def sums_out(g, par):
                act.wait_ge(s_scat_done, g * GT + 2 * GT)
                act.wait_ge(s_acc_free, g + 1)
                A(gsum[:, par, :], PS[:NP, 2 + 2 * par:4 + 2 * par, :].rearrange("p a n -> p (a n)"), ACT.Copy)\
                    .then_inc(s_gsum_ok, 1)
            for par in range(2):
                round_hidden(par, 32)
            scale_weights(0, 0)
            with act.Fori(0, G // 2 - 1) as i:
                round_hidden(0, i * 32 + 64)
                scale_weights(i, 1)
                sums_out(i * 2, 0)
                round_hidden(1, i * 32 + 64)
                scale_weights(i + 1, 0)
                sums_out(i * 2 + 1, 1)
            scale_weights(G // 2 - 1, 1)
            sums_out(G - 2, 0)
            sums_out(G - 1, 1)

            def x2_in(b):
                act.wait_ge(s_xt2_ps, b + 1)
                A(xT2[:, :, b * NP:(b + 1) * NP],
                  PS[:, 6 + b % 2, :].rearrange("p (k n) -> p k n", k=KT)[:, :, 0:NP], ACT.Copy).then_inc(s_xt2_cp, 1)

            for b in range(NB):
                for q in range(2):
                    act.wait_ge(s_mt_ps, 2 * b + q + 1)
                    if b >= 2 and q == 0:
                        act.wait_ge(s_y1_ps, b - 1)
                    v = PS[:, 2 * (b % 2) + q, :].rearrange("p (k n) -> p k n", k=4)[:, :, 0:NP]
                    dstv = msgT[:, b % 2, q * 4 * NP:(q + 1) * 4 * NP].rearrange("p (k n) -> p k n", k=4)
                    if q == 0:
                        ins = A(dstv, v, ACT.Copy)
                    else:
                        A(dstv[:, 0:3, :], v[:, 0:3, :], ACT.Copy)
                        ins = A(dstv[:, 3, :], v[:, 3, :], ACT.Copy, scale=3.0 ** -0.5)
                    ins.then_inc(s_mt_cp, 1)
                if b >= 1:
                    ln_sqrt(2, b - 1)
                if b >= 3:
                    x2_in(b - 3)
            ln_sqrt(2, NB - 1)
            for b in range(NB - 3, NB):
                x2_in(b)

            evac_rows(st_b, NP, s_st_ps, s_st_ok, 0)
            act.wait_ge(s_cols2_ps, 1)
            A(sc[:, :, 0:2], PS[:NP, 3, 0:NB * 2].rearrange("p (b n) -> p b n", n=2), ACT.Copy).then_inc(s_cols2_cp, 1)
            evac_uv(uvrow2, 2, 0, s_uvrow2_ok, s_uvt2_ps)
            for k in range(NB):
                act.wait_ge(s_t2_ok, k + 1)
                if k >= 2:
                    act.wait_ge(s_p2_ok, k - 1)
                A(e2[:, k % 2, :], t2[:, k % 2, :], ACT.Exp, bias=c2[:, 0, k:k + 1]).then_inc(s_e2_ok, 1)
            for n, (b0, f) in enumerate(((0, 0), (3, 1), (0, 2), (0, 3))):
                act.wait_ge(s_l2_agg, n + 1 if f < 3 else 5)
                A(aggr[:, f, :], PS[:, b0:b0 + 3, :].rearrange("p a n -> p (a n)")[:, 0:N], ACT.Copy).then_inc(s_l2_cp, 1)

            HW = HB * NP
            for half in range(2):
                av = aggT[:, :, half * HW:(half + 1) * HW]

                def as3(v):
                    return v.rearrange("p (k n) -> p k n", k=KT)
                act.wait_ge(s_aggT_ok, half + 1)
                act.wait_ge(s_sp_free, 10 * half + 1)
                A(as3(basis[:, 0, :]), av, ACT.Silu).then_inc(s_silu_ok, 1)
                with act.Fori(0, NSPL // 2) as i:
                    for par in range(2):
                        act.wait_ge(s_cslot_ok, i * 2 + (8 * half + par + 1))
                        A(as3(sv), av, ACT.Abs, scale=KAPPA / STEP, bias=cslot[:, par:par + 1]).then_inc(s_sv_ok, 1)
                        act.wait_ge(s_sa_ok, i * 4 + (16 * half + 2 * par + 1))
                        A(sa2, sa, ACT.Square).then_inc(s_sq2_ok, 1)
                        act.wait_ge(s_sa_ok, i * 4 + (16 * half + 2 * par + 2))
                        A(sb2, sbb, ACT.Square).then_inc(s_sq2_ok, 1)
            def z_out(b):
                act.wait_ge(s_z_ps, b + 1)
                A(z_sb[:, b, :], PS[:NP, 5 + b % 2, :], ACT.Copy).then_inc(s_z_cp, 1)
            evac_T(xT3, s_xt3_ps, s_xt3_cp, (7, 7), 3, z_out)
            for b in range(NB):
                ln_sqrt(4, b)

        @block.vector
        def _(dve):
            v = nc.vector
            ch = Chain(dve, s_dve_chain)
            link = ch.link

            v.memset(empty, 0.0).then_inc(s_empty_ok, 1)
            dve.wait_ge(s_empty_ok, 1)
            v.memset(empty[:, :, 0:1], -1.0).then_inc(s_empty_ok, 1)
            v.memset(blk, 0.0)
            dve.wait_ge(s_dst_in, 16)
            link(v.tensor_copy(dstf, dsti))
            for b in range(1, NB):
                link(v.scalar_tensor_tensor(blk, dstf, float(b * NP), blk, ALU.is_ge, ALU.add))
            dve.wait_ge(s_consts, 1)
            for b in range(NB):
                ins = v.tensor_scalar(mask[:, b, :], blk, float(b), None, ALU.is_equal)
            link(ins)
            for b in range(NB):
                ins = v.tensor_tensor_scan(cum[:, b, :], ones[:NP, 0:EC], mask[:, b, :], 0.0, ALU.mult, ALU.add)
            link(ins)
            v.tensor_copy(tot, cum[:, :, EC - 1]).then_inc(s_tot_ok, 1)
            dve.wait_ge(s_rec_in, 48)
            v.scalar_tensor_tensor(rec[:, :, R_DL], blk, float(-NP), dstf, ALU.mult, ALU.add)
            v.tensor_copy(rec[:, :, R_SRCF], srci)
            v.tensor_copy(rec[:, :, R_SRCI].bitcast(i32), srci)
            v.memset(rec[:, :, 3], 0.0)
            v.tensor_copy(rec[:, :, R_Y:R_Y + 4], a4)
            v.tensor_copy(rec[:, :, R_F:R_F + 8], a8)
            dve.wait_ge(s_prefix_ps, 1)
            link(v.tensor_scalar(ngi, PS[:, 5, 16:16 + NB], float(GS - 1), None, ALU.add))
            link(v.tensor_scalar(ngi, ngi, GS.bit_length() - 1, None, ALU.arith_shift_right))
            link(v.tensor_copy(ngf, ngi))
            link(v.tensor_tensor_scan(gend, ones[:, :NB], ngf, 0.0, ALU.mult, ALU.add))
            link(v.tensor_tensor(gbase, gend, ngf, ALU.subtract))
            link(v.tensor_scalar(ngf, gbase, float(GS), -1.0, ALU.mult, ALU.add))
            ins = v.tensor_tensor(base, PS[:NP, 5, 0:NB], ngf[:NP], ALU.add)
            ins.then_inc(s_prefix_cp, 1)
            dve.wait_ge(s_prefix_cp, 1)
            for b in range(NB):
                ins = v.scalar_tensor_tensor(cum[:, b, :], cum[:, b, :], base[:, b:b + 1], mask[:, b, :], ALU.add, ALU.mult)
            link(ins)
            link(v.tensor_reduce(posf, cum.rearrange("p b e -> p e b"), X, ALU.add))
            v.tensor_copy(pos, posf).then_inc(s_rec_ok, 1)
            v.memset(gbf, 0.0)
            link(v.tensor_copy(gf, gi))
            for b in range(1, NB):
                link(v.scalar_tensor_tensor(gbf, gf, gbase[0:1, b:b + 1], gbf, ALU.is_ge, ALU.add))
            link(v.tensor_copy(gblk[:], gbf))

            dve.wait_ge(s_wg_in, 48)
            ptmp = at(12512, [128, 488])
            for k in range(KT):
                for q in range(2):
                    for hh in range(2):
                        c0 = hh * 256
                        link(v.tensor_tensor(ptmp[:, 0:256], w_gat[:, k, c0:c0 + 256], att_b[:, q, c0:c0 + 256], ALU.mult))
                        link(v.tensor_reduce(wa[:, k, q * H + hh * 4:q * H + hh * 4 + 4],
                                             ptmp[:, 0:256].rearrange("p (h c) -> p h c", h=4), X, ALU.add))
            dve.sem_inc(s_wa_ok, 1)
            dve.wait_ge(s_wk_in, 32)
            for b in range(NB):
                dve.wait_ge(s_skip_ps, b + 1)
                ins = v.tensor_tensor(x_sb[:, b, :], x_sb[:, b, :], PS[:NP, 6 + b % 2, :], ALU.add)
                ins.then_inc(s_skip_cp, 1)
                dve.wait_ge(s_skip_cp, b + 1)
                v.tensor_tensor(x_sb[:, b, :], x_sb[:, b, :], b_skip_b, ALU.add)

            dve.wait_ge(s_wl2_in, 48)
            for k in range(KT):
                for q in range(2):
                    link(v.tensor_tensor(tmp2, w_l2[:, k, :], a_b[:, q, :], ALU.mult))
                    link(v.tensor_reduce(wa2[:, k, q:q + 1], tmp2, X, ALU.add))

            dve.sem_inc(s_wa_ok, 1)

            dve.sem_inc(s_cnt_flushed, 2)
            dve.sem_inc(s_cnt_ps, 2)
            dve.sem_inc(s_cnt_left, 2)
            dve.sem_inc(s_h3_out0, 16)
            dve.sem_inc(s_h3_out1, 16)
            dve.sem_inc(s_ft_ps, 2)
            link(v.memset(cnt_d[:], 0))
            dve.wait_ge(s_recs_in, 16)

            def onehots(g, par):
                dve.wait_ge(s_pslot_ok, g + 1)
                for k in range(GT):
                    r = pslot[:, par, k * RW:(k + 1) * RW]
                    ins = v.tensor_scalar(oh_src[:, par * GT + k, :], iota_src[:], r[:, R_SRCF:R_SRCF + 1], None, ALU.is_equal)
                ins.then_inc(s_oh_ok, 1)

            def flush_counts(g, par, ps_count):
                bv = dve.value_load(gblk[0:1, bass.ds(g, 1)], min_val=0, max_val=NB - 1)
                dve.wait_ge(s_cnt_left, ps_count + 2)
                dve.wait_ge(s_cnt_flushed, ps_count + 1)
                dstv = cnt_d[:, bass.ds(bv * N, N)]
                v.tensor_tensor(dstv, cnt_ev[:, par, :], dstv, ALU.add).then_inc(s_cnt_flushed, 1)
            onehots(0, 0)
            onehots(1, 1)
            with dve.Fori(0, G // 2 - 1) as i:
                for par in range(2):
                    onehots(i * 2 + (2 + par), par)
                    flush_counts(i * 2 + par, par, i * 2 + (par + 1))
            flush_counts(G - 2, 0, G - 1)
            flush_counts(G - 1, 1, G)
            dve.wait_ge(s_cnt_flushed, G + 2)
            cd = cnt_d[:].rearrange("p (b n) -> p b n", n=N)
            for b in range(NB):
                if b >= 2:
                    dve.wait_ge(s_cntt_ps, b - 1)
                v.tensor_copy(cnt_f[:, b % 2, :], cd[:, b, :]).then_inc(s_cntf_ok, 1)

            def make_mask(mk, cm, loops):
                link(v.tensor_scalar(mk, cm, 0.0, NEG, ALU.is_equal, ALU.mult))
                if loops:
                    for b in range(NB):
                        d = mk[:, b, b * NP:(b + 1) * NP]
                        ins = v.scalar_tensor_tensor(d, ident[:NP, :NP], 0.0, d, ALU.is_equal, ALU.mult)
                    link(ins)
            make_mask(nomask, cd, True)
            dve.wait_ge(s_cnts_cp, NB)

            def self_loops(op):
                for b in range(NB):
                    d = cnt_s[:, b, b * NP:(b + 1) * NP]
                    ins = v.tensor_tensor(d, d, ident[:NP, :NP], op)
                link(ins)
            self_loops(ALU.add)
            dve.sem_inc(s_asb_free, 2)
            dve.sem_inc(s_max_stage, 1)

            with dve.Fori(0, H // 2) as i:
                ch.enter(i, 2 * NB)
                for par in range(2):
                    dve.wait_ge(s_asb_in0 if par == 0 else s_asb_in1, i * 16 + 16)
                    for b in range(NB):
                        dve.nop(nofuse=True)
                        (link if b == NB - 1 else ch.trail)(
                             v.tensor_tensor_reduce(out=junk[:, b % 2, :], in0=nomask[:, b, :], in1=as_b[:, par, :], scale=1.0,
                                                    scalar=NEG, op0=ALU.add, op1=ALU.max, accum_out=mx1[:, b:b + 1]))
                    v.tensor_copy(mxh[:, bass.ds(i * 2 + par, 1), :].rearrange("p a b -> p (a b)"), mx1[:]).then_inc(s_asb_free, 1)
                    dve.wait_ge(s_asb_free, i * 2 + (par + 3))
            ch.leave(H // 2)
            dve.wait_ge(s_asb_free, 2 + H)
            dve.sem_inc(s_max_stage, 1)

            def softmax_terms(nh, center, neigh, mxv, guard):
                mt = at(18200, [NP, NB * nh]) if nh > 1 else at(27000, [NP, NB])
                mt3 = mt.rearrange("p (b h) -> p b h", h=nh)
                link(v.tensor_tensor(mt3, mxv, center, ALU.add))
                link(v.scalar_tensor_tensor(mt, mt, SLOPE, mt, ALU.mult, ALU.max))
                link(v.tensor_tensor(uv[:, :, 0:nh], center, mt3, ALU.subtract))
                link(v.scalar_tensor_tensor(uv[:, :, nh:2 * nh], center, SLOPE, mt3, ALU.mult, ALU.subtract))
                v.tensor_scalar(sc8[:, 0:nh, :], neigh, 1.0 - SLOPE, None, ALU.mult)
                link(v.tensor_scalar(sc2[:, 0:nh, :], neigh, SLOPE, None, ALU.mult))
            dve.wait_ge(s_mlp_done, 1)
            softmax_terms(H, sc[:, :, H:2 * H], sc[:, :, 0:H].rearrange("p b h -> p h b"),
                          mxh[:].rearrange("p h b -> p b h"), False)
            for n, sblk in enumerate(POOL_P):
                ins = v.tensor_copy(cnt_pool[n], cnt_s[:, sblk, :])
            link(ins)
            dve.sem_inc(s_uv_ok, 1)
            dve.sem_inc(s_uv_free, 2)
            dve.sem_inc(s_head_free, 2)
            dve.sem_inc(s_norm_ok, 1)
            dve.sem_inc(s_pv_done, WR)

            def t_tile(dst, U, V, cc, ok):
                v.scalar_tensor_tensor(dst, U, cc, V, ALU.add, ALU.max).then_inc(ok, 1)

            def p_tile(dst, e, cm, ok):
                v.scalar_tensor_tensor(dst, e, 1.0, cm, ALU.min, ALU.mult).then_inc(ok, 1)

            def first_step(h, i, par, sblk):
                if sblk == 0:
                    v.tensor_copy(c8[:, par, :], sc8[:, bass.ds(h, 1), :].rearrange("p a b -> p (a b)"))
                    link(v.tensor_copy(c2[:, par, :], sc2[:, bass.ds(h, 1), :].rearrange("p a b -> p (a b)")))
                    dve.wait_ge(s_uv_in0 if par == 0 else s_uv_in1, i * 32 + 32)
                dve.wait_ge(s_pv_done, h * NB + (sblk + 1))
                t_tile(wt[:, sblk % WR, :], UV[:, par, 0, :], UV[:, par, 1, :], c8[:, par, sblk:sblk + 1], s_t_ok)

            def recip(i):
                dve.wait_ge(s_head_free, i * 2 + 4)
                v.reciprocal(rrow, rrow).then_inc(s_rrow_ok, 1)

            def dve_head(h, i, par, last=False, rec=None):
                for sblk in range(NB):
                    if sblk + LEAD < NB:
                        first_step(h, i, par, sblk + LEAD)
                    elif not last:
                        first_step(h + 1, i + par, 1 - par, sblk + LEAD - NB)
                    if sblk not in POOL_P:
                        dve.wait_ge(s_e_ok, h * NB + (sblk + 1))
                        p_tile(wt[:, sblk % WR, :], wt[:, sblk % WR, :], cnt_s[:, sblk, :], s_p_ok)
                    if sblk + LEAD == NB:
                        dve.wait_ge(s_t_ok, h * NB + NB)
                        dve.sem_inc(s_uv_free, 1)
                    if sblk == 4 and rec is not None:
                        recip(rec)
            for sblk in range(LEAD):
                first_step(0, 0, 0, sblk)
            dve_head(0, 0, 0)
            with dve.Fori(0, H // 2 - 1) as i:
                ch.enter(i, 2)
                dve_head(i * 2 + 1, i, 1)
                dve_head(i * 2 + 2, i + 1, 0, rec=i)
            ch.leave(H // 2 - 1)
            dve_head(H - 1, H // 2 - 1, 1, last=True)
            def bn_part(k):
                for q in range(5):
                    ins = v.bn_stats(bst1[:, k, q, :], OT[:, k, q * (N // 5):(q + 1) * (N // 5)])
                return ins
            dve.wait_ge(s_norm_ok, H // 2)
            for k in range(KT - 1):
                bn_part(k)
            recip(H // 2 - 1)
            n_p = H * (NB - len(POOL_P))
            dve.wait_ge(s_p_ok, n_p)
            dve.wait_ge(s_pp_ok, H * len(POOL_P))
            dve.wait_ge(s_norm_ok, H // 2 + 1)
            self_loops(ALU.subtract)

            dve.wait_ge(s_bn_in, 48)
            link(bn_part(KT - 1))
            for k in range(KT):
                ins = v.bn_aggr(mv1[:, k, :], bst1[:, k, :, :].rearrange("p q n -> p (q n)"))
            ins.then_inc(s_var_ok, 1)
            dve.wait_ge(s_bnsd_ok, 1)
            link(v.reciprocal(scl1[:], scl1[:]))
            link(v.tensor_tensor(scl1[:], scl1[:], bnp[:, 1, :], ALU.mult))
            link(v.tensor_tensor(shf1[:], mv1[:, :, 0], bnp[:, 0, :], ALU.add))
            link(v.tensor_tensor(shf1[:], bnp[:, 0, :], shf1[:], ALU.subtract))
            link(v.tensor_tensor(shf1[:], shf1[:], scl1[:], ALU.mult))
            v.tensor_tensor(shf1[:], shf1[:], bnp[:, 2, :], ALU.add).then_inc(s_bn_ok, 1)

            def ln_stats(b):
                link(v.bn_stats(bst[:, b, :], x_sb[:, b, :]))
                v.bn_aggr(mv[:, b, :], bst[:, b, :]).then_inc(s_ln_var, 1)

            def layernorm(layer, add, had=0):
                n0 = (layer - 1) * NB
                for b in range(NB + 1):
                    if had <= b < NB:
                        add(b)
                        ln_stats(b)
                    if b >= 1:
                        dve.wait_ge(s_ln_sd, n0 + b)
                        link(v.reciprocal(rstd[:, b - 1:b], rstd[:, b - 1:b]))
                        v.tensor_scalar(x_sb[:, b - 1, :], x_sb[:, b - 1, :], mv[:, b - 1, 0:1], rstd[:, b - 1:b],
                                        ALU.subtract, ALU.mult).then_inc(s_x_ok, 1)
                dve.wait_ge(s_x_ok, n0 + NB)

            def add1(b):
                dve.wait_ge(s_o_ps, b + 1)
                v.tensor_tensor(x_sb[:, b, :], x_sb[:, b, :], PS[:NP, 6 + b % 2, :], ALU.add).then_inc(s_o_cp, 1)
                dve.wait_ge(s_o_cp, b + 1)
            layernorm(1, add1)

            v.memset(acc, 0.0).then_inc(s_acc_zero, 1)
            dve.wait_ge(s_acc_zero, 1)
            dve.wait_ge(s_w1_in, 16 * 6)
            v.tensor_copy(w4r[:, 0, :], w_m4).then_inc(s_w4_ok, 1)
            dve.wait_ge(s_w4_ok, 1)
            v.tensor_tensor(w4r[0:HID, 1, :], w_m4[0:HID, :], w4r[0:HID, 0, :].bitcast(f32), ALU.subtract).then_inc(s_w4_ok, 1)
            dve.wait_ge(s_xup_cp, NB)
            dve.sem_inc(s_prod_ok, GT)
            dve.sem_inc(s_scat_done, GT)
            dve.sem_inc(s_acc_free, 2)
            dve.sem_inc(s_gsum_ok, 2)

            def products(par, k, T, T2, gath):
                dve.wait_ge(s_gath[par * GT + k], gath)
                xg = ring[:, par * GT + k, :].rearrange("p (q n) -> p q n", q=4)
                y = gslot[:, par, k * RW + R_Y:k * RW + R_Y + 4]
                wk = ws[:, k, :].rearrange("p (q n) -> p q n", q=5)
                pr = prod[:, k, :].rearrange("p (q n) -> p q n", q=8)
                dve.wait_ge(s_ws_ok, T(1))
                v.scalar_tensor_tensor(q4[:, 0, :], xg[:, 2, :], y[:, 2:3], qa[:, k, :], ALU.mult, ALU.add).then_inc(s_q_ok, 1)
                dve.wait_ge(s_scat_done, T(1))
                v.tensor_scalar(sel[:, par * GT + k, :], iota_dst[:], gslot[:, par, k * RW + R_DL:k * RW + R_DL + 1], None,
                                ALU.is_equal)
                v.tensor_tensor(pr[:, 0:4, :], wk[:, 0:4, :], xg[:, 0:1, :].to_broadcast([128, 4, MUL]), ALU.mult)
                dve.wait_ge(s_q_ok, T2(1))
                v.scalar_tensor_tensor(q4[:, 1, :], xg[:, 3, :], y[:, 3:4], q4[:, 0, :], ALU.mult, ALU.add).then_inc(s_q_ok, 1)
                v.tensor_tensor(pr[:, 4:7, :], wk[:, 4:5, :].to_broadcast([128, 3, MUL]), xg[:, 1:4, :], ALU.mult)
                dve.wait_ge(s_q_ok, T2(2))
                v.tensor_tensor(pr[:, 7, :], PS[:, (0, 1, 6, 7)[k], 3 * MUL:4 * MUL], q4[:, 1, :], ALU.mult).then_inc(s_prod_ok, 1)

            def split_hidden(par, n):
                dve.wait_ge(s_h3hi_ok, n)
                v.tensor_tensor(h3r[HID:128, par, :], h3[HID:128, par, :], h3r[HID:128, par, :].bitcast(f32), ALU.subtract)\
                    .then_inc(s_h3_ok, 1)
            split_hidden(0, 1)
            split_hidden(1, 2)
            for k in range(GT):
                products(0, k, lambda m, k=k: k + m, lambda m, k=k: 2 * k + m, 16)
            with dve.Fori(0, G // 2 - 1) as i:
                for par in (1, 0):
                    g = i * 2 + (2 - par)
                    off = 4 * (2 - par)
                    split_hidden(1 - par, i * 2 + (4 - par))
                    for k in range(GT):
                        products(par, k, lambda m, k=k: i * 8 + (off + k + m), lambda m, k=k: i * 16 + (2 * (off + k) + m),
                                 i * 16 + (16 if par else 32))
            dve.wait_ge(s_h3_ok, G)
            dve.sem_inc(s_h3_ok, 1)
            for k in range(GT):
                products(1, k, lambda m, k=k: (G - 1) * GT + k + m, lambda m, k=k: 2 * ((G - 1) * GT + k) + m, 16 * (G // 2))
            dve.wait_ge(s_acc_free, G + 2)
            dve.sem_inc(s_acc_done, 1)
            oscale = SILU2 * HID ** -0.5 * (2 * MUL) ** -0.5 / 10.0

            def add2(b):
                dve.wait_ge(s_y1_ps, b + 1)
                v.scalar_tensor_tensor(x_sb[:, b, 0:MUL], PS[:NP, 4 + b % 2, 0:MUL], oscale, x_sb[:, b, 0:MUL], ALU.mult, ALU.add)
                xv = x_sb[:, b, MUL:D].rearrange("p (u m) -> p m u", m=3)
                v.scalar_tensor_tensor(xv, PS[:NP, 4 + b % 2, MUL:D].rearrange("p (m u) -> p m u", m=3), oscale, xv,
                                       ALU.mult, ALU.add).then_inc(s_y1_cp, 1)
                dve.wait_ge(s_y1_cp, b + 1)
            layernorm(2, add2)

            v.tensor_copy(w_rep, wa2[:, :, 1:2].to_broadcast([128, KT, NP])).then_inc(s_wrep_ok, 1)
            link(v.tensor_scalar(nomask2, cnt_s[:], 0.0, NEG, ALU.is_equal, ALU.mult))
            dve.wait_ge(s_st_ok, 3)
            for b in range(NB):
                (link if b in (0, NB - 1) else ch.trail)(
                     v.tensor_tensor_reduce(out=junk2[:, b % 2, :], in0=nomask2[:, b, :], in1=st_b, scale=1.0, scalar=NEG,
                                            op0=ALU.add, op1=ALU.max, accum_out=mx1[:, b:b + 1]))
            link(v.scalar_tensor_tensor(mx1[:], mx1[:], 0.5 * NEG, mx1[:], ALU.is_gt, ALU.mult))
            dve.wait_ge(s_cols2_cp, 1)
            softmax_terms(1, sc[:, :, 0:1], sc[:, :, 1:2].rearrange("p b h -> p h b"), mx1[:].unsqueeze(2), True)
            v.tensor_copy(c8[:, 0, :], sc8[:, 0, :])
            link(v.tensor_copy(c2[:, 0, :], sc2[:, 0, :]))
            dve.sem_inc(s_uv2_ok, 1)
            dve.sem_inc(s_sp_free, 2)
            dve.wait_ge(s_uv2_in, 32)
            for k in range(NB + 1):
                if k < NB:
                    t_tile(t2[:, k % 2, :], UV2[:, 0, :], UV2[:, 1, :], c8[:, 0, k:k + 1], s_t2_ok)
                if k >= 1:
                    dve.wait_ge(s_e2_ok, k)
                    p_tile(P50[:, k - 1, :], e2[:, (k - 1) % 2, :], cd[:, k - 1, :], s_p2_ok)
            link(v.tensor_reduce(deg[:], cd, X, ALU.add))
            link(v.tensor_scalar(cen[:], cen[:], -KAPPA, KAPPA * (1.0 + 1.0 / STEP), ALU.mult, ALU.add))
            dve.wait_ge(s_l2_agg, 4)
            link(v.tensor_scalar(rden2, PS[:, 3:6, :].rearrange("p a n -> p (a n)")[:, 0:N], 0.5, None, ALU.max))
            link(v.reciprocal(rden2, rden2))
            dve.wait_ge(s_l2_agg, 5)
            dve.wait_ge(s_l2_cp, KT)
            for half in range(2):
                cols = slice(half * HB * NP, (half + 1) * HB * NP)
                v.tensor_tensor(aggT[:, :, cols], aggr[:, :, cols],
                                rden2[:, cols].unsqueeze(1).to_broadcast([128, KT, HB * NP]), ALU.mult).then_inc(s_aggT_ok, 1)
            dve.wait_ge(s_aggT_ok, 2)
            for half in range(2):
                with dve.Fori(0, NSPL // 2) as i:
                    ch.enter(i, 4)
                    for par in range(2):
                        slot = 1 - par
                        v.tensor_copy(cslot[:, par:par + 1], cen[:, bass.ds(i * 2 + par, 1)]).then_inc(s_cslot_ok, 1)
                        dve.wait_ge(s_sv_ok, i * 2 + (8 * half + par + 1))
                        v.tensor_scalar(sa, sv, 2 * KAPPA, 2 * KAPPA, ALU.min, ALU.subtract).then_inc(s_sa_ok, 1)
                        v.tensor_scalar(sbb, sv, KAPPA, KAPPA, ALU.min, ALU.subtract).then_inc(s_sa_ok, 1)
                        dve.wait_ge(s_sq2_ok, i * 4 + (16 * half + 2 * par + 1))
                        link(v.tensor_tensor(sa2, sa2, sa, ALU.mult))
                        dve.wait_ge(s_sq2_ok, i * 4 + (16 * half + 2 * par + 2))
                        link(v.tensor_tensor(sb2, sb2, sbb, ALU.mult))
                        dve.wait_ge(s_sp_free, i * 2 + (9 * half + par + 2))
                        v.scalar_tensor_tensor(basis[:, slot, :], sb2, 4.0, sa2, ALU.mult, ALU.subtract).then_inc(s_basis_ok, 1)
                ch.leave(NSPL // 2)
                dve.wait_ge(s_sp_free, 9 * half + 11)
                if half == 0:
                    for b in range(HB):
                        v.tensor_tensor(x_sb[:, b, :], x_sb[:, b, :], PS[:NP, b, :], ALU.add).then_inc(s_y2_cp, 1)
                    dve.wait_ge(s_y2_cp, HB)
                    for b in range(HB):
                        ln_stats(b)

            def add3(b):
                v.tensor_tensor(x_sb[:, b, :], x_sb[:, b, :], PS[:NP, b - HB, :], ALU.add).then_inc(s_y2_cp, 1)
                dve.wait_ge(s_y2_cp, b + 1)
            layernorm(3, add3, had=HB)

            link(v.tensor_scalar(deg[:], deg[:], 1.0, None, ALU.max))
            link(v.reciprocal(deg[:], deg[:]))

            def add4(b):
                dve.wait_ge(s_y3_ps, b + 1)
                v.tensor_scalar(fin[:, b % 2, :], PS[:NP, b % 2, :], deg[:, b:b + 1], None, ALU.mult).then_inc(s_fin_ok, 1)
                dve.wait_ge(s_fin_ok, 2 * b + 1)
                v.tensor_tensor(fin[:, b % 2, :], fin[:, b % 2, :], PS[:NP, 4 + b % 2, :], ALU.add).then_inc(s_fin_ok, 1)
                dve.wait_ge(s_fin_ok, 2 * b + 2)
                v.scalar_tensor_tensor(x_sb[:, b, :], fin[:, b % 2, :], 0.0, x_sb[:, b, :], ALU.max, ALU.add).then_inc(s_y3_cp, 1)
                dve.wait_ge(s_y3_cp, b + 1)
            layernorm(4, add4)


_INS = ("x", "src", "dst", "edge_attr_4", "edge_attr_8", "L0_gnn_W_gat", "L0_gnn_att_src", "L0_gnn_att_dst",
        "L0_gnn_gat_bias", "L0_gnn_bn_gamma", "L0_gnn_bn_beta", "L0_gnn_W_skip", "L0_gnn_b_skip",
        "L1_gnn_W_up0", "L1_gnn_W_up1", "L1_gnn_W_mlp1", "L1_gnn_W_mlp2", "L1_gnn_W_mlp3", "L1_gnn_W_mlp4",
        "L1_gnn_W_out0", "L1_gnn_W_out1", "L2_gnn_W", "L2_gnn_a")


def kernel(**inputs):
    import numpy as _np
    import concourse.bacc as _bacc
    from concourse import mybir as _mybir
    from concourse.bass_utils import run_bass_kernel_spmd as _run

    nc = _bacc.Bacc("TRN2", target_bir_lowering=False, num_devices=1)
    laid = {name: _np.asarray(inputs[name]) for name in _INS}
    for name in ("L0_gnn_gat_bias", "L0_gnn_bn_gamma", "L0_gnn_bn_beta"):
        laid[name] = laid[name].reshape(KT, 128).T
    laid["L1_gnn_W_mlp4"] = laid["L1_gnn_W_mlp4"].reshape(HID, 4, MUL)[:, [0, 2, 1, 3], :].reshape(HID, 4 * MUL)
    laid["base_wT"] = _np.asarray(inputs["L2_gnn_base_w"]).T
    laid["spline_wT"] = _np.asarray(inputs["L2_gnn_spline_w"]).transpose(2, 1, 0)
    laid["w_l3T"] = _np.asarray(inputs["L3_gnn_w"]).T
    arrays, args = {}, {}
    for name, v in laid.items():
        v = _np.ascontiguousarray(v)
        arrays[f"in_{name}"] = v
        args[name] = nc.dram_tensor(f"in_{name}", v.shape, _mybir.dt.from_np(v.dtype), kind="ExternalInput").ap()
    out = nc.dram_tensor("out", (N, D), _mybir.dt.float32, kind="ExternalOutput").ap()
    build(nc, args, out)
    r = _run(nc, [arrays], core_ids=[0])
    return r.results[0]["out"]
```
